# Optimizing a Trainium2 kernel written in Bass

```python
import numpy as np
import jax
import jax.numpy as jnp

def _softmax(x, axis=-1):
    return jax.nn.softmax(x, axis=axis)

def _gelu(x):
    return jax.nn.gelu(x, approximate=True)

def _silu(x):
    return jax.nn.silu(x)

def _sigmoid(x):
    return jax.nn.sigmoid(x)

def _layernorm(x, axis=-1, eps=1e-05):
    m = jnp.mean(x, axis=axis, keepdims=True)
    v = jnp.var(x, axis=axis, keepdims=True)
    return (x - m) / jnp.sqrt(v + eps)

def _scatter_add(tgt, idx, src, axis=0):
    return tgt.at[idx].add(src)

def _segment_sum(src, seg, n):
    return jax.ops.segment_sum(src, seg, n)
kernel_name = 'mk_gnn_resnorm_d4_gnn_r8_8be140'

def setup_inputs(seed: int=0):
    np.random.seed(seed)
    _w = jnp.asarray

    def _rec_inputs():
        import jax
        import jax.numpy as jnp
        _gk = jax.random.key(seed)
        x = -0.000202 + 1 * jax.random.normal(jax.random.fold_in(_gk, 1), (6250, 128), jnp.float32)
        _s = jax.random.randint(jax.random.fold_in(_gk, 2), (50000,), 0, 6250, jnp.int32)
        _d = jax.random.randint(jax.random.fold_in(_gk, 3), (50000,), 0, 6250, jnp.int32)
        _loop = jnp.arange(6250, dtype=jnp.int32)
        src = jnp.concatenate([_s, _d, _loop])
        dst = jnp.concatenate([_d, _s, _loop])
        _o = jnp.argsort(dst, stable=True)
        src = src[_o]
        dst = dst[_o]
        edge_attr_32 = 0.000196303 + 1.00016 * jax.random.normal(jax.random.fold_in(_gk, 12), (106250, 32), jnp.float32)
        edge_attr_50 = 0.000229061 + 1.00009 * jax.random.normal(jax.random.fold_in(_gk, 13), (106250, 50), jnp.float32)
        edge_weight = jax.random.uniform(jax.random.fold_in(_gk, 15), (106250,), jnp.float32, 0.0, 0.999998)
        return (x, src, dst, edge_attr_32, edge_attr_50, edge_weight)
    x, src, dst, edge_attr_32, edge_attr_50, edge_weight = _rec_inputs()

    def _L0_gnn_setup():
        import jax, jax.numpy as jnp
        import numpy as np
        N, E = (6250, 100000)
        IN_DIM = 128
        OUT_DIM = 128
        H = 8
        D = OUT_DIM // H
        LN_EPS = 1e-05
        key = jax.random.key(seed)
        ks = jax.random.split(key, 16)
        s_in = 1.0 / np.sqrt(IN_DIM)
        s_out = 1.0 / np.sqrt(OUT_DIM)
        return {'x': jax.random.normal(ks[0], (N, IN_DIM), dtype=jnp.float32), 'edge_index': jax.random.randint(ks[1], (2, E), 0, N, dtype=jnp.int32), 'edge_attr': jax.random.uniform(ks[2], (E,), dtype=jnp.float32), 'Wq': jax.random.normal(ks[3], (H, IN_DIM, D), dtype=jnp.float32) * s_in, 'bq': jnp.zeros((H, D), dtype=jnp.float32), 'Wk': jax.random.normal(ks[4], (H, IN_DIM, D), dtype=jnp.float32) * s_in, 'bk': jnp.zeros((H, D), dtype=jnp.float32), 'Wv': jax.random.normal(ks[5], (H, IN_DIM, D), dtype=jnp.float32) * s_in, 'bv': jnp.zeros((H, D), dtype=jnp.float32), 'We': jax.random.normal(ks[6], (H, D), dtype=jnp.float32), 'Wskip': jax.random.normal(ks[7], (H, IN_DIM, D), dtype=jnp.float32) * s_in, 'bskip': jnp.zeros((H, D), dtype=jnp.float32), 'Wo': jax.random.normal(ks[8], (OUT_DIM, OUT_DIM), dtype=jnp.float32) * s_out, 'bo': jnp.zeros((OUT_DIM,), dtype=jnp.float32), 'gamma': jnp.ones((OUT_DIM,), dtype=jnp.float32), 'beta': jnp.zeros((OUT_DIM,), dtype=jnp.float32)}
    _L0_gnn_all = _L0_gnn_setup()
    _L0_gnn_in = {k: v for k, v in _L0_gnn_all.items() if k in ('Wq', 'bq', 'Wk', 'bk', 'Wv', 'bv', 'We', 'Wskip', 'bskip', 'Wo', 'bo', 'gamma', 'beta')}
    del _L0_gnn_all

    def _L1_gnn_setup():
        import jax, jax.numpy as jnp
        import numpy as np
        N, E = (6250, 100000)
        NODE_DIM, EDGE_DIM, HIDDEN_DIM = (128, 32, 128)
        LN_EPS = 1e-05
        key = jax.random.key(seed)
        ks = jax.random.split(key, 10)

        def lin(k, fan_in, fan_out):
            bound = 1.0 / np.sqrt(fan_in)
            kw, kb = jax.random.split(k)
            W = jax.random.uniform(kw, (fan_out, fan_in), jnp.float32, -bound, bound)
            b = jax.random.uniform(kb, (fan_out,), jnp.float32, -bound, bound)
            return (W, b)
        x = jax.random.normal(ks[0], (N, NODE_DIM), jnp.float32)
        edge_index = jax.random.randint(ks[1], (2, E), 0, N, jnp.int64)
        edge_attr = jax.random.normal(ks[2], (E, EDGE_DIM), jnp.float32)
        W1, b1 = lin(ks[3], 2 * NODE_DIM + EDGE_DIM, HIDDEN_DIM)
        W2, b2 = lin(ks[4], HIDDEN_DIM, HIDDEN_DIM)
        Wu, bu = lin(ks[5], HIDDEN_DIM, NODE_DIM)
        gamma = jnp.ones((NODE_DIM,), jnp.float32)
        beta = jnp.zeros((NODE_DIM,), jnp.float32)
        return {'x': x, 'edge_attr': edge_attr, 'W1': W1, 'b1': b1, 'W2': W2, 'b2': b2, 'Wu': Wu, 'bu': bu, 'gamma': gamma, 'beta': beta, 'edge_index': edge_index}
    _L1_gnn_all = _L1_gnn_setup()
    _L1_gnn_in = {k: v for k, v in _L1_gnn_all.items() if k in ('W1', 'b1', 'W2', 'b2', 'Wu', 'bu', 'gamma', 'beta')}
    del _L1_gnn_all

    def _L2_gnn_setup():
        import jax, jax.numpy as jnp
        import numpy as np
        N = 6250
        E = 75000
        HID = 128
        NF = 128
        NG = 50
        CUTOFF = 10.0
        LOG2 = float(np.log(2.0))

        def ssp(x):
            return jax.nn.softplus(x) - LOG2
        key = jax.random.key(seed)
        ks = jax.random.split(key, 12)
        h = jax.random.normal(ks[0], (N, HID), dtype=jnp.float32)
        edge_index = jax.random.randint(ks[1], (2, E), 0, N)
        edge_weight = jax.random.uniform(ks[2], (E,), dtype=jnp.float32) * CUTOFF
        edge_attr = jax.random.normal(ks[3], (E, NG), dtype=jnp.float32)

        def xavier(k, shape):
            fan_out, fan_in = shape
            lim = np.sqrt(6.0 / (fan_in + fan_out))
            return jax.random.uniform(k, shape, jnp.float32, -lim, lim)
        mlp_w0 = xavier(ks[4], (NF, NG))
        mlp_b0 = jnp.zeros((NF,), jnp.float32)
        mlp_w2 = xavier(ks[5], (NF, NF))
        mlp_b2 = jnp.zeros((NF,), jnp.float32)
        lin1_w = xavier(ks[6], (NF, HID))
        lin2_w = xavier(ks[7], (HID, NF))
        lin2_b = jnp.zeros((HID,), jnp.float32)
        lin_w = xavier(ks[8], (HID, HID))
        lin_b = jnp.zeros((HID,), jnp.float32)
        return {'h': h, 'edge_index': edge_index, 'edge_weight': edge_weight, 'edge_attr': edge_attr, 'mlp_w0': mlp_w0, 'mlp_b0': mlp_b0, 'mlp_w2': mlp_w2, 'mlp_b2': mlp_b2, 'lin1_w': lin1_w, 'lin2_w': lin2_w, 'lin2_b': lin2_b, 'lin_w': lin_w, 'lin_b': lin_b}
    _L2_gnn_all = _L2_gnn_setup()
    _L2_gnn_in = {k: v for k, v in _L2_gnn_all.items() if k in ('mlp_w0', 'mlp_b0', 'mlp_w2', 'mlp_b2', 'lin1_w', 'lin2_w', 'lin2_b', 'lin_w', 'lin_b')}
    del _L2_gnn_all

    def _L3_gnn_setup():
        import jax, jax.numpy as jnp
        import numpy as np
        NUM_STEPS = 1

        def _seg_mean(vals, idx, num_nodes):
            s = jax.ops.segment_sum(vals, idx, num_segments=num_nodes)
            cnt = jax.ops.segment_sum(jnp.ones((vals.shape[0],), vals.dtype), idx, num_segments=num_nodes)
            return s / jnp.maximum(cnt, 1.0)[:, None]

        def _gru_cell(a, h, w_ih, w_hh, b_ih, b_hh):
            gi = a @ w_ih.T + b_ih
            gh = h @ w_hh.T + b_hh
            H = h.shape[1]
            i_r, i_z, i_n = (gi[:, :H], gi[:, H:2 * H], gi[:, 2 * H:])
            h_r, h_z, h_n = (gh[:, :H], gh[:, H:2 * H], gh[:, 2 * H:])
            r = jax.nn.sigmoid(i_r + h_r)
            z = jax.nn.sigmoid(i_z + h_z)
            n = jnp.tanh(i_n + r * h_n)
            return (1.0 - z) * n + z * h
        key = jax.random.key(seed)
        ks = jax.random.split(key, 8)
        N, E, H = (12500, 80000, 128)
        sc = 1.0 / np.sqrt(H)
        feat = jax.random.normal(ks[0], (N, H), jnp.float32)
        src = jax.random.randint(ks[1], (E,), 0, N, jnp.int32)
        dst = jax.random.randint(ks[2], (E,), 0, N, jnp.int32)
        W_in = jax.random.normal(ks[3], (H, H), jnp.float32) * sc
        W_out = jax.random.normal(ks[4], (H, H), jnp.float32) * sc
        w_ih = jax.random.normal(ks[5], (3 * H, 2 * H), jnp.float32) * sc
        w_hh = jax.random.normal(ks[6], (3 * H, H), jnp.float32) * sc
        return {'feat': feat, 'src': src, 'dst': dst, 'W_in': W_in, 'b_in': jnp.zeros((H,), jnp.float32), 'W_out': W_out, 'b_out': jnp.zeros((H,), jnp.float32), 'w_ih': w_ih, 'w_hh': w_hh, 'b_ih': jnp.zeros((3 * H,), jnp.float32), 'b_hh': jnp.zeros((3 * H,), jnp.float32)}
    _L3_gnn_all = _L3_gnn_setup()
    _L3_gnn_in = {k: v for k, v in _L3_gnn_all.items() if k in ('W_in', 'b_in', 'W_out', 'b_out', 'w_ih', 'w_hh', 'b_ih', 'b_hh')}
    del _L3_gnn_all
    return {'x': x, 'src': src, 'dst': dst, 'edge_attr_32': edge_attr_32, 'edge_attr_50': edge_attr_50, 'edge_weight': edge_weight, 'L0_gnn_Wq': _L0_gnn_in['Wq'], 'L0_gnn_bq': _L0_gnn_in['bq'], 'L0_gnn_Wk': _L0_gnn_in['Wk'], 'L0_gnn_bk': _L0_gnn_in['bk'], 'L0_gnn_Wv': _L0_gnn_in['Wv'], 'L0_gnn_bv': _L0_gnn_in['bv'], 'L0_gnn_We': _L0_gnn_in['We'], 'L0_gnn_Wskip': _L0_gnn_in['Wskip'], 'L0_gnn_bskip': _L0_gnn_in['bskip'], 'L0_gnn_Wo': _L0_gnn_in['Wo'], 'L0_gnn_bo': _L0_gnn_in['bo'], 'L0_gnn_gamma': _L0_gnn_in['gamma'], 'L0_gnn_beta': _L0_gnn_in['beta'], 'L1_gnn_W1': _L1_gnn_in['W1'], 'L1_gnn_b1': _L1_gnn_in['b1'], 'L1_gnn_W2': _L1_gnn_in['W2'], 'L1_gnn_b2': _L1_gnn_in['b2'], 'L1_gnn_Wu': _L1_gnn_in['Wu'], 'L1_gnn_bu': _L1_gnn_in['bu'], 'L1_gnn_gamma': _L1_gnn_in['gamma'], 'L1_gnn_beta': _L1_gnn_in['beta'], 'L2_gnn_mlp_w0': _L2_gnn_in['mlp_w0'], 'L2_gnn_mlp_b0': _L2_gnn_in['mlp_b0'], 'L2_gnn_mlp_w2': _L2_gnn_in['mlp_w2'], 'L2_gnn_mlp_b2': _L2_gnn_in['mlp_b2'], 'L2_gnn_lin1_w': _L2_gnn_in['lin1_w'], 'L2_gnn_lin2_w': _L2_gnn_in['lin2_w'], 'L2_gnn_lin2_b': _L2_gnn_in['lin2_b'], 'L2_gnn_lin_w': _L2_gnn_in['lin_w'], 'L2_gnn_lin_b': _L2_gnn_in['lin_b'], 'L3_gnn_W_in': _L3_gnn_in['W_in'], 'L3_gnn_b_in': _L3_gnn_in['b_in'], 'L3_gnn_W_out': _L3_gnn_in['W_out'], 'L3_gnn_b_out': _L3_gnn_in['b_out'], 'L3_gnn_w_ih': _L3_gnn_in['w_ih'], 'L3_gnn_w_hh': _L3_gnn_in['w_hh'], 'L3_gnn_b_ih': _L3_gnn_in['b_ih'], 'L3_gnn_b_hh': _L3_gnn_in['b_hh']}

def reference(x, src, dst, edge_attr_32, edge_attr_50, edge_weight, L0_gnn_Wq, L0_gnn_bq, L0_gnn_Wk, L0_gnn_bk, L0_gnn_Wv, L0_gnn_bv, L0_gnn_We, L0_gnn_Wskip, L0_gnn_bskip, L0_gnn_Wo, L0_gnn_bo, L0_gnn_gamma, L0_gnn_beta, L1_gnn_W1, L1_gnn_b1, L1_gnn_W2, L1_gnn_b2, L1_gnn_Wu, L1_gnn_bu, L1_gnn_gamma, L1_gnn_beta, L2_gnn_mlp_w0, L2_gnn_mlp_b0, L2_gnn_mlp_w2, L2_gnn_mlp_b2, L2_gnn_lin1_w, L2_gnn_lin2_w, L2_gnn_lin2_b, L2_gnn_lin_w, L2_gnn_lin_b, L3_gnn_W_in, L3_gnn_b_in, L3_gnn_W_out, L3_gnn_b_out, L3_gnn_w_ih, L3_gnn_w_hh, L3_gnn_b_ih, L3_gnn_b_hh):
    import jax
    import jax.numpy as jnp

    def _L0_gnn_ref(x, edge_index, edge_attr, Wq, bq, Wk, bk, Wv, bv, We, Wskip, bskip, Wo, bo, gamma, beta):
        import jax, jax.numpy as jnp
        import numpy as np
        N, E = (6250, 100000)
        IN_DIM = 128
        OUT_DIM = 128
        H = 8
        D = OUT_DIM // H
        LN_EPS = 1e-05
        n = x.shape[0]
        h, _, d = Wq.shape
        src, dst = (edge_index[0], edge_index[1])
        q = jnp.einsum('ni,hid->nhd', x, Wq) + bq
        k = jnp.einsum('ni,hid->nhd', x, Wk) + bk
        v = jnp.einsum('ni,hid->nhd', x, Wv) + bv
        e = edge_attr[:, None, None] * We[None, :, :]
        ke = k[src] + e
        alpha = jnp.einsum('ehd,ehd->eh', q[dst], ke) / jnp.sqrt(jnp.asarray(d, x.dtype))
        m = jax.ops.segment_max(alpha, dst, num_segments=n)
        m = jnp.where(jnp.isfinite(m), m, 0.0)
        ex = jnp.exp(alpha - m[dst])
        denom = jax.ops.segment_sum(ex, dst, num_segments=n)
        w = ex / jnp.maximum(denom[dst], 1e-16)
        agg = jax.ops.segment_sum(w[:, :, None] * (v[src] + e), dst, num_segments=n)
        skip = jnp.einsum('ni,hid->nhd', x, Wskip) + bskip
        heads_cat = (agg + skip).reshape(n, h * d)
        out = heads_cat @ Wo + bo
        out = out + x
        mu = out.mean(-1, keepdims=True)
        var = out.var(-1, keepdims=True)
        out = (out - mu) * jax.lax.rsqrt(var + LN_EPS) * gamma + beta
        return out

    def _L1_gnn_ref(x, edge_attr, W1, b1, W2, b2, Wu, bu, gamma, beta, edge_index):
        import jax, jax.numpy as jnp
        import numpy as np
        N, E = (6250, 100000)
        NODE_DIM, EDGE_DIM, HIDDEN_DIM = (128, 32, 128)
        LN_EPS = 1e-05
        src, dst = (edge_index[0], edge_index[1])
        msg_input = jnp.concatenate([x[src], x[dst], edge_attr], axis=-1)
        h = jax.nn.relu(msg_input @ W1.T + b1)
        messages = h @ W2.T + b2
        agg = jax.ops.segment_sum(messages, dst, num_segments=x.shape[0])
        upd = jax.nn.relu(agg @ Wu.T + bu)
        y = x + upd
        mean = jnp.mean(y, axis=-1, keepdims=True)
        var = jnp.mean(jnp.square(y - mean), axis=-1, keepdims=True)
        return (y - mean) * jax.lax.rsqrt(var + LN_EPS) * gamma + beta

    def _L2_gnn_ref(h, edge_index, edge_weight, edge_attr, mlp_w0, mlp_b0, mlp_w2, mlp_b2, lin1_w, lin2_w, lin2_b, lin_w, lin_b):
        import jax, jax.numpy as jnp
        import numpy as np
        N = 6250
        E = 75000
        HID = 128
        NF = 128
        NG = 50
        CUTOFF = 10.0
        LOG2 = float(np.log(2.0))

        def ssp(x):
            return jax.nn.softplus(x) - LOG2
        src, dst = (edge_index[0], edge_index[1])
        h1 = h @ lin1_w.T
        c = 0.5 * (jnp.cos(edge_weight / CUTOFF * jnp.pi) + 1.0)
        W = ssp(edge_attr @ mlp_w0.T + mlp_b0) @ mlp_w2.T + mlp_b2
        message = c[:, None] * (W * h1[src])
        agg = jax.ops.segment_sum(message, dst, num_segments=h.shape[0])
        h2 = (h1 + agg) @ lin2_w.T + lin2_b
        return ssp(h2) @ lin_w.T + lin_b

    def _L3_gnn_ref(feat, src, dst, W_in, b_in, W_out, b_out, w_ih, w_hh, b_ih, b_hh):
        import jax, jax.numpy as jnp
        import numpy as np
        NUM_STEPS = 1

        def _seg_mean(vals, idx, num_nodes):
            s = jax.ops.segment_sum(vals, idx, num_segments=num_nodes)
            cnt = jax.ops.segment_sum(jnp.ones((vals.shape[0],), vals.dtype), idx, num_segments=num_nodes)
            return s / jnp.maximum(cnt, 1.0)[:, None]

        def _gru_cell(a, h, w_ih, w_hh, b_ih, b_hh):
            gi = a @ w_ih.T + b_ih
            gh = h @ w_hh.T + b_hh
            H = h.shape[1]
            i_r, i_z, i_n = (gi[:, :H], gi[:, H:2 * H], gi[:, 2 * H:])
            h_r, h_z, h_n = (gh[:, :H], gh[:, H:2 * H], gh[:, 2 * H:])
            r = jax.nn.sigmoid(i_r + h_r)
            z = jax.nn.sigmoid(i_z + h_z)
            n = jnp.tanh(i_n + r * h_n)
            return (1.0 - z) * n + z * h
        N = feat.shape[0]
        h = feat
        for _ in range(NUM_STEPS):
            feat_in = h @ W_in.T + b_in
            feat_out = h @ W_out.T + b_out
            a_in = _seg_mean(feat_in[src], dst, N)
            a_out = _seg_mean(feat_out[dst], src, N)
            a = jnp.concatenate((a_in, a_out), axis=1)
            h = _gru_cell(a, h, w_ih, w_hh, b_ih, b_hh)
        return h
    edge_index = jnp.stack([src, dst])
    x = _layernorm(x + _L0_gnn_ref(x, edge_index, edge_weight, L0_gnn_Wq, L0_gnn_bq, L0_gnn_Wk, L0_gnn_bk, L0_gnn_Wv, L0_gnn_bv, L0_gnn_We, L0_gnn_Wskip, L0_gnn_bskip, L0_gnn_Wo, L0_gnn_bo, L0_gnn_gamma, L0_gnn_beta), axis=-1)
    x = _layernorm(x + _L1_gnn_ref(x, edge_attr_32, L1_gnn_W1, L1_gnn_b1, L1_gnn_W2, L1_gnn_b2, L1_gnn_Wu, L1_gnn_bu, L1_gnn_gamma, L1_gnn_beta, edge_index), axis=-1)
    x = _layernorm(x + _L2_gnn_ref(x, edge_index, edge_weight, edge_attr_50, L2_gnn_mlp_w0, L2_gnn_mlp_b0, L2_gnn_mlp_w2, L2_gnn_mlp_b2, L2_gnn_lin1_w, L2_gnn_lin2_w, L2_gnn_lin2_b, L2_gnn_lin_w, L2_gnn_lin_b), axis=-1)
    x = _layernorm(x + _L3_gnn_ref(x, src, dst, L3_gnn_W_in, L3_gnn_b_in, L3_gnn_W_out, L3_gnn_b_out, L3_gnn_w_ih, L3_gnn_w_hh, L3_gnn_b_ih, L3_gnn_b_hh), axis=-1)
    return x

_drawn_inputs = setup_inputs


def setup_inputs(seed=0):
    import zlib

    import numpy as np

    out = dict(_drawn_inputs(seed))
    spreads = {'L0_gnn_bq': (0.0, 0.694),
     'L0_gnn_bk': (0.0, 2.0),
     'L0_gnn_bv': (0.0, 0.1),
     'L0_gnn_bskip': (0.0, 0.1),
     'L0_gnn_bo': (0.0, 0.1),
     'L0_gnn_gamma': (1.0, 0.2),
     'L0_gnn_beta': (0.0, 0.1),
     'L1_gnn_gamma': (1.0, 0.2),
     'L1_gnn_beta': (0.0, 0.1),
     'L2_gnn_mlp_b0': (0.0, 0.1),
     'L2_gnn_mlp_b2': (0.0, 0.1),
     'L2_gnn_lin2_b': (0.0, 0.1),
     'L2_gnn_lin_b': (0.0, 0.1),
     'L3_gnn_b_in': (0.0, 0.32),
     'L3_gnn_b_out': (0.0, 0.276),
     'L3_gnn_b_ih': (0.0, 0.271),
     'L3_gnn_b_hh': (0.0, 0.381)}
    factors = {'L1_gnn_bu': 3.225}
    for name, (base, spread) in spreads.items():
        noise = np.random.default_rng([zlib.crc32(name.encode()), seed]).standard_normal(out[name].shape)
        drawn = base * np.exp(spread * noise) if base else spread * noise
        out[name] = jnp.asarray(drawn.astype(out[name].dtype))
    for name, factor in factors.items():
        out[name] = (out[name] * factor).astype(out[name].dtype)
    return out
```

```python
from contextlib import ExitStack

import concourse.bass as bass
from concourse import mybir

F32 = mybir.dt.float32
I32 = mybir.dt.int32
BF16 = mybir.dt.bfloat16
ALU = mybir.AluOpType
ACT = mybir.ActivationFunctionType
AX_X = mybir.AxisListType.X
PE_ENGINE = mybir.EngineType.PE
DVE_ENGINE = mybir.EngineType.DVE
SP_ENGINE = mybir.EngineType.SP

P = 128
N = 6250
E = 106250
F = 128
H = 8
D = F // H
A1, A2 = 32, 50
NB = -(-N // P)
NT = NB + 1
U = 4
R = 4
TILES = -(-(E // P + NB) // (U * R)) * U * R
BATCHES = TILES // U
SLOTS = TILES * P
CHUNK = -(-(E + P) // P)
EP = CHUNK * P
NOWHERE = 1 << 20
SU = 8
JC = -(-TILES // P)
SQ = 8
SP_PARTS = TILES // SQ
SL = SQ * P
FAR = -1.0e30
LN_EPS = 1e-5
LOG2 = 0.6931471805599453
assert CHUNK % SU == 0 and (CHUNK // SU) % R == 0 and TILES % SQ == 0 and NB <= BATCHES // R - 1

C_EX, C_EW, C_CNT, C_END = F, F + H, F + 2 * H, F + 2 * H + 1
QW = F + H

ACC0, ACC_N = 0, NT * C_END + 6
B1_0 = ACC_N
B1_N = 2 * H * SL - ACC_N
B2_0 = B1_0 + B1_N
B2_N = TILES * H
ARENA = B2_0 + B2_N


def at_least(eng, sem, value, tick):
    if isinstance(value, int):
        if value > 0:
            eng.wait_ge(sem, value)
        return
    eng.wait_ge(sem, value)
    eng.sem_inc(tick, 1)


def rounds(eng, count, ring, step, peeled=1):
    for k in range(peeled * ring):
        step(k, k // ring, k % ring)
    with eng.Fori(peeled, count // ring) as i:
        for r in range(ring):
            step(i * ring + r, i, r)


class Core:

    def __init__(self, nc):
        self.nc, self.used, self.w = nc, [], {}

    def semaphore(self, name):
        self.used.append(self.nc.alloc_semaphore(name=name))
        return self.used[-1]

    def clear_semaphores(self):
        self.nc.clear_and_free_semaphores(self.used)
        self.nc.all_engine_barrier()
        self.used = []


def arena(c, start, shape, dtype=F32):
    n = 1
    for s in shape:
        n *= s
    words = n if dtype != BF16 else n // 2
    ap = c.arena[:, start:start + words]
    if dtype != F32:
        ap = ap.bitcast(dtype)
    if len(shape) == 2:
        return ap.rearrange("p (a b) -> p a b", b=shape[1])
    if len(shape) == 3:
        return ap.rearrange("p (a b c) -> p a b c", b=shape[1], c=shape[2])
    return ap


def wide(ap, n):
    return ap.unsqueeze(2).broadcast_to([ap.shape[0], ap.shape[1], n])


def over(ap, n):
    return ap.unsqueeze(1).broadcast_to([ap.shape[0], n, ap.shape[1]])


def stage_setup(nc, c, t):
    with ExitStack() as ctx:
        sem = lambda n: c.semaphore(n)
        loaded, base, ready, cleared = sem("su_loaded"), sem("su_base"), sem("su_ready"), sem("su_cleared")
        filled, ints, copied = sem("su_filled"), sem("su_ints"), sem("su_copied")
        jint = ctx.enter_context(nc.sbuf_tensor("jint", [P, TILES], I32))
        pint = ctx.enter_context(nc.sbuf_tensor("pint", [P, 8], I32))
        fill = ctx.enter_context(nc.sbuf_tensor("fill", [P, SLOTS * 2 // P], F32))
        loads = [(c.src_i, t["src"].rearrange("(p n) -> p n", p=P)),
                 (c.dst_i, t["dst"].rearrange("(p n) -> p n", p=P))]
        whole = N // P * P
        block = ctx.enter_context(nc.Block())

        @block.sync
        def _(sp):
            for dst, src in loads:
                sp.dma_start(dst, src).then_inc(loaded, 16)
            sp.dma_start(c.x[:, 0:N // P, :], t["x"][0:whole, :].rearrange("(t p) f -> p t f", p=P)).then_inc(loaded, 16)
            sp.wait_ge(cleared, 1)
            sp.dma_start(c.x[0:N - whole, N // P, :], t["x"][whole:N, :]).then_inc(loaded, 16)
            sp.wait_ge(filled, 1)
            sp.dma_start(c.records.rearrange("(p n) two -> p (n two)", p=P), fill[:, :]).then_inc(loaded, 16)
            sp.wait_ge(loaded, 16 * (len(loads) + 3))

        @block.gpsimd
        def _(pool):
            pool.iota(jint[:, :], [[1, TILES]], base=0, channel_multiplier=0).then_inc(ints, 1)
            pool.iota(pint[:, :], [[0, 8]], base=0, channel_multiplier=1).then_inc(ints, 1)
            pool.memset(c.ones[:, :], 1.0).then_inc(base, 1)
            pool.memset(c.ident[:, :], 0.0).then_inc(base, 1)
            pool.wait_ge(base, 2)
            pool.affine_select(out=c.ident[:, :], in_=c.ident[:, :], compare_op=ALU.not_equal, fill=1.0,
                               base=0, pattern=[[-1, P]], channel_multiplier=1).then_inc(base, 1)
            pool.affine_select(out=c.before[:, :], in_=c.ones[:, :], compare_op=ALU.is_gt, fill=0.0,
                               base=0, pattern=[[1, P]], channel_multiplier=-1).then_inc(base, 1)
            pool.affine_select(out=c.previous[:, :], in_=c.ones[:, :], compare_op=ALU.is_equal, fill=0.0,
                               base=1, pattern=[[-1, P]], channel_multiplier=1).then_inc(base, 1)
            pool.wait_ge(base, 5)
            pool.memset(fill[:, :], float(NOWHERE)).then_inc(filled, 1)

        @block.scalar
        def _(act):
            act.wait_ge(loaded, 16 * (len(loads) + 3))
            act.activation(c.src_f[:, :], c.src_i, ACT.Copy).then_inc(copied, 1)
            act.activation(c.dst_f[:, :], c.dst_i, ACT.Copy).then_inc(copied, 1)

        @block.vector
        def _(dve):
            dve.memset(c.x[:, N // P:NT, :], 0.0).then_inc(cleared, 1)
            dve.wait_ge(ints, 2)
            dve.tensor_copy(c.j[:, :], jint[:, :]).then_inc(ready, 1)
            dve.tensor_copy(c.part[:, :], pint[:, 0:1]).then_inc(ready, 1)
            dve.wait_ge(ready, 2)
            dve.tensor_scalar(c.bounds[:, :], c.j[:, 0:NB], float(P), float(P), ALU.mult, ALU.add).then_inc(ready, 1)


def stage_lists(nc, c, t):
    with ExitStack() as ctx:
        sem = lambda n: c.semaphore(n)
        sb = lambda n, s, d: ctx.enter_context(nc.sbuf_tensor(n, s, d))
        pb = lambda n, s, d: ctx.enter_context(nc.psum_tensor(n, s, d))
        counted, tick, v, m = sem("li_counted"), sem("li_tick"), sem("li_v"), sem("li_m")
        gathered, floats, turned = [sem(f"li_gathered{i}") for i in range(3)], sem("li_floats"), sem("li_turned")
        sined = sem("li_sined")
        junk = sb("li_junk", [P, CHUNK], F32)
        count = {s: sb(f"li_count_{s}", [P, NB], F32) for s in "ds"}
        small = {s: sb(f"li_small_{s}", [P, 8], F32) for s in "ds"}
        whole = {s: sb(f"li_whole_{s}", [P, 1], I32) for s in "ds"}
        inside, past, wider = arena(c, B1_0, [TILES]), arena(c, B1_0 + TILES, [TILES]), sb("li_wider", [P, P], F32)
        slot0 = sb("li_slot0", [NB, NB], F32)
        own = sb("li_own", [P, NB], F32)
        cols_f, cols_i = sb("li_cols_f", [P, 8], F32), sb("li_cols_i", [P, 8], I32)
        fields_i = arena(c, ACC0, [2, JC, P], I32)
        fields = arena(c, B1_0 + 2 * TILES, [3, JC, P])
        bucket_f = arena(c, B2_0, [TILES])
        mask, mask2 = arena(c, B2_0 + TILES, [TILES]), arena(c, B2_0 + 2 * TILES, [TILES])
        half = TILES // 2
        ps = pb("li_ps", [P, 512], F32)
        psw = pb("li_psw", [P, 2, 512], F32)
        psb = pb("li_psb", [P, 2, 512], F32)
        psf = pb("li_psf", [P, 2, 512], F32)
        flat = {"src": t["src"], "dst": t["dst"], "w": t["edge_weight"]}
        block = ctx.enter_context(nc.Block())
        V = {}
        M = {name: n + 1 for n, name in enumerate([
            "dends", "dstarts", "dfirst", "cols", "dbucket", "sends", "sstarts", "sfirst", "sbucket", "base",
            "turnedsrc", "turneddst", "turnedw"])}

        @block.vector
        def _(dve):
            n = [0]

            def done(ins, name=None):
                n[0] += 1
                ins.then_inc(v, 1)
                if name:
                    V[name] = n[0]
                dve.wait_ge(v, n[0])

            def counts(side, key):
                def one(b):
                    return dve.tensor_scalar(junk[:, :], key[:, :], c.bounds[:, bass.ds(b, 1)], 0.0, ALU.is_lt,
                                             ALU.add, accum_out=count[side][:, bass.ds(b, 1)])
                base = 0 if side == "d" else NB
                if base:
                    dve.wait_ge(counted, base)
                one(0).then_inc(counted, 1)
                with dve.Fori(1, NB) as b:
                    at_least(dve, counted, b + base, tick)
                    one(b).then_inc(counted, 1)
                dve.wait_ge(counted, base + NB)

            def tiles_of(side):
                s = small[side][0:NB, :]
                dve.wait_ge(m, M[side + "ends"])
                done(dve.tensor_copy(s[:, 0:1], ps[0:NB, 0:1]), side + "ends")
                dve.wait_ge(m, M[side + "starts"])
                done(dve.tensor_copy(s[:, 1:2], ps[0:NB, 1:2]))
                done(dve.tensor_tensor(s[:, 2:3], s[:, 0:1], s[:, 1:2], ALU.subtract))
                done(dve.tensor_scalar(whole[side][0:NB, :], s[:, 2:3], float(P - 1), None, ALU.add))
                done(dve.tensor_scalar(whole[side][0:NB, :], whole[side][0:NB, :], 7, None, ALU.arith_shift_right))
                done(dve.tensor_copy(s[:, 3:4], whole[side][0:NB, :]))
                done(dve.tensor_scalar(s[:, 3:4], s[:, 3:4], 1.0, None, ALU.max), side + "tiles")
                dve.wait_ge(m, M[side + "first"])
                done(dve.tensor_copy(s[:, 4:5], ps[0:NB, 2:3]))
                done(dve.tensor_tensor(s[:, 5:6], s[:, 4:5], s[:, 3:4], ALU.add))
                done(dve.scalar_tensor_tensor(out=s[:, 6:7], in0=s[:, 4:5], scalar=-float(P), in1=s[:, 1:2],
                                              op0=ALU.mult, op1=ALU.add))
                done(dve.tensor_scalar(past[0:NB, :], c.j[0:NB, :], s[:, 5:6], None, ALU.is_ge), side + "past")

            counts("d", c.dst_f)
            tiles_of("d")
            s = small["d"][0:NB, :]
            done(dve.tensor_scalar(inside[0:NB, :], c.j[0:NB, :], s[:, 4:5], None, ALU.is_ge))
            done(dve.tensor_tensor(inside[0:NB, :], inside[0:NB, :], past[0:NB, :], ALU.subtract))
            done(dve.tensor_scalar(wider[0:NB, :], c.ones[0:NB, :], s[:, 6:7], None, ALU.mult), "wider")
            done(dve.memset(cols_f[:, :], 0.0))
            dve.wait_ge(m, M["cols"])
            for k in range(JC):
                q = min(P, TILES - k * P)
                done(dve.tensor_scalar(cols_f[0:q, k:k + 1], c.part[0:q, :], float(P), float(k * P * P), ALU.mult, ALU.add))
                done(dve.tensor_tensor(cols_f[0:q, k:k + 1], cols_f[0:q, k:k + 1], ps[0:q, 8 + k:9 + k], ALU.add))
            done(dve.tensor_scalar(cols_i[:, :], cols_f[:, :], float(E - 1), None, ALU.min), "columns")
            dve.wait_ge(m, M["dbucket"])
            for h in range(2):
                at = slice(h * half, (h + 1) * half)
                done(dve.scalar_tensor_tensor(out=mask[32:33, at], in0=c.j[32:33, at], scalar=float(P), in1=psw[32:33, h, 0:half],
                                              op0=ALU.mult, op1=ALU.add))
                done(dve.tensor_copy(bucket_f[:, at], psb[:, h, 0:half]))
            done(dve.tensor_scalar(c.edge0, mask[32:33, :], float(E - 1), None, ALU.min))
            done(dve.tensor_copy(c.bucket_d, bucket_f[0:1, :]), "dused")

            counts("s", c.src_f)
            tiles_of("s")
            dve.wait_ge(m, M["sbucket"])
            for h in range(2):
                at = slice(h * half, (h + 1) * half)
                done(dve.tensor_scalar(c.window_s[:, at], psb[:, h, 0:half], float(P), None, ALU.mult))
                done(dve.tensor_copy(c.bucket_s[:, at], psb[64:65, h, 0:half]))
            done(dve.tensor_scalar(slot0[:, :], c.ident[0:NB, 0:NB], small["s"][0:NB, 4:5], float(P), ALU.mult, ALU.mult))
            done(dve.tensor_copy(own[:, :], count["s"][:, :]))
            done(dve.tensor_tensor(own[:, 1:NB], count["s"][:, 1:NB], count["s"][:, 0:NB - 1], ALU.subtract), "own")
            dve.wait_ge(m, M["base"])
            done(dve.tensor_scalar(c.base[:, :], ps[:, 64:64 + NB], -1.0, None, ALU.add))
            done(dve.tensor_scalar(c.src_i, c.src_i, 7, None, ALU.arith_shift_right))
            done(dve.tensor_copy(c.src_bucket[:, :], c.src_i))
            done(dve.tensor_scalar(c.slot_of[:, :], c.src_bucket[:, :], float(NB), float(4 * SLOTS), ALU.is_ge, ALU.mult))

            for f, name in enumerate(["src", "dst", "w"]):
                dve.wait_ge(m, M["turned" + name])
                for h, (a, b) in enumerate(((0, 512), (512, TILES))):
                    got = psf[:, h, 0:b - a]
                    if name == "src":
                        ins = dve.tensor_scalar(c.gather_d[:, a:b], got, float(N - 1), None, ALU.min)
                    elif name == "dst":
                        ins = dve.scalar_tensor_tensor(out=c.local_d[:, a:b], in0=bucket_f[:, a:b], scalar=-float(P), in1=got,
                                                       op0=ALU.mult, op1=ALU.add)
                    else:
                        ins = dve.tensor_copy(c.weight[:, a:b], got)
                    done(ins, f"took{name}{h}")
            done(dve.tensor_scalar(mask, c.local_d[:, :], 0.0, None, ALU.is_ge))
            done(dve.tensor_scalar(mask2, c.local_d[:, :], float(P), None, ALU.is_lt))
            done(dve.tensor_tensor(mask, mask, mask2, ALU.mult))
            done(dve.scalar_tensor_tensor(out=mask2, in0=bucket_f, scalar=float(P), in1=c.local_d[:, :], op0=ALU.mult, op1=ALU.add))
            done(dve.scalar_tensor_tensor(out=mask, in0=mask2, scalar=1.0, in1=mask, op0=ALU.add, op1=ALU.mult))
            done(dve.tensor_scalar(c.key[:, :], mask, -1.0, None, ALU.add))
            big = 1.5 * 2.0 ** 23
            done(dve.tensor_scalar(mask, c.weight[:, :], 1.0 / 20.0, None, ALU.mult))
            done(dve.tensor_scalar(mask2, mask, big, None, ALU.add))
            done(dve.tensor_scalar(mask2, mask2, -big, None, ALU.add))
            done(dve.tensor_tensor(mask, mask, mask2, ALU.subtract), "sine_arg")
            dve.wait_ge(sined, 1)
            done(dve.tensor_tensor(mask, mask2, mask2, ALU.mult))
            done(dve.tensor_scalar(c.cutoff[:, :], mask, -1.0, 1.0, ALU.mult, ALU.add))

        @block.gpsimd
        def _(pool):
            pool.wait_ge(v, V["columns"])
            for f, name in enumerate(["src", "dst", "w"]):
                table = flat[name].rearrange("(e one) -> e one", one=1)
                for k in range(JC):
                    to = fields[:, 2, k, :] if name == "w" else fields_i[:, f, k, :]
                    pool.indirect_dma_start(to, None, table, bass.IndirectOffsetOnAxis(cols_i[:, k:k + 1], 0))\
                        .then_inc(gathered[f], 16)

        @block.scalar
        def _(act):
            for f in range(2):
                act.wait_ge(gathered[f], 16 * JC)
                act.activation(fields[:, f, :, :], fields_i[:, f, :, :], ACT.Copy).then_inc(floats, 1)
            act.wait_ge(v, V["sine_arg"])
            act.activation(mask2, mask, ACT.Sin, scale=3.141592653589793).then_inc(sined, 1)

        @block.tensor
        def _(pe):
            n = [0]

            def mark(ins, name):
                n[0] += 1
                ins.then_inc(m, 1)
                assert M[name] == n[0]

            for side in "ds":
                s = small[side]
                pe.wait_ge(counted, NB if side == "d" else 2 * NB)
                if side == "s":
                    pe.wait_ge(v, V["dused"])
                mark(pe.matmul(ps[0:NB, 0:1], count[side][:, :], c.ones[:, 0:1], start=True, stop=True), side + "ends")
                pe.wait_ge(v, V[side + "ends"])
                mark(pe.matmul(ps[0:NB, 1:2], c.previous[0:NB, 0:NB], s[0:NB, 0:1], start=True, stop=True), side + "starts")
                pe.wait_ge(v, V[side + "tiles"])
                mark(pe.matmul(ps[0:NB, 2:3], c.before[0:NB, 0:NB], s[0:NB, 3:4], start=True, stop=True), side + "first")
                if side == "d":
                    pe.wait_ge(v, V["wider"])
                    for k in range(JC):
                        q = min(P, TILES - k * P)
                        ins = pe.matmul(ps[0:q, 8 + k:9 + k], inside[0:NB, k * P:k * P + q], s[0:NB, 6:7], start=True, stop=True)
                    mark(ins, "cols")
                    for h in range(2):
                        pe.matmul(psw[:, h, 0:half], wider[0:NB, :], inside[0:NB, h * half:(h + 1) * half], start=True, stop=True)
                pe.wait_ge(v, V[side + "past"])
                for h in range(2):
                    ins = pe.matmul(psb[:, h, 0:half], c.ones[0:NB, :], past[0:NB, h * half:(h + 1) * half], start=True, stop=True)
                mark(ins, side + "bucket")
            pe.wait_ge(v, V["own"])
            pe.matmul(ps[:, 64:64 + NB], c.before[:, :], own[:, :], start=True, stop=False)
            mark(pe.matmul(ps[:, 64:64 + NB], c.ones[0:NB, :], slot0[:, :], start=False, stop=True), "base")
            for f, name in enumerate(["src", "dst", "w"]):
                if f < 2:
                    pe.wait_ge(floats, f + 1)
                else:
                    pe.wait_ge(gathered[2], 16 * JC)
                if f:
                    pe.wait_ge(v, V[f"took{['src', 'dst', 'w'][f - 1]}1"])
                for k in range(JC):
                    q = min(P, TILES - k * P)
                    ins = pe.transpose(psf[:, k // 4, k % 4 * P:k % 4 * P + q], fields[0:q, f, k, :], c.ident[0:q, 0:q])
                mark(ins, "turned" + name)


def sweep(nc, c, name, sources, products, vector=None, scalar=None, store=None):
    with ExitStack() as ctx:
        sem = lambda n: c.semaphore(name + n)
        turned, copied, multiplied, tick = sem("_turned"), sem("_copied"), sem("_multiplied"), sem("_tick")
        staged = sem("_staged")
        fixed = ctx.enter_context(nc.sbuf_tensor(name + "_fixed", [P, 2, len(sources), P], F32))
        vec, sca = sem("_vector"), sem("_scalar")
        stored = [sem(f"_stored{q}") for q in range(2)]
        xt = ctx.enter_context(nc.sbuf_tensor(name + "_xt", [P, 2, len(sources), P], F32))
        ring = ctx.enter_context(nc.sbuf_tensor(name + "_ring", [P, 2, 384], F32)) if store else None
        pt = ctx.enter_context(nc.psum_tensor(name + "_pt", [P, 2, 512], F32))
        po = ctx.enter_context(nc.psum_tensor(name + "_po", [P, 2, 512], F32))
        n_src = len(sources)
        n_store = len(store(0)) if store else 0
        block = ctx.enter_context(nc.Block())

        @block.gpsimd
        def _(pool):
            def step(k, i, q):
                at_least(pool, turned, k - 1, tick)
                for s, (src, m) in enumerate(sources):
                    pool.tensor_copy(fixed[:, q, s, 0:m], src(k)).then_inc(staged, 1)
            rounds(pool, NT, 2, step)

        @block.tensor
        def _(pe):
            def turn(k, q):
                at_least(pe, staged, n_src * (k + 1), tick)
                at_least(pe, copied, n_src * (k - 1), tick)
                for s, (src, m) in enumerate(sources):
                    ins = pe.transpose(pt[0:m, q, s * P:(s + 1) * P], fixed[:, q, s, 0:m], c.ident[:, :])
                ins.then_inc(turned, 1)

            def multiply(k, q):
                at_least(pe, copied, n_src * (k + 1), tick)
                if vector:
                    at_least(pe, vec, k - 1, tick)
                if scalar:
                    at_least(pe, sca, k - 1, tick)
                for n, (s, rhs, a, b) in enumerate(products):
                    m = rhs.shape[0]
                    lhs = c.ones[0:m, :] if s is None else xt[0:m, q, s, :]
                    ins = pe.matmul(po[:, q, a:b], lhs, rhs, start=(n == 0), stop=(n == len(products) - 1))
                ins.then_inc(multiplied, 1)

            def step(k, i, q):
                turn(k, q)
                if not isinstance(k, int) or k > 0:
                    multiply(k - 1, 1 - q)
            rounds(pe, NT, 2, step)
            multiply(NT - 1, (NT - 1) % 2)

        @block.scalar
        def _(act):
            def copy(k, q):
                at_least(act, turned, k + 1, tick)
                at_least(act, multiplied, k - 1, tick)
                for s, (src, m) in enumerate(sources):
                    act.activation(xt[0:m, q, s, :], pt[0:m, q, s * P:(s + 1) * P], ACT.Copy).then_inc(copied, 1)

            def evacuate(k, i, q):
                at_least(act, multiplied, k + 1, tick)
                if vector:
                    at_least(act, vec, k + 1, tick)
                if store:
                    at_least(act, stored[q], i * 16 * n_store, tick)
                scalar(act, k, po[:, q, :], ring[:, q, :] if store else None).then_inc(sca, 1)

            def step(k, i, q):
                copy(k, q)
                if scalar and (not isinstance(k, int) or k > 0):
                    evacuate(k - 1, i if q else i - 1, 1 - q)
            rounds(act, NT, 2, step, peeled=2)
            if scalar:
                evacuate(NT - 1, NT // 2 - 1, 1)

        if vector:
            @block.vector
            def _(dve):
                def step(k, i, q):
                    at_least(dve, multiplied, k + 1, tick)
                    vector(dve, k, po[:, q, :]).then_inc(vec, 1)
                rounds(dve, NT, 2, step)

        if store:
            @block.sync
            def _(sp):
                def step(k, i, q):
                    at_least(sp, sca, k + 1, tick)
                    for dram, a, b in store(k):
                        sp.dma_start(dram, ring[:, q, a:b]).then_inc(stored[q], 16)
                rounds(sp, NT, 2, step)
                for q in range(2):
                    sp.wait_ge(stored[q], NT // 2 * 16 * n_store)


def vector_scalar_stage(nc, c, name, steps):
    with ExitStack() as ctx:
        done = c.semaphore(name + "_done")
        block = ctx.enter_context(nc.Block())

        def run(eng, mine):
            for n, (who, step) in enumerate(steps):
                if who == mine:
                    if n:
                        eng.wait_ge(done, n)
                    step(eng).then_inc(done, 1)

        @block.vector
        def _(dve):
            run(dve, "v")

        @block.scalar
        def _(act):
            run(act, "s")


def norm_steps(c, y, squares, small, gamma=None, beta=None, residual=None, out=None):
    s, r = small[:, 0, :], small[:, 1, :]
    steps = [
        ("v", lambda e: e.tensor_reduce(s, y, AX_X, ALU.add)),
        ("v", lambda e: e.tensor_scalar(s, s, 1.0 / F, None, ALU.mult)),
        ("v", lambda e: e.tensor_tensor(y, y, wide(s, F), ALU.subtract)),
        ("s", lambda e: e.activation(squares, y, ACT.Square)),
        ("v", lambda e: e.tensor_reduce(s, squares, AX_X, ALU.add)),
        ("v", lambda e: e.tensor_scalar(s, s, 1.0 / F, LN_EPS, ALU.mult, ALU.add)),
        ("s", lambda e: e.activation(r, s, ACT.Sqrt)),
        ("v", lambda e: e.reciprocal(s, r)),
        ("v", lambda e: e.tensor_tensor(y if out is None else out, y, wide(s, F), ALU.mult)),
    ]
    if gamma is not None:
        steps += [("v", lambda e: e.tensor_tensor(y, y, over(gamma, NT), ALU.mult)),
                  ("v", lambda e: e.tensor_tensor(y, y, over(beta, NT), ALU.add))]
    if residual is not None:
        steps += [("v", lambda e: e.tensor_tensor(y, y, residual, ALU.add))]
    return steps


def split_steps(full, parts):
    return [
        ("s", lambda e: e.activation(parts[0], full, ACT.Copy)),
        ("v", lambda e: e.tensor_tensor(full, full, parts[0], ALU.subtract)),
        ("s", lambda e: e.activation(parts[1], full, ACT.Copy)),
        ("v", lambda e: e.tensor_tensor(full, full, parts[1], ALU.subtract)),
        ("s", lambda e: e.activation(parts[2], full, ACT.Copy)),
    ]


def gather_rows(pool, c, table, index, ring, index_ready, arrived, freed, tick):
    def step(k, i, r):
        at_least(pool, index_ready, k + 1, tick)
        for sem, per in freed:
            if isinstance(sem, list):
                at_least(pool, sem[r], per * i, tick)
            else:
                at_least(pool, sem, per * (k - R + 1), tick)
        for u in range(U):
            pool.indirect_dma_start(ring[:, r, u, :], None, table, bass.IndirectOffsetOnAxis(index[:, r, u:u + 1], 0))\
                .then_inc(arrived[r], 16)
    rounds(pool, BATCHES, R, step)


def take_index(act, source, index, k, i, r, arrived, index_ready, tick):
    at_least(act, arrived[r], i * 16 * U, tick)
    act.activation(index[:, r, :], source[:, bass.ds(k * U, U)], ACT.Copy).then_inc(index_ready, 1)


def is_first(k):
    return isinstance(k, int) and k == 0


def loaded_values(nc, row, k, engine, top):
    return nc.values_load_multi_w_load_instructions(
        row[:, bass.ds(k * U, U)], engines=(engine,), min_val=0, max_val=top,
        skip_runtime_bounds_check_because="the vector engine made them within these bounds")[1]


def add_to_buckets(nc, dve, acc, buckets, psum, width, k, added, tick):
    which = loaded_values(nc, buckets, k, DVE_ENGINE, NT - 1)
    for u in range(U):
        at_least(dve, added, k * U + u, tick)
        to = acc[:, bass.ds(which[u], 1), 0:width].rearrange("p one f -> p (one f)")
        dve.tensor_tensor(to, to, psum[:, u, 0:width], ALU.add).then_inc(added, 1)


def stage_attention_scores(nc, c):
    with ExitStack() as ctx:
        sem = lambda n: c.semaphore("at_" + n)
        sb = lambda n, s, d: ctx.enter_context(nc.sbuf_tensor("at_" + n, s, d))
        index, ring = sb("index", [P, R, U], I32), sb("ring", [P, R, U, 2 * F], F32)
        hot, hot_t, prod, we = sb("hot", [P, 2, U, P], F32), sb("hot_t", [P, 2, U, P], BF16), sb("prod", [P, 2, U, F], F32), sb("we", [P, 2, U, H], F32)
        rank, match = sb("rank", [P, CHUNK], F32), sb("match", [P, CHUNK], F32)
        pt = ctx.enter_context(nc.psum_tensor("at_pt", [P, 2, U, P], F32))
        pq = ctx.enter_context(nc.psum_tensor("at_pq", [P, 2, U, 256], F32))
        index_ready, arrived, kept = sem("index"), [sem(f"arrived{r}") for r in range(R)], [sem(f"kept{r}") for r in range(R)]
        hots, turned, copied, queried, producted, reduced, weighed, scored, ranked, tick = (
            sem(n) for n in ("hots", "turned", "copied", "queried", "producted", "reduced", "weighed", "scored", "ranked", "tick"))
        block = ctx.enter_context(nc.Block())

        @block.gpsimd
        def _(pool):
            gather_rows(pool, c, c.kv, index, ring, index_ready, arrived, [(producted, 1), (kept, 16)], tick)

        @block.sync
        def _(sp):
            def step(k, i, r):
                at_least(sp, arrived[r], 16 * U * (i + 1), tick)
                sp.dma_start(c.values[bass.ds(k, 1), :, :, :].rearrange("one p u f -> p (one u) f"), ring[:, r, :, F:2 * F]).then_inc(kept[r], 16)
            rounds(sp, BATCHES, R, step)
            for r in range(R):
                sp.wait_ge(kept[r], 16 * BATCHES // R)

        @block.scalar
        def _(act):
            def copy(k, q):
                at_least(act, turned, k + 1, tick)
                at_least(act, queried, k - 1, tick)
                act.activation(hot_t[:, q, :, :], pt[:, q, :, :], ACT.Copy).then_inc(copied, 1)

            def step(k, i, r):
                take_index(act, c.gather_d, index, k, i, r, arrived, index_ready, tick)
                if not is_first(k):
                    copy(k - 1, (r - 1) % 2)
            rounds(act, BATCHES, R, step)
            copy(BATCHES - 1, 1)

        @block.tensor
        def _(pe):
            def turn(k, q):
                at_least(pe, hots, k + 1, tick)
                at_least(pe, copied, k - 1, tick)
                for u in range(U):
                    ins = pe.transpose(pt[:, q, u, :], hot[:, q, u, :], c.ident[:, :])
                ins.then_inc(turned, 1)

            def query(k, q):
                which = loaded_values(nc, c.bucket_d, k, PE_ENGINE, NT - 1)
                at_least(pe, copied, k + 1, tick)
                at_least(pe, weighed, k - 1, tick)
                at_least(pe, producted, k - 1, tick)
                for u in range(U):
                    for n, part in enumerate(c.query_parts):
                        ins = pe.matmul(pq[:, q, u, 0:QW], hot_t[:, q, u, :],
                                        part[:, bass.ds(which[u], 1), :].rearrange("p one f -> p (one f)"),
                                        start=(n == 0), stop=(n == 2))
                ins.then_inc(queried, 1)

            def step(k, i, r):
                turn(k, r % 2)
                if not is_first(k):
                    query(k - 1, (r - 1) % 2)
            rounds(pe, BATCHES, R, step)
            query(BATCHES - 1, 1)

        @block.vector
        def _(dve):
            def one_hot(k, q):
                at_least(dve, turned, k - 1, tick)
                dve.tensor_tensor(hot[:, q, :, :], over(c.j[:, 0:P], U), wide(c.local_d[:, bass.ds(k * U, U)], P), ALU.is_equal).then_inc(hots, 1)

            def score(k, i, r):
                q = r % 2
                at_least(dve, queried, k + 1, tick)
                at_least(dve, arrived[r], 16 * U * (i + 1), tick)
                at_least(dve, reduced, k - 1, tick)
                dve.tensor_tensor(prod[:, q, :, :], pq[:, q, :, 0:F], ring[:, r, :, 0:F], ALU.mult).then_inc(producted, 1)
                at_least(dve, scored, k - 1, tick)
                dve.tensor_tensor(we[:, q, :, :], pq[:, q, :, F:QW], wide(c.weight[:, bass.ds(k * U, U)], H), ALU.mult).then_inc(weighed, 1)
                at_least(dve, producted, k + 1, tick)
                to = c.alpha[:, bass.ds(k * U, U), :].rearrange("p u h -> p (u h)")
                dve.tensor_reduce(to, prod[:, q, :, :].rearrange("p u (h d) -> p (u h) d", d=D), AX_X, ALU.add).then_inc(reduced, 1)
                at_least(dve, reduced, k + 1, tick)
                at_least(dve, weighed, k + 1, tick)
                dve.tensor_tensor(to, to, we[:, q, :, :].rearrange("p u h -> p (u h)"), ALU.add).then_inc(scored, 1)

            def rank_bucket(b):
                at_least(dve, ranked, b * 4, tick)
                dve.tensor_scalar(match[:, :], c.src_bucket[:, :], c.j[:, bass.ds(b, 1)], None, ALU.is_equal).then_inc(ranked, 1)
                at_least(dve, ranked, b * 4 + 1, tick)
                dve.tensor_tensor_scan(rank[:, :], c.ones[:, 0:1].broadcast_to([P, CHUNK]), match[:, :], c.base[:, bass.ds(b, 1)], ALU.mult, ALU.add).then_inc(ranked, 1)
                at_least(dve, ranked, b * 4 + 2, tick)
                dve.tensor_tensor(rank[:, :], rank[:, :], match[:, :], ALU.mult).then_inc(ranked, 1)
                at_least(dve, ranked, b * 4 + 3, tick)
                dve.tensor_tensor(c.slot_of[:, :], c.slot_of[:, :], rank[:, :], ALU.add).then_inc(ranked, 1)

            def step(k, i, r):
                one_hot(k, r % 2)
                if not is_first(k):
                    score(k - 1, i if r else i - 1, (r - 1) % R)
            for r in range(R):
                step(r, 0, r)
            rank_bucket(0)
            with dve.Fori(1, NB) as i:
                for r in range(R):
                    step(i * R + r, i, r)
                rank_bucket(i)
            with dve.Fori(NB, BATCHES // R) as i:
                for r in range(R):
                    step(i * R + r, i, r)
            score(BATCHES - 1, BATCHES // R - 1, R - 1)
            dve.wait_ge(scored, BATCHES)


def stage_attention_max(nc, c):
    with ExitStack() as ctx:
        v, m, s = (c.semaphore("mx_" + n) for n in ("v", "m", "s"))
        sb = lambda n, shape: ctx.enter_context(nc.sbuf_tensor("mx_" + n, shape, F32))
        a = arena(c, ACC0, [H, SL])[0:SP_PARTS, :, :]
        b = arena(c, ACC0 + H * SL, [H, SL])[0:SP_PARTS, :, :]
        pen, keys = sb("pen", [P, SL + 2]), sb("keys", [P, SL])
        ends, carry = sb("ends", [P, 4, H]), sb("carry", [P, 2, H])
        row = sb("row", [H, 10, P])
        pt = ctx.enter_context(nc.psum_tensor("mx_pt", [P, 4, 512], F32))
        Q = SP_PARTS
        pieces = [(h, g) for h in range(H) for g in range(SQ // 4)]
        block = ctx.enter_context(nc.Block())
        V, M, S = {}, {}, {}
        order = [f"keys{g}" for g in range(SQ // 4)] + [f"in{h}{g}" for h, g in pieces] + ["ends", "back0", "ends1", "back1"]
        order += [f"out{n}" for n in range(2 * H)]
        for n, name in enumerate(order):
            M[name] = n + 1
        takes = ([f"keys{g}" for g in range(SQ // 4)] + [f"in{h}{g}" for h, g in pieces])
        for n, name in enumerate(takes):
            S[name] = n + 1

        @block.vector
        def _(dve):
            n = [0]

            def done(ins, name=None):
                n[0] += 1
                ins.then_inc(v, 1)
                if name:
                    V[name] = n[0]
                dve.wait_ge(v, n[0])

            dve.wait_ge(s, S[f"keys{SQ // 4 - 1}"])
            done(dve.memset(pen[:, :], 0.0))
            done(dve.tensor_tensor(pen[0:Q, 1:SL], keys[0:Q, 1:SL], keys[0:Q, 0:SL - 1], ALU.not_equal))
            done(dve.tensor_scalar(pen[0:Q, 1:SL], pen[0:Q, 1:SL], FAR, None, ALU.mult))
            done(dve.tensor_copy(ends[0:Q, 2, :], keys[0:Q, 0:1].broadcast_to([Q, H])))
            done(dve.tensor_copy(ends[0:Q, 3, :], keys[0:Q, SL - 1:SL].broadcast_to([Q, H])))
            dve.wait_ge(s, len(takes))

            def scan(to, src, initial, backward):
                for h in range(H):
                    x0 = initial if isinstance(initial, float) else initial[0:Q, h:h + 1]
                    if backward:
                        ins = dve.tensor_tensor_scan(to[:, h, ::-1], pen[0:Q, 1:SL + 1][:, ::-1], src[:, h, ::-1], x0, ALU.add, ALU.max)
                    else:
                        ins = dve.tensor_tensor_scan(to[:, h, :], pen[0:Q, 0:SL], src[:, h, :], x0, ALU.add, ALU.max)
                    n[0] += 1
                    ins.then_inc(v, 1)
                dve.wait_ge(v, n[0])

            scan(b, a, FAR, False)
            done(dve.tensor_copy(ends[0:Q, 0, :], b[:, :, SL - 1]), "ends")
            dve.wait_ge(m, M["ends"])
            for f, w in ((0, 2), (1, 3), (2, 0)):
                done(dve.tensor_copy(row[:, f, 0:Q], pt[0:H, 0, w * P:w * P + Q]), "took")
            done(dve.tensor_tensor(row[:, 3, 0:Q], row[:, 0, 0:Q], row[:, 1, 0:Q], ALU.is_equal))
            done(dve.memset(row[:, 4, :], 0.0))
            done(dve.tensor_tensor(row[:, 4, 1:Q], row[:, 0, 1:Q], row[:, 1, 0:Q - 1], ALU.is_equal))
            done(dve.tensor_tensor(row[:, 5, 0:Q], row[:, 3, 0:Q], row[:, 4, 0:Q], ALU.mult))
            done(dve.tensor_scalar(row[:, 5, 0:Q], row[:, 5, 0:Q], -FAR, FAR, ALU.mult, ALU.add))
            done(dve.tensor_tensor_scan(row[:, 6, 0:Q], row[:, 5, 0:Q], row[:, 2, 0:Q], FAR, ALU.add, ALU.max))
            done(dve.tensor_scalar(row[:, 8, 0:Q], row[:, 4, 0:Q], -FAR, FAR, ALU.mult, ALU.add))
            done(dve.memset(row[:, 7, :], FAR))
            done(dve.tensor_tensor(row[:, 7, 1:Q], row[:, 8, 1:Q], row[:, 6, 0:Q - 1], ALU.add), "carry0")
            dve.wait_ge(m, M["back0"])
            done(dve.tensor_copy(carry[0:Q, 0, :], pt[0:Q, 1, 0:H]))
            scan(b, a, carry[:, 0, :], False)
            scan(a, b, FAR, True)
            done(dve.tensor_copy(ends[0:Q, 1, :], a[:, :, 0]), "ends1")
            dve.wait_ge(m, M["ends1"])
            done(dve.tensor_copy(row[:, 2, 0:Q], pt[0:H, 0, P:P + Q]))
            done(dve.memset(row[:, 5, :], 0.0))
            done(dve.tensor_tensor(row[:, 5, 0:Q - 1], row[:, 3, 0:Q - 1], row[:, 4, 1:Q], ALU.mult))
            done(dve.tensor_scalar(row[:, 5, 0:Q], row[:, 5, 0:Q], -FAR, FAR, ALU.mult, ALU.add))
            done(dve.tensor_tensor_scan(row[:, 6, 0:Q][:, ::-1], row[:, 5, 0:Q][:, ::-1], row[:, 2, 0:Q][:, ::-1], FAR, ALU.add, ALU.max))
            done(dve.memset(row[:, 7, :], FAR))
            done(dve.tensor_tensor(row[:, 7, 0:Q - 1], row[:, 8, 1:Q], row[:, 6, 1:Q], ALU.add), "carry1")
            dve.wait_ge(m, M["back1"])
            done(dve.tensor_copy(carry[0:Q, 1, :], pt[0:Q, 1, 0:H]))
            scan(a, b, carry[:, 1, :], True)
            V["max"] = n[0]
            for h in range(H):
                for g in range(2):
                    k = 2 * h + g
                    dve.wait_ge(m, M[f"out{k}"])
                    got = pt[:, 2 + k % 2, 0:4 * Q].rearrange("p (i q) -> p q i", i=4)
                    al = c.alpha[:, :, h].rearrange("p (q i) -> p q i", i=SQ)[:, :, 4 * g:4 * g + 4]
                    done(dve.tensor_tensor(al, al, got, ALU.subtract), f"out{k}")
            done(dve.tensor_scalar(c.alpha[:, :, :], c.alpha[:, :, :], 0.0, None, ALU.min), "cut")

        @block.tensor
        def _(pe):
            def mark(ins, name):
                ins.then_inc(m, 1)

            bank = 0
            for g in range(SQ // 4):
                for i in range(4):
                    ins = pe.transpose(pt[0:Q, bank, i * P:(i + 1) * P], c.key[:, 4 * g + i::SQ], c.ident[:, :])
                mark(ins, f"keys{g}")
                bank += 1
            for h, g in pieces:
                if bank >= 4:
                    pe.wait_ge(s, bank - 3)
                for i in range(4):
                    ins = pe.transpose(pt[0:Q, bank % 4, i * P:(i + 1) * P], c.alpha[:, 4 * g + i::SQ, h], c.ident[:, :])
                mark(ins, f"in{h}{g}")
                bank += 1
            pe.wait_ge(s, len(takes))
            pe.wait_ge(v, V["ends"])
            for w in (0, 2, 3):
                ins = pe.transpose(pt[0:H, 0, w * P:w * P + Q], ends[0:Q, w, :], c.ident[0:Q, 0:Q])
            mark(ins, "ends")
            pe.wait_ge(v, V["carry0"])
            mark(pe.transpose(pt[0:Q, 1, 0:H], row[:, 7, 0:Q], c.ident[0:H, 0:H]), "back0")
            pe.wait_ge(v, V["ends1"])
            mark(pe.transpose(pt[0:H, 0, P:P + Q], ends[0:Q, 1, :], c.ident[0:Q, 0:Q]), "ends1")
            pe.wait_ge(v, V["carry1"])
            mark(pe.transpose(pt[0:Q, 1, 0:H], row[:, 7, 0:Q], c.ident[0:H, 0:H]), "back1")
            pe.wait_ge(v, V["max"])
            for h in range(H):
                for g in range(2):
                    k = 2 * h + g
                    if k >= 2:
                        pe.wait_ge(v, V[f"out{k - 2}"])
                    for i in range(4):
                        ins = pe.transpose(pt[:, 2 + k % 2, i * Q:(i + 1) * Q],
                                           a[:, h, (4 * g + i) * P:(4 * g + i + 1) * P], c.ident[0:Q, 0:Q])
                    mark(ins, f"out{k}")

        @block.scalar
        def _(act):
            for n, name in enumerate(takes):
                act.wait_ge(m, M[name])
                src = pt[0:Q, n % 4, :]
                if name.startswith("keys"):
                    g = int(name[4:])
                    to = keys[0:Q, g * 512:(g + 1) * 512]
                else:
                    h, g = int(name[2]), int(name[3])
                    to = a[:, h, g * 512:(g + 1) * 512]
                act.activation(to, src, ACT.Copy).then_inc(s, 1)
            act.wait_ge(v, V["cut"])
            act.activation(c.alpha[:, :, :], c.alpha[:, :, :], ACT.Exp).then_inc(s, 1)


def stage_attention_sums(nc, c):
    with ExitStack() as ctx:
        sem = lambda n: c.semaphore("as_" + n)
        sb = lambda n, s, d: ctx.enter_context(nc.sbuf_tensor("as_" + n, s, d))
        acc = arena(c, ACC0, [NT, C_END])
        ring = sb("ring", [P, R, U, F], F32)
        hot, msg = sb("hot", [P, 2, U, P], F32), sb("msg", [P, 2, U, C_END], F32)
        slot, rec = sb("slot", [P, R, SU], I32), sb("rec", [P, R, SU, 2], F32)
        pa = ctx.enter_context(nc.psum_tensor("as_pa", [P, 2, U, 256], F32))
        arrived, scattered = [sem(f"arrived{r}") for r in range(R)], [sem(f"scattered{r}") for r in range(R)]
        hots, made, summed, added, packed, start, tick = (sem(n) for n in ("hots", "made", "summed", "added", "packed", "start", "tick"))
        block = ctx.enter_context(nc.Block())
        S_BATCHES = CHUNK // SU

        @block.gpsimd
        def _(pool):
            def step(k, i, r):
                at_least(pool, packed, 3 * (k + 1), tick)
                for u in range(SU):
                    pool.indirect_dma_start(c.records, bass.IndirectOffsetOnAxis(slot[:, r, u:u + 1], 0), rec[:, r, u, :], None,
                                            bounds_check=SLOTS - 1, oob_is_err=False).then_inc(scattered[r], 16)
            rounds(pool, S_BATCHES, R, step)
            for r in range(R):
                pool.wait_ge(scattered[r], 16 * SU * S_BATCHES // R)

        @block.scalar
        def _(act):
            def step(k, i, r):
                at_least(act, scattered[r], 16 * SU * i, tick)
                act.activation(slot[:, r, :], c.slot_of[:, bass.ds(k * SU, SU)], ACT.Copy).then_inc(packed, 1)
                act.activation(rec[:, r, :, 0], c.dst_f[:, bass.ds(k * SU, SU)], ACT.Copy).then_inc(packed, 1)
                act.activation(rec[:, r, :, 1], c.src_f[:, bass.ds(k * SU, SU)], ACT.Copy).then_inc(packed, 1)
            rounds(act, S_BATCHES, R, step)

        @block.sync
        def _(sp):
            def step(k, i, r):
                at_least(sp, made, 4 * (k - R + 1), tick)
                sp.dma_start(ring[:, r, :, :].rearrange("p u f -> p (u f)"), c.values[bass.ds(k, 1), :, :, :].rearrange("one p u f -> p (one u f)"))\
                    .then_inc(arrived[r], 16)
            rounds(sp, BATCHES, R, step)

        @block.tensor
        def _(pe):
            def step(k, i, r):
                q = r % 2
                at_least(pe, made, 4 * (k + 1), tick)
                at_least(pe, added, U * (k - 1), tick)
                if is_first(k):
                    pe.wait_ge(start, 2)
                for u in range(U):
                    ins = pe.matmul(pa[:, q, u, 0:C_END], hot[:, q, u, :], msg[:, q, u, :], start=True, stop=True)
                ins.then_inc(summed, 1)
            rounds(pe, BATCHES, R, step)

        @block.vector
        def _(dve):
            dve.memset(acc, 0.0).then_inc(start, 1)
            dve.memset(msg[:, :, :, C_CNT:C_END], 1.0).then_inc(start, 1)
            dve.wait_ge(start, 2)

            def make(k, i, r):
                q = r % 2
                at = bass.ds(k * U, U)
                ex = c.alpha[:, at, :]
                at_least(dve, summed, k - 1, tick)
                at_least(dve, arrived[r], 16 * (i + 1), tick)
                dve.tensor_tensor(hot[:, q, :, :], over(c.j[:, 0:P], U), wide(c.local_d[:, at], P), ALU.is_equal).then_inc(made, 1)
                dve.tensor_copy(msg[:, q, :, C_EX:C_EW], ex).then_inc(made, 1)
                dve.tensor_tensor(msg[:, q, :, C_EW:C_CNT], ex, wide(c.weight[:, at], H), ALU.mult).then_inc(made, 1)
                dve.tensor_tensor(msg[:, q, :, 0:F].rearrange("p u (h d) -> p u h d", d=D),
                                  ex.unsqueeze(3).broadcast_to([P, U, H, D]),
                                  ring[:, r, :, :].rearrange("p u (h d) -> p u h d", d=D), ALU.mult).then_inc(made, 1)

            def add(k, r):
                at_least(dve, summed, k + 1, tick)
                add_to_buckets(nc, dve, acc, c.bucket_d, pa[:, r % 2, :, :], C_END, k, added, tick)

            def step(k, i, r):
                make(k, i, r)
                if not is_first(k):
                    add(k - 1, (r - 1) % R)
            rounds(dve, BATCHES, R, step)
            add(BATCHES - 1, R - 1)
            dve.wait_ge(added, BATCHES * U)


def stage_edges(nc, c, name, table, acc, buckets, gather, local, layer=None):
    with ExitStack() as ctx:
        sem = lambda n: c.semaphore(name + n)
        sb = lambda n, s, d=F32: ctx.enter_context(nc.sbuf_tensor(name + n, s, d))
        pb = lambda n, s: ctx.enter_context(nc.psum_tensor(name + n, s, F32))
        index, ring = sb("index", [P, R, U], I32), sb("ring", [P, R, U, F])
        hot = sb("hot", [P, R, U, P])
        width_a = F + 1 if layer is None else F
        pa = pb("pa", [P, 2, U, 256 if layer is None else F])
        arrived, attributes = [sem(f"arrived{r}") for r in range(R)], [sem(f"attributes{r}") for r in range(R)]
        index_ready, hots, summed, added, start, tick = (sem(n) for n in ("index", "hots", "summed", "added", "start", "tick"))
        turned, copied, first, second, third, sent, ready = (sem(n) for n in ("turned", "copied", "first", "second", "third", "sent", "ready"))
        if layer:
            width = A1 if layer == 1 else A2
            attr = sb("attr", [width, R, U * P])
            msg = sb("msg", [P, 2, U, P])
            tmp = sb("tmp", [P, 2, U, P])
            ph = pb("ph", [P, 2, U, F])
            pt = pb("pt", [P, 2, U, P])
        if layer == 1:
            hot_t = sb("hot_t", [P, 2, U, P], BF16)
        if layer == 2:
            soft = sb("soft", [P, 2, U, P])
            pos = sb("pos", [P, 2, U, P])
        attr_dram = {1: c.attr1, 2: c.attr2}.get(layer)
        freed = summed if layer is None else (first if layer == 1 else sent)
        block = ctx.enter_context(nc.Block())

        @block.gpsimd
        def _(pool):
            gather_rows(pool, c, table, index, ring, index_ready, arrived, [(freed, 1)], tick)

        if layer:
            @block.sync
            def _(sp):
                def step(k, i, r):
                    e0 = loaded_values(nc, c.edge0, k, SP_ENGINE, E - 1)
                    at_least(sp, ready, k - R + 1, tick)
                    for u in range(U):
                        sp.dma_start(attr[:, r, u * P:(u + 1) * P], attr_dram[:, bass.ds(e0[u], P)]).then_inc(attributes[r], 16)
                rounds(sp, BATCHES, R, step)

        @block.scalar
        def _(act):
            def work(k, i, r):
                q = r % 2
                if layer == 1:
                    at_least(act, turned, k + 1, tick)
                    at_least(act, ready, k - 1, tick)
                    act.activation(hot_t[:, q, :, :], pt[:, q, :, :], ACT.Copy).then_inc(copied, 1)
                if layer == 2:
                    x = pt[:, q, :, :]
                    at_least(act, ready, k + 1, tick)
                    at_least(act, second, k - 1, tick)
                    act.activation(pos[:, q, :, :], x, ACT.Relu, bias=c.w["mlp_b0"][:, 0:1]).then_inc(copied, 1)
                    act.activation(tmp[:, q, :, :], x, ACT.Abs, bias=c.w["mlp_b0"][:, 0:1]).then_inc(copied, 1)
                    at_least(act, copied, 4 * k + 2, tick)
                    act.activation(tmp[:, q, :, :], tmp[:, q, :, :], ACT.Exp, scale=-1.0).then_inc(copied, 1)
                    at_least(act, copied, 4 * k + 3, tick)
                    act.activation(tmp[:, q, :, :], tmp[:, q, :, :], ACT.Ln, bias=c.ones[:, 0:1]).then_inc(copied, 1)

            def relu(k, i, r):
                q = r % 2
                at_least(act, first, k + 1, tick)
                at_least(act, summed, k - 1, tick)
                act.activation(msg[:, q, :, :], tmp[:, q, :, :], ACT.Relu).then_inc(sent, 1)

            def step(k, i, r):
                take_index(act, gather, index, k, i, r, arrived, index_ready, tick)
                if layer and not is_first(k):
                    work(k - 1, i if r else i - 1, (r - 1) % R)
                if layer == 1 and not (isinstance(k, int) and k < 2):
                    relu(k - 2, i if r > 1 else i - 1, (r - 2) % R)
            rounds(act, BATCHES, R, step)
            last = BATCHES - 1
            if layer:
                work(last, BATCHES // R - 1, R - 1)
            if layer == 1:
                relu(last - 1, BATCHES // R - 1, R - 2)
                relu(last, BATCHES // R - 1, R - 1)

        @block.tensor
        def _(pe):
            def turn(k, i, r):
                q = r % 2
                if layer == 1:
                    at_least(pe, hots, k + 1, tick)
                    at_least(pe, copied, k - 1, tick)
                    for u in range(U):
                        ins = pe.transpose(pt[:, q, u, :], hot[:, r, u, :], c.ident[:, :])
                    ins.then_inc(turned, 1)
                if layer == 2:
                    at_least(pe, attributes[r], 16 * U * (i + 1), tick)
                    at_least(pe, copied, 4 * (k - 1), tick)
                    pe.matmul(pt[:, q, :, :].rearrange("p u f -> p (u f)"), c.w["mlp_w0"][:, :], attr[:, r, :], start=True, stop=True).then_inc(ready, 1)

            def hidden(k, i, r):
                q = r % 2
                if layer == 1:
                    which = loaded_values(nc, buckets, k, PE_ENGINE, NT - 1)
                    at_least(pe, copied, k + 1, tick)
                    at_least(pe, attributes[r], 16 * U * (i + 1), tick)
                    at_least(pe, first, k - 1, tick)
                    for u in range(U):
                        for n, part in enumerate(c.dst_parts):
                            pe.matmul(ph[:, q, u, :], hot_t[:, q, u, :], part[:, bass.ds(which[u], 1), :].rearrange("p one f -> p (one f)"),
                                      start=(n == 0), stop=False)
                        ins = pe.matmul(ph[:, q, u, :], attr[:, r, u * P:(u + 1) * P], c.w["w1e"][:, :], start=False, stop=True)
                    ins.then_inc(ready, 1)
                if layer == 2:
                    at_least(pe, second, k + 1, tick)
                    at_least(pe, sent, k - 1, tick)
                    for u in range(U):
                        pe.matmul(ph[:, q, u, :], soft[:, q, u, :], c.w["mlp_w2"][:, :], start=True, stop=False)
                        ins = pe.matmul(ph[:, q, u, :], c.ones[0:1, :], c.w["mlp_b2"][:, :], start=False, stop=True)
                    ins.then_inc(third, 1)

            def total(k, i, r):
                q = r % 2
                if layer is None:
                    at_least(pe, hots, k + 1, tick)
                    at_least(pe, arrived[r], 16 * U * (i + 1), tick)
                else:
                    at_least(pe, sent, k + 1, tick)
                    at_least(pe, hots, (U if layer == 2 else 1) * (k + 1), tick)
                at_least(pe, added, U * (k - 1), tick)
                for u in range(U):
                    rhs = ring[:, r, u, :] if layer is None else msg[:, q, u, :]
                    ins = pe.matmul(pa[:, q, u, 0:F], hot[:, r, u, :], rhs, start=True, stop=True)
                    if layer is None:
                        ins = pe.matmul(pa[:, q, u, F:F + 1], hot[:, r, u, :], c.ones[:, 0:1], start=True, stop=True)
                ins.then_inc(summed, 1)

            lag = {None: 0, 1: 2, 2: 2}[layer]

            def step(k, i, r):
                back = lambda n: (k - n, i if r >= n else i - 1, (r - n) % R)
                known = k if isinstance(k, int) else R
                turn(k, i, r)
                if layer and known >= 1:
                    hidden(*back(1))
                if known >= lag:
                    total(*back(lag))
            rounds(pe, BATCHES, R, step)
            last = BATCHES // R - 1
            if layer:
                hidden(BATCHES - 1, last, R - 1)
                total(BATCHES - 2, last, R - 2)
                total(BATCHES - 1, last, R - 1)

        @block.vector
        def _(dve):
            dve.memset(acc, 0.0).then_inc(start, 1)
            dve.wait_ge(start, 1)

            def one_hot(k, i, r):
                at = bass.ds(k * U, U)
                at_least(dve, summed, k - R + 1, tick)
                if layer == 2:
                    for u in range(U):
                        dve.tensor_scalar(hot[:, r, u, :], c.j[:, 0:P], local[:, bass.ds(k * U + u, 1)], c.cutoff[:, bass.ds(k * U + u, 1)],
                                          ALU.is_equal, ALU.mult).then_inc(hots, 1)
                    return
                if layer == 1:
                    at_least(dve, turned, k - R + 1, tick)
                dve.tensor_tensor(hot[:, r, :, :], over(c.j[:, 0:P], U), wide(local[:, at], P), ALU.is_equal).then_inc(hots, 1)

            def message(k, i, r):
                q = r % 2
                if layer == 1:
                    at_least(dve, ready, k + 1, tick)
                    at_least(dve, arrived[r], 16 * U * (i + 1), tick)
                    at_least(dve, sent, k - 1, tick)
                    dve.tensor_tensor(tmp[:, q, :, :], ph[:, q, :, :], ring[:, r, :, :], ALU.add).then_inc(first, 1)
                if layer == 2:
                    at_least(dve, third, k + 1, tick)
                    at_least(dve, arrived[r], 16 * U * (i + 1), tick)
                    dve.tensor_tensor(msg[:, q, :, :], ph[:, q, :, :], ring[:, r, :, :], ALU.mult).then_inc(sent, 1)

            def soften(k, i, r):
                q = r % 2
                at_least(dve, copied, 4 * (k + 1), tick)
                at_least(dve, third, k - 1, tick)
                dve.scalar_tensor_tensor(out=soft[:, q, :, :].rearrange("p u f -> p (u f)"), in0=pos[:, q, :, :].rearrange("p u f -> p (u f)"),
                                         scalar=-LOG2, in1=tmp[:, q, :, :].rearrange("p u f -> p (u f)"), op0=ALU.add, op1=ALU.add).then_inc(second, 1)

            def add(k, i, r):
                at_least(dve, summed, k + 1, tick)
                add_to_buckets(nc, dve, acc, buckets, pa[:, r % 2, :, :], width_a, k, added, tick)

            def step(k, i, r):
                back = lambda n: (k - n, i if r >= n else i - 1, (r - n) % R)
                known = k if isinstance(k, int) else R
                if layer is None:
                    one_hot(k, i, r)
                    if known >= 1:
                        add(*back(1))
                if layer == 1:
                    one_hot(k, i, r)
                    if known >= 1:
                        message(*back(1))
                    if known >= 2:
                        add(*back(2))
                if layer == 2:
                    if known >= 1:
                        soften(*back(1))
                    if known >= 2:
                        message(*back(2))
                        add_after(*back(2))
                    one_hot(k, i, r)

            def add_after(k, i, r):
                if not (isinstance(k, int) and k < 1):
                    add(k - 1, None, (r - 1) % R)

            rounds(dve, BATCHES, R, step)
            last = BATCHES // R - 1
            if layer is None:
                add(BATCHES - 1, last, R - 1)
            if layer == 1:
                message(BATCHES - 1, last, R - 1)
                add(BATCHES - 2, last, R - 2)
                add(BATCHES - 1, last, R - 1)
            if layer == 2:
                soften(BATCHES - 1, last, R - 1)
                message(BATCHES - 2, last, R - 2)
                add(BATCHES - 3, last, R - 3)
                message(BATCHES - 1, last, R - 1)
                add(BATCHES - 2, last, R - 2)
                add(BATCHES - 1, last, R - 1)
            dve.wait_ge(added, BATCHES * U)


def load_weights(nc, c, ctx, t, name, natural=(), rows=(), wide_rows=()):
    loaded = c.semaphore(name + "_weights")
    loads = []
    for group, how in ((natural, 0), (rows, 0), (wide_rows, 1)):
        for attr, src in group:
            src = t[src] if isinstance(src, str) else src
            tile = ctx.enter_context(nc.sbuf_tensor(name + "_" + attr, [P, src.shape[1]] if how else list(src.shape), F32))
            c.w[attr] = tile
            loads.append((tile[:, :], src.broadcast_to([P, src.shape[1]]) if how else src))
    with ExitStack() as inner:
        block = inner.enter_context(nc.Block())

        @block.sync
        def _(sp):
            for to, src in loads:
                sp.dma_start(to, src).then_inc(loaded, 16)
            sp.wait_ge(loaded, 16 * len(loads))


def tile_rows(table, k, a=0, b=None):
    return table[bass.ds(k, 1), :, a:b if b else table.shape[2]].rearrange("one p f -> p (one f)")


def at_tile(whole, k, a=0, b=None):
    return whole[:, bass.ds(k, 1), a:b if b else whole.shape[2]].rearrange("p one f -> p (one f)")


def attention_layer(nc, c, t, small):
    with ExitStack() as ctx:
        load_weights(nc, c, ctx, t, "l0", natural=[(n, "L0_" + n) for n in ("wq", "wk", "wv", "wskip", "wo")],
                     rows=[("bias4", "L0_bias4"), ("bo", "L0_bo")],
                     wide_rows=[(n, "L0_" + n) for n in ("we", "gamma", "beta")])
        q_full = arena(c, 3 * NT * QW // 2, [NT, QW])
        by_we = arena(c, 3 * NT * QW // 2 + NT * QW, [NT, F])
        c.alpha = arena(c, B2_0, [TILES, H])
        c.query_parts = [arena(c, n * NT * QW // 2, [NT, QW], BF16) for n in range(3)]

        def keep(k):
            return [(tile_rows(c.kv3, k), 0, 2 * F), (tile_rows(c.skip, k), 2 * F, 3 * F)]

        sweep(nc, c, "qkv", [(lambda k: at_tile(c.x, k), P)],
              [(None, c.w["bias4"][:, :], 0, 4 * F)] + [(0, w[:, :], n * F, (n + 1) * F) for n, w in enumerate((c.w["wq"], c.w["wk"], c.w["wv"], c.w["wskip"]))],
              vector=lambda e, k, po: e.tensor_scalar(at_tile(q_full, k, 0, F), po[:, 0:F], 1.0 / D ** 0.5, None, ALU.mult),
              scalar=lambda e, k, po, ring: e.activation(ring[:, :], po[:, F:4 * F], ACT.Copy), store=keep)
        vector_scalar_stage(nc, c, "query", [
            ("v", lambda e: e.tensor_tensor(by_we, q_full[:, :, 0:F], over(c.w["we"][:, :], NT), ALU.mult)),
            ("v", lambda e: e.tensor_reduce(q_full[:, :, F:QW], by_we.rearrange("p t (h d) -> p t h d", d=D), AX_X, ALU.add)),
        ] + split_steps(q_full, c.query_parts))
        stage_attention_scores(nc, c)
        stage_attention_max(nc, c)
        stage_attention_sums(nc, c)
        load_whole(nc, c, arena(c, B2_0, [NT, F]), c.skip, "skip")

        acc, heads, y = arena(c, ACC0, [NT, C_END]), arena(c, B1_0, [NT, F]), arena(c, B2_0, [NT, F])
        by_head = heads.rearrange("p t (h d) -> p t h d", d=D)
        den = acc[:, :, C_EX:C_EW]
        spread = lambda a: a.unsqueeze(3).broadcast_to([P, NT, H, D])
        vector_scalar_stage(nc, c, "heads", [
            ("v", lambda e: e.tensor_copy(c.count[:, :], acc[:, :, C_CNT])),
            ("v", lambda e: e.tensor_scalar(den, den, 1e-16, None, ALU.max)),
            ("v", lambda e: e.reciprocal(den, den)),
            ("v", lambda e: e.tensor_copy(by_head, spread(acc[:, :, C_EW:C_CNT]))),
            ("v", lambda e: e.tensor_tensor(heads, heads, over(c.w["we"][:, :], NT), ALU.mult)),
            ("v", lambda e: e.tensor_tensor(heads, heads, acc[:, :, 0:F], ALU.add)),
            ("v", lambda e: e.tensor_tensor(by_head, by_head, spread(den), ALU.mult)),
            ("v", lambda e: e.tensor_tensor(heads, heads, y, ALU.add)),
        ])
        sweep(nc, c, "wo", [(lambda k: at_tile(heads, k), P)], [(None, c.w["bo"][:, :], 0, F), (0, c.w["wo"][:, :], 0, F)],
              vector=lambda e, k, po: e.tensor_tensor(at_tile(y, k), po[:, 0:F], at_tile(c.x, k), ALU.add))
        vector_scalar_stage(nc, c, "norm0", norm_steps(c, y, heads, small, c.w["gamma"][:, :], c.w["beta"][:, :], c.x[:, :, :])
                            + norm_steps(c, y, heads, small, out=c.x[:, :, :]))


def load_whole(nc, c, to, table, name):
    with ExitStack() as ctx:
        loaded = c.semaphore(name + "_loaded")
        block = ctx.enter_context(nc.Block())

        @block.sync
        def _(sp):
            sp.dma_start(to, table.rearrange("t p f -> p t f")).then_inc(loaded, 16)
            sp.wait_ge(loaded, 16)


def edge_mlp_layer(nc, c, t, small):
    with ExitStack() as ctx:
        load_weights(nc, c, ctx, t, "l1", natural=[(n, "L1_" + n) for n in ("w1s", "w1d", "w1e", "w2", "b2_col", "wu")],
                     rows=[("b1", "L1_b1"), ("bu", "L1_bu")], wide_rows=[("gamma", "L1_gamma"), ("beta", "L1_beta")])
        acc, full, mid, y = arena(c, ACC0, [NT, F]), arena(c, ACC0, [NT, F]), arena(c, B1_0, [NT, F]), arena(c, B2_0, [NT, F])
        c.dst_parts = [arena(c, B1_0 + n * NT * F // 2, [NT, F], BF16) for n in range(3)]
        w_both = ctx.enter_context(nc.sbuf_tensor("l1_both", [P, F], F32))
        b_both = ctx.enter_context(nc.sbuf_tensor("l1_b_both", [P, F], F32))
        b_row = ctx.enter_context(nc.sbuf_tensor("l1_b_row", [1, F], F32))
        sweep(nc, c, "l1in", [(lambda k: at_tile(c.x, k), P)],
              [(0, c.w["w1s"][:, :], 0, F), (0, c.w["w1d"][:, :], F, 2 * F), (None, c.w["b1"][:, :], F, 2 * F)],
              vector=lambda e, k, po: e.tensor_copy(at_tile(full, k), po[:, F:2 * F]),
              scalar=lambda e, k, po, ring: e.activation(ring[:, 0:F], po[:, 0:F], ACT.Copy),
              store=lambda k: [(tile_rows(c.table3, k), 0, F)])
        vector_scalar_stage(nc, c, "split1", split_steps(full, c.dst_parts))
        with ExitStack() as inner:
            made = c.semaphore("l1_made")
            took = c.semaphore("l1_took")
            pw = inner.enter_context(nc.psum_tensor("l1_pw", [P, 512], F32))
            block = inner.enter_context(nc.Block())

            @block.tensor
            def _(pe):
                pe.matmul(pw[:, 0:F], c.w["w2"][:, :], c.w["wu"][:, :], start=True, stop=True).then_inc(made, 1)
                pe.matmul(pw[:, F:2 * F], c.w["b2_col"][:, 0:1].broadcast_to([P, P]), c.w["wu"][:, :], start=True, stop=True).then_inc(made, 1)

            @block.vector
            def _(dve):
                dve.wait_ge(made, 2)
                dve.tensor_copy(w_both[:, :], pw[:, 0:F]).then_inc(took, 1)
                dve.tensor_copy(b_both[:, :], pw[:, F:2 * F]).then_inc(took, 1)
        stage_edges(nc, c, "e1_", c.table, acc, c.bucket_d, c.gather_d, c.local_d, layer=1)
        sweep(nc, c, "l1out", [(lambda k: at_tile(acc, k), P)], [(None, c.w["bu"][:, :], 0, F), (0, w_both[:, :], 0, F)],
              vector=lambda e, k, po: e.scalar_tensor_tensor(out=at_tile(mid, k), in0=b_both[:, :], scalar=c.count[:, bass.ds(k, 1)],
                                                             in1=po[:, 0:F], op0=ALU.mult, op1=ALU.add))
        vector_scalar_stage(nc, c, "norm1", [
            ("s", lambda e: e.activation(y, mid, ACT.Relu)),
            ("v", lambda e: e.tensor_tensor(y, y, c.x[:, :, :], ALU.add)),
        ] + norm_steps(c, y, mid, small, c.w["gamma"][:, :], c.w["beta"][:, :], c.x[:, :, :]) + norm_steps(c, y, mid, small, out=c.x[:, :, :]))


def filter_layer(nc, c, t, small):
    with ExitStack() as ctx:
        load_weights(nc, c, ctx, t, "l2", natural=[(n, "L2_" + n) for n in ("mlp_w0", "mlp_b0", "mlp_w2", "lin1", "lin2", "lin")],
                     rows=[("mlp_b2", "L2_mlp_b2"), ("lin2_b", "L2_lin2_b"), ("lin_b", "L2_lin_b")])
        acc, h1, z = arena(c, ACC0, [NT, F]), arena(c, B1_0, [NT, F]), arena(c, B2_0, [NT, F])
        sweep(nc, c, "l2in", [(lambda k: at_tile(c.x, k), P)], [(0, c.w["lin1"][:, :], 0, F)],
              vector=lambda e, k, po: e.tensor_copy(at_tile(h1, k), po[:, 0:F]),
              scalar=lambda e, k, po, ring: e.activation(ring[:, 0:F], po[:, 0:F], ACT.Copy),
              store=lambda k: [(tile_rows(c.table3, k), 0, F)])
        stage_edges(nc, c, "e2_", c.table, acc, c.bucket_d, c.gather_d, c.local_d, layer=2)
        vector_scalar_stage(nc, c, "l2sum", [("v", lambda e: e.tensor_tensor(h1, h1, acc, ALU.add))])
        sweep(nc, c, "l2mid", [(lambda k: at_tile(h1, k), P)], [(None, c.w["lin2_b"][:, :], 0, F), (0, c.w["lin2"][:, :], 0, F)],
              vector=lambda e, k, po: e.tensor_copy(at_tile(z, k), po[:, 0:F]))
        vector_scalar_stage(nc, c, "l2soft", [
            ("s", lambda e: e.activation(h1, z, ACT.Abs)),
            ("s", lambda e: e.activation(h1, h1, ACT.Exp, scale=-1.0)),
            ("s", lambda e: e.activation(h1, h1, ACT.Ln, bias=c.ones[:, 0:1])),
            ("s", lambda e: e.activation(z, z, ACT.Relu)),
            ("v", lambda e: e.scalar_tensor_tensor(out=h1, in0=z, scalar=-LOG2, in1=h1, op0=ALU.add, op1=ALU.add)),
        ])
        sweep(nc, c, "l2out", [(lambda k: at_tile(h1, k), P)], [(None, c.w["lin_b"][:, :], 0, F), (0, c.w["lin"][:, :], 0, F)],
              vector=lambda e, k, po: e.tensor_tensor(at_tile(z, k), po[:, 0:F], at_tile(c.x, k), ALU.add))
        vector_scalar_stage(nc, c, "norm2", norm_steps(c, z, h1, small, out=c.x[:, :, :]))


def stage_records(nc, c, gather_s, local_s):
    with ExitStack() as ctx:
        sem = lambda n: c.semaphore("re_" + n)
        loaded, stored, turned, took = sem("loaded"), sem("stored"), sem("turned"), sem("took")
        rec = arena(c, ACC0, [JC, 2 * P])
        ps = ctx.enter_context(nc.psum_tensor("re_ps", [P, 2, 2, 512], F32))
        full = TILES // P
        rest = TILES - full * P
        slots = c.records.rearrange("(j p) two -> j (p two)", p=P)
        block = ctx.enter_context(nc.Block())

        @block.sync
        def _(sp):
            sp.dma_start(c.table3.rearrange("t p f -> p t f"), c.x[:, :, :]).then_inc(stored, 16)
            sp.dma_start(rec[:, 0:full, :], slots[0:full * P, :].rearrange("(k j) f -> j k f", j=P)).then_inc(loaded, 16)
            sp.dma_start(rec[0:rest, full, :], slots[full * P:TILES, :]).then_inc(loaded, 16)
            sp.wait_ge(stored, 16)

        @block.tensor
        def _(pe):
            pe.wait_ge(loaded, 32)
            for f in range(2):
                for k in range(JC):
                    q = min(P, TILES - k * P)
                    ins = pe.transpose(ps[:, f, k // 4, k % 4 * P:k % 4 * P + q], rec[0:q, k, f::2], c.ident[0:q, 0:q])
            ins.then_inc(turned, 1)

        @block.vector
        def _(dve):
            dve.wait_ge(turned, 1)
            for h, (a, b) in enumerate(((0, 512), (512, TILES))):
                dve.tensor_scalar(gather_s[:, a:b], ps[:, 0, h, 0:b - a], float(N - 1), None, ALU.min).then_inc(took, 1)
                dve.tensor_tensor(local_s[:, a:b], ps[:, 1, h, 0:b - a], c.window_s[:, a:b], ALU.subtract).then_inc(took, 1)


def gated_layer(nc, c, t, small, out):
    with ExitStack() as ctx:
        load_weights(nc, c, ctx, t, "l3", natural=[(n, "L3_" + n) for n in ("w_in", "w_out", "wih1", "wih2", "whh", "b_in_col", "b_out_col")],
                     rows=[("b_ih", "L3_b_ih"), ("b_hh", "L3_b_hh")])
        with ExitStack() as edges:
            gather_s = edges.enter_context(nc.sbuf_tensor("gather_s", [P, TILES], F32))
            local_s = edges.enter_context(nc.sbuf_tensor("local_s", [P, TILES], F32))
            fwd, rev = arena(c, ACC0, [NT, F + 1]), arena(c, B1_0, [NT, F + 1])
            stage_records(nc, c, gather_s, local_s)
            stage_edges(nc, c, "e3_", c.table, fwd, c.bucket_d, c.gather_d, c.local_d)
            stage_edges(nc, c, "e4_", c.table, rev, c.bucket_s, gather_s, local_s)
        p_in = ctx.enter_context(nc.sbuf_tensor("l3_p_in", [P, 3 * F], F32))
        p_out = ctx.enter_context(nc.sbuf_tensor("l3_p_out", [P, 3 * F], F32))
        bias = [ctx.enter_context(nc.sbuf_tensor(f"l3_bias{n}", [1, 4 * F], F32)) for n in range(3)]
        seen = ctx.enter_context(nc.sbuf_tensor("l3_seen", [P, NT, 2], F32))
        with ExitStack() as inner:
            made = c.semaphore("l3_made")
            took = c.semaphore("l3_took")
            pw = inner.enter_context(nc.psum_tensor("l3_pw", [P, 4, 512], F32))
            block = inner.enter_context(nc.Block())

            @block.tensor
            def _(pe):
                pe.matmul(pw[:, 0, 0:3 * F], c.w["w_in"][:, :], c.w["wih1"][:, :], start=True, stop=True).then_inc(made, 1)
                pe.matmul(pw[:, 1, 0:3 * F], c.w["w_out"][:, :], c.w["wih2"][:, :], start=True, stop=True).then_inc(made, 1)
                pe.matmul(pw[0:1, 2, 0:3 * F], c.w["b_in_col"][:, :], c.w["wih1"][:, :], start=True, stop=True).then_inc(made, 1)
                pe.matmul(pw[0:1, 3, 0:3 * F], c.w["b_out_col"][:, :], c.w["wih2"][:, :], start=True, stop=True).then_inc(made, 1)

            @block.vector
            def _(dve):
                n = [0]

                def done(ins):
                    n[0] += 1
                    ins.then_inc(took, 1)
                    dve.wait_ge(took, n[0])
                dve.wait_ge(made, 4)
                done(dve.tensor_copy(p_in[:, :], pw[:, 0, 0:3 * F]))
                done(dve.tensor_copy(p_out[:, :], pw[:, 1, 0:3 * F]))
                for b, bank in ((0, 2), (1, 3)):
                    done(dve.memset(bias[b][:, :], 0.0))
                    done(dve.tensor_copy(bias[b][:, 0:3 * F], pw[0:1, bank, 0:3 * F]))
                done(dve.tensor_tensor(bias[2][:, 0:2 * F], c.w["b_ih"][:, 0:2 * F], c.w["b_hh"][:, 0:2 * F], ALU.add))
                done(dve.tensor_copy(bias[2][:, 2 * F:3 * F], c.w["b_ih"][:, 2 * F:3 * F]))
                done(dve.tensor_copy(bias[2][:, 3 * F:4 * F], c.w["b_hh"][:, 2 * F:3 * F]))
                for n_, acc in enumerate((fwd, rev)):
                    count = acc[:, :, F]
                    done(dve.tensor_scalar(seen[:, :, n_], count, 1.0, None, ALU.min))
                    done(dve.tensor_scalar(count, count, 1.0, None, ALU.max))
                    done(dve.reciprocal(count, count))
                    done(dve.tensor_tensor(acc[:, :, 0:F], acc[:, :, 0:F], wide(count, F), ALU.mult))
        y = arena(c, B2_0, [NT, F])
        stage_gates(nc, c, fwd, rev, seen, p_in, p_out, bias, y)
        squares = arena(c, B1_0, [NT, F])
        vector_scalar_stage(nc, c, "norm3", norm_steps(c, y, squares, small))
        with ExitStack() as last:
            stored = c.semaphore("stored")
            block = last.enter_context(nc.Block())
            whole = N // P * P

            @block.sync
            def _(sp):
                sp.dma_start(out[0:whole, :].rearrange("(t p) f -> p t f", p=P), y[:, 0:N // P, :]).then_inc(stored, 16)
                sp.dma_start(out[whole:N, :], y[0:N - whole, N // P, :]).then_inc(stored, 16)
                sp.wait_ge(stored, 32)


def stage_gates(nc, c, fwd, rev, seen, p_in, p_out, bias, y):
    with ExitStack() as ctx:
        sem = lambda n: c.semaphore("ga_" + n)
        turned, copied, multiplied, squashed, vec, tick = (sem(n) for n in ("turned", "copied", "multiplied", "squashed", "vec", "tick"))
        xt = ctx.enter_context(nc.sbuf_tensor("ga_xt", [P, 2, 3, P], F32))
        st = ctx.enter_context(nc.sbuf_tensor("ga_st", [1, 2, 2, P], F32))
        gates = ctx.enter_context(nc.sbuf_tensor("ga_gates", [P, 2, 2 * F], F32))
        new = ctx.enter_context(nc.sbuf_tensor("ga_new", [P, 2, F], F32))
        pt = ctx.enter_context(nc.psum_tensor("ga_pt", [P, 2, 512], F32))
        ps = ctx.enter_context(nc.psum_tensor("ga_ps", [P, 2, 512], F32))
        po = ctx.enter_context(nc.psum_tensor("ga_po", [P, 2, 512], F32))
        VEC = 5
        staged = sem("staged")
        fixed = ctx.enter_context(nc.sbuf_tensor("ga_fixed", [P, 2, 3, P], F32))
        flags = ctx.enter_context(nc.sbuf_tensor("ga_flags", [P, 2, 2], F32))
        block = ctx.enter_context(nc.Block())

        @block.gpsimd
        def _(pool):
            def step(k, i, q):
                at_least(pool, turned, k - 1, tick)
                for n, src in enumerate((at_tile(fwd, k, 0, F), at_tile(rev, k, 0, F), at_tile(c.x, k))):
                    pool.tensor_copy(fixed[:, q, n, :], src).then_inc(staged, 1)
                pool.tensor_copy(flags[:, q, :], at_tile(seen, k)).then_inc(staged, 1)
            rounds(pool, NT, 2, step)

        @block.tensor
        def _(pe):
            def turn(k, q):
                at_least(pe, staged, 4 * (k + 1), tick)
                at_least(pe, copied, 3 * (k - 1), tick)
                for n in range(3):
                    pe.transpose(pt[:, q, n * P:(n + 1) * P], fixed[:, q, n, :], c.ident[:, :])
                for n in range(2):
                    ins = pe.transpose(ps[0:1, q, n * P:(n + 1) * P], flags[:, q, n:n + 1], c.ident[:, :])
                ins.then_inc(turned, 1)

            def multiply(k, q):
                at_least(pe, copied, 3 * (k + 1), tick)
                at_least(pe, vec, VEC * (k - 1), tick)
                b = po[:, q, :]
                pe.matmul(b, c.ones[0:1, :], bias[2][:, :], start=True, stop=False)
                pe.matmul(b, st[:, q, 0, :], bias[0][:, :], start=False, stop=False)
                pe.matmul(b, st[:, q, 1, :], bias[1][:, :], start=False, stop=False)
                pe.matmul(b[:, 0:3 * F], xt[:, q, 0, :], p_in[:, :], start=False, stop=False)
                pe.matmul(b[:, 0:3 * F], xt[:, q, 1, :], p_out[:, :], start=False, stop=False)
                pe.matmul(b[:, 0:2 * F], xt[:, q, 2, :], c.w["whh"][:, 0:2 * F], start=False, stop=False)
                pe.matmul(b[:, 3 * F:4 * F], xt[:, q, 2, :], c.w["whh"][:, 2 * F:3 * F], start=False, stop=True).then_inc(multiplied, 1)

            def step(k, i, q):
                turn(k, q)
                if not is_first(k):
                    multiply(k - 1, 1 - q)
            rounds(pe, NT, 2, step)
            multiply(NT - 1, 1)

        @block.scalar
        def _(act):
            def copy(k, q):
                at_least(act, turned, k + 1, tick)
                at_least(act, multiplied, k - 1, tick)
                act.activation(xt[:, q, :, :], pt[:, q, 0:3 * P].rearrange("p (n m) -> p n m", m=P), ACT.Copy).then_inc(copied, 1)
                for n in range(2):
                    act.activation(st[:, q, n, :], ps[0:1, q, n * P:(n + 1) * P], ACT.Copy).then_inc(copied, 1)

            def squash(k, q):
                at_least(act, multiplied, k + 1, tick)
                at_least(act, vec, VEC * (k - 1), tick)
                act.activation(gates[:, q, :], po[:, q, 0:2 * F], ACT.Sigmoid).then_inc(squashed, 1)
                at_least(act, vec, VEC * k + 2, tick)
                act.activation(new[:, q, :], new[:, q, :], ACT.Tanh).then_inc(squashed, 1)

            def step(k, i, q):
                copy(k, q)
                if not is_first(k):
                    squash(k - 1, 1 - q)
            rounds(act, NT, 2, step)
            squash(NT - 1, 1)

        @block.vector
        def _(dve):
            def step(k, i, q):
                n, x, to = new[:, q, :], at_tile(c.x, k), at_tile(y, k)
                r, z = gates[:, q, 0:F], gates[:, q, F:2 * F]
                at_least(dve, squashed, 2 * k + 1, tick)
                dve.tensor_tensor(n, r, po[:, q, 3 * F:4 * F], ALU.mult).then_inc(vec, 1)
                at_least(dve, vec, VEC * k + 1, tick)
                dve.tensor_tensor(n, n, po[:, q, 2 * F:3 * F], ALU.add).then_inc(vec, 1)
                at_least(dve, squashed, 2 * k + 2, tick)
                dve.tensor_tensor(to, x, n, ALU.subtract).then_inc(vec, 1)
                at_least(dve, vec, VEC * k + 3, tick)
                dve.tensor_tensor(to, to, z, ALU.mult).then_inc(vec, 1)
                at_least(dve, vec, VEC * k + 4, tick)
                dve.tensor_tensor(to, to, n, ALU.add).then_inc(vec, 1)
            rounds(dve, NT, 2, step)
            dve.wait_ge(vec, VEC * NT)
            dve.tensor_tensor(y, y, c.x[:, :, :], ALU.add).then_inc(vec, 1)


def gnn_kernel(nc, t, out):
    c = Core(nc)
    scratch = lambda name, shape: nc.dram_tensor(name, shape, F32, kind="Internal").ap()
    c.records = scratch("records", (SLOTS, 2))
    c.kv3 = scratch("keys_values", (NT, P, 2 * F))
    c.kv = c.kv3.rearrange("t p f -> (t p) f")
    c.skip = scratch("skip", (NT, P, F))
    c.values = scratch("edge_values", (BATCHES, P, U, F))
    c.table3 = scratch("table", (NT, P, F))
    c.table = c.table3.rearrange("t p f -> (t p) f")
    c.attr1, c.attr2 = t["edge_attr_32"], t["edge_attr_50"]
    with ExitStack() as ctx:
        sb = lambda ctx, name, shape, dt=F32: ctx.enter_context(nc.sbuf_tensor(name, shape, dt))
        c.arena = sb(ctx, "arena", [P, ARENA])
        c.x = sb(ctx, "nodes", [P, NT, F])
        c.ident, c.ones = sb(ctx, "ident", [P, P]), sb(ctx, "ones", [P, P])
        c.j, c.part, c.bounds = sb(ctx, "j", [P, TILES]), sb(ctx, "part", [P, 1]), sb(ctx, "bounds", [P, NB])
        c.gather_d, c.local_d, c.weight, c.cutoff = (sb(ctx, n, [P, TILES]) for n in ("gather_d", "local_d", "weight", "cutoff"))
        c.window_s = sb(ctx, "window_s", [P, TILES], BF16)
        c.count = sb(ctx, "count", [P, NT])
        small = sb(ctx, "small", [P, 2, NT])
        ints = sb(ctx, "ints", [P, TILES], I32)
        c.bucket_d, c.edge0, c.bucket_s = ints[0:1, :], ints[32:33, :], ints[64:65, :]
        with ExitStack() as early:
            c.key = sb(early, "key", [P, TILES])
            c.src_f, c.dst_f, c.src_bucket, c.slot_of = (sb(early, n, [P, CHUNK]) for n in ("src_f", "dst_f", "src_bucket", "slot_of"))
            c.base = sb(early, "base", [P, NB])
            with ExitStack() as first:
                c.before, c.previous = sb(first, "before", [P, P]), sb(first, "previous", [P, P])
                c.src_i, c.dst_i = arena(c, ACC0 + 2048, [CHUNK], I32), arena(c, ACC0 + 2048 + CHUNK, [CHUNK], I32)
                stage_setup(nc, c, t)
                stage_lists(nc, c, t)
            attention_layer(nc, c, t, small)
        c.clear_semaphores()
        edge_mlp_layer(nc, c, t, small)
        c.clear_semaphores()
        filter_layer(nc, c, t, small)
        c.clear_semaphores()
        gated_layer(nc, c, t, small, out)


def kernel(**inputs):
    import numpy as np
    import concourse.bacc as bacc
    from concourse.bass_utils import run_bass_kernel_spmd as run

    g = {name: np.asarray(a) for name, a in inputs.items()}
    row = lambda name: g[name].reshape(1, -1)
    heads = lambda name: g[name].transpose(1, 0, 2).reshape(F, H * D)
    pad = EP - E
    at = {
        "x": g["x"],
        "src": np.concatenate([g["src"], np.full(pad, NOWHERE, g["src"].dtype)]),
        "dst": np.concatenate([g["dst"], np.full(pad, NOWHERE, g["dst"].dtype)]),
        "edge_weight": np.concatenate([g["edge_weight"], np.zeros(pad, np.float32)]),
        "edge_attr_32": np.pad(g["edge_attr_32"].T, ((0, 0), (0, pad))),
        "edge_attr_50": np.pad(g["edge_attr_50"].T, ((0, 0), (0, pad))),
        "L0_wq": heads("L0_gnn_Wq"), "L0_wk": heads("L0_gnn_Wk"), "L0_wv": heads("L0_gnn_Wv"), "L0_wskip": heads("L0_gnn_Wskip"),
        "L0_bias4": np.concatenate([row("L0_gnn_bq"), row("L0_gnn_bk"), row("L0_gnn_bv"), row("L0_gnn_bskip")], axis=1),
        "L0_we": row("L0_gnn_We"), "L0_wo": g["L0_gnn_Wo"], "L0_bo": row("L0_gnn_bo"),
        "L0_gamma": row("L0_gnn_gamma"), "L0_beta": row("L0_gnn_beta"),
        "L1_w1s": g["L1_gnn_W1"][:, 0:F].T, "L1_w1d": g["L1_gnn_W1"][:, F:2 * F].T, "L1_w1e": g["L1_gnn_W1"][:, 2 * F:].T,
        "L1_w2": g["L1_gnn_W2"], "L1_b2_col": g["L1_gnn_b2"].reshape(F, 1), "L1_wu": g["L1_gnn_Wu"].T,
        "L1_b1": row("L1_gnn_b1"), "L1_bu": row("L1_gnn_bu"), "L1_gamma": row("L1_gnn_gamma"), "L1_beta": row("L1_gnn_beta"),
        "L2_mlp_w0": g["L2_gnn_mlp_w0"].T, "L2_mlp_b0": g["L2_gnn_mlp_b0"].reshape(F, 1), "L2_mlp_w2": g["L2_gnn_mlp_w2"].T,
        "L2_mlp_b2": row("L2_gnn_mlp_b2"), "L2_lin1": g["L2_gnn_lin1_w"].T, "L2_lin2": g["L2_gnn_lin2_w"].T,
        "L2_lin2_b": row("L2_gnn_lin2_b"), "L2_lin": g["L2_gnn_lin_w"].T, "L2_lin_b": row("L2_gnn_lin_b"),
        "L3_w_in": g["L3_gnn_W_in"], "L3_w_out": g["L3_gnn_W_out"], "L3_b_in_col": g["L3_gnn_b_in"].reshape(F, 1),
        "L3_b_out_col": g["L3_gnn_b_out"].reshape(F, 1), "L3_wih1": g["L3_gnn_w_ih"][:, 0:F].T, "L3_wih2": g["L3_gnn_w_ih"][:, F:2 * F].T,
        "L3_whh": g["L3_gnn_w_hh"].T, "L3_b_ih": row("L3_gnn_b_ih"), "L3_b_hh": row("L3_gnn_b_hh"),
    }
    nc = bacc.Bacc("TRN2", target_bir_lowering=False, num_devices=1)
    arrays, t = {}, {}
    for name, a in at.items():
        a = np.ascontiguousarray(a)
        arrays[name] = a
        t[name] = nc.dram_tensor(name, a.shape, mybir.dt.from_np(a.dtype), kind="ExternalInput").ap()
    out = nc.dram_tensor("out", (N, F), F32, kind="ExternalOutput").ap()
    gnn_kernel(nc, t, out)
    return run(nc, [arrays], core_ids=[0]).results[0]["out"]
```

```python
from contextlib import ExitStack

import concourse.bass as bass
from concourse import mybir

F32 = mybir.dt.float32
I32 = mybir.dt.int32
BF16 = mybir.dt.bfloat16
ALU = mybir.AluOpType
ACT = mybir.ActivationFunctionType
AX_X = mybir.AxisListType.X
PE_ENGINE = mybir.EngineType.PE
DVE_ENGINE = mybir.EngineType.DVE
SP_ENGINE = mybir.EngineType.SP

P = 128
N = 6250
E = 106250
F = 128
H = 8
D = F // H
A1, A2 = 32, 50
NB = -(-N // P)
NT = NB + 1
U = 4
R = 4
TILES = -(-(E // P + NB) // (U * R)) * U * R
BATCHES = TILES // U
SLOTS = TILES * P
CHUNK = -(-(E + P) // P)
EP = CHUNK * P
NOWHERE = 1 << 20
SU = 8
JC = -(-TILES // P)
SQ = 8
SP_PARTS = TILES // SQ
SL = SQ * P
FAR = -1.0e30
LN_EPS = 1e-5
LOG2 = 0.6931471805599453
assert R == 4 and CHUNK % SU == 0 and (CHUNK // SU) % R == 0 and TILES % SQ == 0 and NB <= BATCHES // R - 1

C_EX, C_EW, C_CNT, C_END = F, F + H, F + 2 * H, F + 2 * H + 1
QW = F + H

ACC0, ACC_N = 0, NT * C_END + 6
B1_0 = ACC_N
B1_N = 2 * H * SL - ACC_N
B2_0 = B1_0 + B1_N
B2_N = TILES * H
ARENA = B2_0 + B2_N


def at_least(eng, sem, value, tick):
    if isinstance(value, int):
        if value > 0:
            eng.wait_ge(sem, value)
        return
    eng.wait_ge(sem, value)
    eng.sem_inc(tick, 1)


def rounds(eng, count, ring, step, peeled=1):
    for k in range(peeled * ring):
        step(k, k // ring, k % ring)
    with eng.Fori(peeled, count // ring) as i:
        for r in range(ring):
            step(i * ring + r, i, r)


class Core:

    def __init__(self, nc):
        self.nc, self.used, self.w = nc, [], {}

    def semaphore(self, name):
        self.used.append(self.nc.alloc_semaphore(name=name))
        return self.used[-1]

    def clear_semaphores(self):
        self.nc.clear_and_free_semaphores(self.used)
        self.nc.all_engine_barrier()
        self.used = []


def arena(c, start, shape, dtype=F32):
    n = 1
    for s in shape:
        n *= s
    words = n if dtype != BF16 else n // 2
    ap = c.arena[:, start:start + words]
    if dtype != F32:
        ap = ap.bitcast(dtype)
    if len(shape) == 2:
        return ap.rearrange("p (a b) -> p a b", b=shape[1])
    if len(shape) == 3:
        return ap.rearrange("p (a b c) -> p a b c", b=shape[1], c=shape[2])
    return ap


def wide(ap, n):
    return ap.unsqueeze(2).broadcast_to([ap.shape[0], ap.shape[1], n])


def over(ap, n):
    return ap.unsqueeze(1).broadcast_to([ap.shape[0], n, ap.shape[1]])


def stage_setup(nc, c, t):
    with ExitStack() as ctx:
        sem = lambda n: c.semaphore(n)
        loaded, base, ready, cleared = sem("su_loaded"), sem("su_base"), sem("su_ready"), sem("su_cleared")
        filled, ints, copied = sem("su_filled"), sem("su_ints"), sem("su_copied")
        jint = ctx.enter_context(nc.sbuf_tensor("jint", [P, TILES], I32))
        pint = ctx.enter_context(nc.sbuf_tensor("pint", [P, 8], I32))
        fill = ctx.enter_context(nc.sbuf_tensor("fill", [P, SLOTS * 2 // P], F32))
        loads = [(c.src_i, t["src"].rearrange("(p n) -> p n", p=P)),
                 (c.dst_i, t["dst"].rearrange("(p n) -> p n", p=P))]
        whole = N // P * P
        block = ctx.enter_context(nc.Block())

        @block.sync
        def _(sp):
            for dst, src in loads:
                sp.dma_start(dst, src).then_inc(loaded, 16)
            sp.dma_start(c.x[:, 0:N // P, :], t["x"][0:whole, :].rearrange("(t p) f -> p t f", p=P)).then_inc(loaded, 16)
            sp.wait_ge(cleared, 1)
            sp.dma_start(c.x[0:N - whole, N // P, :], t["x"][whole:N, :]).then_inc(loaded, 16)
            sp.wait_ge(filled, 1)
            sp.dma_start(c.records.rearrange("(p n) two -> p (n two)", p=P), fill[:, :]).then_inc(loaded, 16)
            sp.wait_ge(loaded, 16 * (len(loads) + 3))

        @block.gpsimd
        def _(pool):
            pool.iota(jint[:, :], [[1, TILES]], base=0, channel_multiplier=0).then_inc(ints, 1)
            pool.iota(pint[:, :], [[0, 8]], base=0, channel_multiplier=1).then_inc(ints, 1)
            pool.memset(c.ones[:, :], 1.0).then_inc(base, 1)
            pool.memset(c.ident[:, :], 0.0).then_inc(base, 1)
            pool.wait_ge(base, 2)
            pool.affine_select(out=c.ident[:, :], in_=c.ident[:, :], compare_op=ALU.not_equal, fill=1.0,
                               base=0, pattern=[[-1, P]], channel_multiplier=1).then_inc(base, 1)
            pool.affine_select(out=c.before[:, :], in_=c.ones[:, :], compare_op=ALU.is_gt, fill=0.0,
                               base=0, pattern=[[1, P]], channel_multiplier=-1).then_inc(base, 1)
            pool.affine_select(out=c.previous[:, :], in_=c.ones[:, :], compare_op=ALU.is_equal, fill=0.0,
                               base=1, pattern=[[-1, P]], channel_multiplier=1).then_inc(base, 1)
            pool.wait_ge(base, 5)
            pool.memset(fill[:, :], float(NOWHERE)).then_inc(filled, 1)

        @block.scalar
        def _(act):
            act.wait_ge(loaded, 16 * (len(loads) + 3))
            act.activation(c.src_f[:, :], c.src_i, ACT.Copy).then_inc(copied, 1)
            act.activation(c.dst_f[:, :], c.dst_i, ACT.Copy).then_inc(copied, 1)

        @block.vector
        def _(dve):
            dve.memset(c.x[:, N // P:NT, :], 0.0).then_inc(cleared, 1)
            dve.wait_ge(ints, 2)
            dve.tensor_copy(c.j[:, :], jint[:, :]).then_inc(ready, 1)
            dve.tensor_copy(c.part[:, :], pint[:, 0:1]).then_inc(ready, 1)
            dve.wait_ge(ready, 2)
            dve.tensor_scalar(c.bounds[:, :], c.j[:, 0:NB], float(P), float(P), ALU.mult, ALU.add).then_inc(ready, 1)


def stage_lists(nc, c, t):
    with ExitStack() as ctx:
        sem = lambda n: c.semaphore(n)
        sb = lambda n, s, d: ctx.enter_context(nc.sbuf_tensor(n, s, d))
        pb = lambda n, s, d: ctx.enter_context(nc.psum_tensor(n, s, d))
        counted, tick, v, m = sem("li_counted"), sem("li_tick"), sem("li_v"), sem("li_m")
        gathered, floats, turned = [sem(f"li_gathered{i}") for i in range(3)], sem("li_floats"), sem("li_turned")
        sined, stored = sem("li_sined"), sem("li_stored")
        junk = sb("li_junk", [P, CHUNK], F32)
        count = {s: sb(f"li_count_{s}", [P, NB], F32) for s in "ds"}
        small = {s: sb(f"li_small_{s}", [P, 8], F32) for s in "ds"}
        whole = {s: sb(f"li_whole_{s}", [P, 1], I32) for s in "ds"}
        inside, past, wider = arena(c, B1_0, [TILES]), arena(c, B1_0 + TILES, [TILES]), sb("li_wider", [P, P], F32)
        slot0 = sb("li_slot0", [NB, NB], F32)
        own = sb("li_own", [P, NB], F32)
        cols_f, cols_i = sb("li_cols_f", [P, 8], F32), sb("li_cols_i", [P, 8], I32)
        bucket_c = sb("li_bucket_c", [P, 8], F32)
        rows_bf = arena(c, ACC0 + 4 * 1024, [JC, P], BF16)
        fields_i = arena(c, ACC0, [2, JC, P], I32)
        fields = arena(c, B1_0 + 2 * TILES, [3, JC, P])
        bucket_f = arena(c, B2_0, [TILES])
        mask, mask2 = arena(c, B2_0 + TILES, [TILES]), arena(c, B2_0 + 2 * TILES, [TILES])
        half = TILES // 2
        ps = pb("li_ps", [P, 512], F32)
        psw = pb("li_psw", [P, 2, 512], F32)
        psb = pb("li_psb", [P, 2, 512], F32)
        psf = pb("li_psf", [P, 2, 512], F32)
        psc = pb("li_psc", [P, 512], F32)
        flat = {"src": t["src"], "dst": t["dst"], "w": t["edge_weight"]}
        block = ctx.enter_context(nc.Block())
        V = {}
        M = {name: n + 1 for n, name in enumerate([
            "dends", "dstarts", "dfirst", "cols", "dbucket", "sends", "sstarts", "sfirst", "sbucket", "base",
            "turnedsrc", "turneddst", "turnedw"])}

        @block.vector
        def _(dve):
            n = [0]

            def done(ins, name=None):
                n[0] += 1
                ins.then_inc(v, 1)
                if name:
                    V[name] = n[0]
                dve.wait_ge(v, n[0])

            def counts(side, key):
                def one(b):
                    return dve.tensor_scalar(junk[:, :], key[:, :], c.bounds[:, bass.ds(b, 1)], 0.0, ALU.is_lt,
                                             ALU.add, accum_out=count[side][:, bass.ds(b, 1)])
                base = 0 if side == "d" else NB
                if base:
                    dve.wait_ge(counted, base)
                one(0).then_inc(counted, 1)
                with dve.Fori(1, NB) as b:
                    at_least(dve, counted, b + base, tick)
                    one(b).then_inc(counted, 1)
                dve.wait_ge(counted, base + NB)

            def tiles_of(side):
                s = small[side][0:NB, :]
                dve.wait_ge(m, M[side + "ends"])
                done(dve.tensor_copy(s[:, 0:1], ps[0:NB, 0:1]), side + "ends")
                dve.wait_ge(m, M[side + "starts"])
                done(dve.tensor_copy(s[:, 1:2], ps[0:NB, 1:2]))
                done(dve.tensor_tensor(s[:, 2:3], s[:, 0:1], s[:, 1:2], ALU.subtract))
                done(dve.tensor_scalar(whole[side][0:NB, :], s[:, 2:3], float(P - 1), None, ALU.add))
                done(dve.tensor_scalar(whole[side][0:NB, :], whole[side][0:NB, :], 7, None, ALU.arith_shift_right))
                done(dve.tensor_copy(s[:, 3:4], whole[side][0:NB, :]))
                done(dve.tensor_scalar(s[:, 3:4], s[:, 3:4], 1.0, None, ALU.max), side + "tiles")
                dve.wait_ge(m, M[side + "first"])
                done(dve.tensor_copy(s[:, 4:5], ps[0:NB, 2:3]))
                done(dve.tensor_tensor(s[:, 5:6], s[:, 4:5], s[:, 3:4], ALU.add))
                done(dve.scalar_tensor_tensor(out=s[:, 6:7], in0=s[:, 4:5], scalar=-float(P), in1=s[:, 1:2],
                                              op0=ALU.mult, op1=ALU.add))
                done(dve.tensor_scalar(past[0:NB, :], c.j[0:NB, :], s[:, 5:6], None, ALU.is_ge), side + "past")

            counts("d", c.dst_f)
            tiles_of("d")
            s = small["d"][0:NB, :]
            done(dve.tensor_scalar(inside[0:NB, :], c.j[0:NB, :], s[:, 4:5], None, ALU.is_ge))
            done(dve.tensor_tensor(inside[0:NB, :], inside[0:NB, :], past[0:NB, :], ALU.subtract))
            done(dve.tensor_scalar(wider[0:NB, :], c.ones[0:NB, :], s[:, 6:7], None, ALU.mult), "wider")
            done(dve.memset(cols_f[:, :], 0.0))
            done(dve.memset(bucket_c[:, :], 0.0))
            dve.wait_ge(m, M["cols"])
            for k in range(JC):
                q = min(P, TILES - k * P)
                done(dve.tensor_scalar(cols_f[0:q, k:k + 1], c.part[0:q, :], float(P), float(k * P * P), ALU.mult, ALU.add))
                done(dve.tensor_tensor(cols_f[0:q, k:k + 1], cols_f[0:q, k:k + 1], ps[0:q, 8 + k:9 + k], ALU.add))
            done(dve.tensor_scalar(cols_i[:, :], cols_f[:, :], float(E - 1), None, ALU.min), "columns")
            dve.wait_ge(m, M["dbucket"])
            for k in range(JC):
                q = min(P, TILES - k * P)
                done(dve.tensor_scalar(bucket_c[0:q, k:k + 1], psc[0:q, k:k + 1], -float(P), None, ALU.mult))
            for h in range(2):
                at = slice(h * half, (h + 1) * half)
                done(dve.scalar_tensor_tensor(out=mask[32:33, at], in0=c.j[32:33, at], scalar=float(P), in1=psw[32:33, h, 0:half],
                                              op0=ALU.mult, op1=ALU.add))
                done(dve.tensor_copy(bucket_f[:, at], psb[:, h, 0:half]))
            done(dve.tensor_scalar(c.edge0, mask[32:33, :], float(E - 1), None, ALU.min))
            done(dve.tensor_copy(c.bucket_d, bucket_f[0:1, :]), "dused")

            counts("s", c.src_f)
            tiles_of("s")
            dve.wait_ge(m, M["sbucket"])
            for h in range(2):
                at = slice(h * half, (h + 1) * half)
                done(dve.tensor_scalar(c.window_s[:, at], psb[:, h, 0:half], float(P), None, ALU.mult))
                done(dve.tensor_copy(c.bucket_s[:, at], psb[64:65, h, 0:half]))
            done(dve.tensor_scalar(slot0[:, :], c.ident[0:NB, 0:NB], small["s"][0:NB, 4:5], float(P), ALU.mult, ALU.mult))
            done(dve.tensor_copy(own[:, :], count["s"][:, :]))
            done(dve.tensor_tensor(own[:, 1:NB], count["s"][:, 1:NB], count["s"][:, 0:NB - 1], ALU.subtract), "own")
            dve.wait_ge(m, M["base"])
            done(dve.tensor_scalar(c.base[:, :], ps[:, 64:64 + NB], -1.0, None, ALU.add))
            done(dve.tensor_scalar(c.src_i, c.src_i, 7, None, ALU.arith_shift_right))
            done(dve.tensor_copy(c.src_bucket[:, :], c.src_i))
            done(dve.tensor_scalar(c.slot_of[:, :], c.src_bucket[:, :], float(NB), float(4 * SLOTS), ALU.is_ge, ALU.mult))

            dve.wait_ge(floats, 2)
            for k in range(JC):
                q = min(P, TILES - k * P)
                done(dve.tensor_scalar(rows_bf[0:q, k, :], fields[0:q, 1, k, :], bucket_c[0:q, k:k + 1], None, ALU.add), "rows")
            for f, name in enumerate(["src", "dst", "w"]):
                dve.wait_ge(m, M["turned" + name])
                for h, (a, b) in enumerate(((0, 512), (512, TILES))):
                    got = psf[:, h, 0:b - a]
                    if name == "src":
                        ins = dve.tensor_scalar(c.gather_d[:, a:b], got, float(N - 1), None, ALU.min)
                    elif name == "dst":
                        ins = dve.scalar_tensor_tensor(out=c.local_d[:, a:b], in0=bucket_f[:, a:b], scalar=-float(P), in1=got,
                                                       op0=ALU.mult, op1=ALU.add)
                    else:
                        ins = dve.tensor_copy(c.weight[:, a:b], got)
                    done(ins, f"took{name}{h}")
            done(dve.tensor_scalar(mask, c.local_d[:, :], 0.0, None, ALU.is_ge))
            done(dve.tensor_scalar(mask2, c.local_d[:, :], float(P), None, ALU.is_lt))
            done(dve.tensor_tensor(mask, mask, mask2, ALU.mult))
            done(dve.scalar_tensor_tensor(out=mask2, in0=bucket_f, scalar=float(P), in1=c.local_d[:, :], op0=ALU.mult, op1=ALU.add))
            done(dve.scalar_tensor_tensor(out=mask, in0=mask2, scalar=1.0, in1=mask, op0=ALU.add, op1=ALU.mult))
            done(dve.tensor_scalar(c.key[:, :], mask, -1.0, None, ALU.add))
            big = 1.5 * 2.0 ** 23
            done(dve.tensor_scalar(mask, c.weight[:, :], 1.0 / 20.0, None, ALU.mult))
            done(dve.tensor_scalar(mask2, mask, big, None, ALU.add))
            done(dve.tensor_scalar(mask2, mask2, -big, None, ALU.add))
            done(dve.tensor_tensor(mask, mask, mask2, ALU.subtract), "sine_arg")
            dve.wait_ge(sined, 1)
            done(dve.tensor_tensor(mask, mask2, mask2, ALU.mult))
            done(dve.tensor_scalar(c.cutoff[:, :], mask, -1.0, 1.0, ALU.mult, ALU.add))

        @block.gpsimd
        def _(pool):
            pool.wait_ge(v, V["columns"])
            for f, name in enumerate(["src", "dst", "w"]):
                table = flat[name].rearrange("(e one) -> e one", one=1)
                for k in range(JC):
                    to = fields[:, 2, k, :] if name == "w" else fields_i[:, f, k, :]
                    pool.indirect_dma_start(to, None, table, bass.IndirectOffsetOnAxis(cols_i[:, k:k + 1], 0))\
                        .then_inc(gathered[f], 16)

        @block.sync
        def _(sp):
            sp.wait_ge(v, V["rows"])
            full, rest = TILES // P, TILES % P
            sp.dma_start(c.local_rows[0:full * P, :].rearrange("(k j) f -> j k f", j=P), rows_bf[:, 0:full, :]).then_inc(stored, 16)
            sp.dma_start(c.local_rows[full * P:TILES, :], rows_bf[0:rest, full, :]).then_inc(stored, 16)
            sp.wait_ge(stored, 32)

        @block.scalar
        def _(act):
            for f in range(2):
                act.wait_ge(gathered[f], 16 * JC)
                act.activation(fields[:, f, :, :], fields_i[:, f, :, :], ACT.Copy).then_inc(floats, 1)
            act.wait_ge(v, V["sine_arg"])
            act.activation(mask2, mask, ACT.Sin, scale=3.141592653589793).then_inc(sined, 1)

        @block.tensor
        def _(pe):
            n = [0]

            def mark(ins, name):
                n[0] += 1
                ins.then_inc(m, 1)
                assert M[name] == n[0]

            for side in "ds":
                s = small[side]
                pe.wait_ge(counted, NB if side == "d" else 2 * NB)
                if side == "s":
                    pe.wait_ge(v, V["dused"])
                mark(pe.matmul(ps[0:NB, 0:1], count[side][:, :], c.ones[:, 0:1], start=True, stop=True), side + "ends")
                pe.wait_ge(v, V[side + "ends"])
                mark(pe.matmul(ps[0:NB, 1:2], c.previous[0:NB, 0:NB], s[0:NB, 0:1], start=True, stop=True), side + "starts")
                pe.wait_ge(v, V[side + "tiles"])
                mark(pe.matmul(ps[0:NB, 2:3], c.before[0:NB, 0:NB], s[0:NB, 3:4], start=True, stop=True), side + "first")
                if side == "d":
                    pe.wait_ge(v, V["wider"])
                    for k in range(JC):
                        q = min(P, TILES - k * P)
                        ins = pe.matmul(ps[0:q, 8 + k:9 + k], inside[0:NB, k * P:k * P + q], s[0:NB, 6:7], start=True, stop=True)
                    mark(ins, "cols")
                    for h in range(2):
                        pe.matmul(psw[:, h, 0:half], wider[0:NB, :], inside[0:NB, h * half:(h + 1) * half], start=True, stop=True)
                pe.wait_ge(v, V[side + "past"])
                for h in range(2):
                    ins = pe.matmul(psb[:, h, 0:half], c.ones[0:NB, :], past[0:NB, h * half:(h + 1) * half], start=True, stop=True)
                if side == "d":
                    for k in range(JC):
                        q = min(P, TILES - k * P)
                        ins = pe.matmul(psc[0:q, k:k + 1], past[0:NB, k * P:k * P + q], c.ones[0:NB, 0:1], start=True, stop=True)
                mark(ins, side + "bucket")
            pe.wait_ge(v, V["own"])
            pe.matmul(ps[:, 64:64 + NB], c.before[:, :], own[:, :], start=True, stop=False)
            mark(pe.matmul(ps[:, 64:64 + NB], c.ones[0:NB, :], slot0[:, :], start=False, stop=True), "base")
            for f, name in enumerate(["src", "dst", "w"]):
                if f < 2:
                    pe.wait_ge(floats, f + 1)
                else:
                    pe.wait_ge(gathered[2], 16 * JC)
                if f:
                    pe.wait_ge(v, V[f"took{['src', 'dst', 'w'][f - 1]}1"])
                for k in range(JC):
                    q = min(P, TILES - k * P)
                    ins = pe.transpose(psf[:, k // 4, k % 4 * P:k % 4 * P + q], fields[0:q, f, k, :], c.ident[0:q, 0:q])
                mark(ins, "turned" + name)


def sweep(nc, c, name, sources, products, vector=None, scalar=None, store=None):
    with ExitStack() as ctx:
        sem = lambda n: c.semaphore(name + n)
        turned, copied, multiplied, tick = sem("_turned"), sem("_copied"), sem("_multiplied"), sem("_tick")
        staged = sem("_staged")
        fixed = ctx.enter_context(nc.sbuf_tensor(name + "_fixed", [P, 2, len(sources), P], F32))
        vec, sca = sem("_vector"), sem("_scalar")
        stored = [sem(f"_stored{q}") for q in range(2)]
        xt = ctx.enter_context(nc.sbuf_tensor(name + "_xt", [P, 2, len(sources), P], F32))
        ring = ctx.enter_context(nc.sbuf_tensor(name + "_ring", [P, 2, 384], F32)) if store else None
        pt = ctx.enter_context(nc.psum_tensor(name + "_pt", [P, 2, 512], F32))
        po = ctx.enter_context(nc.psum_tensor(name + "_po", [P, 2, 512], F32))
        n_src = len(sources)
        n_store = len(store(0)) if store else 0
        block = ctx.enter_context(nc.Block())

        @block.gpsimd
        def _(pool):
            def step(k, i, q):
                at_least(pool, turned, k - 1, tick)
                for s, (src, m) in enumerate(sources):
                    pool.tensor_copy(fixed[:, q, s, 0:m], src(k)).then_inc(staged, 1)
            rounds(pool, NT, 2, step)

        @block.tensor
        def _(pe):
            def turn(k, q):
                at_least(pe, staged, n_src * (k + 1), tick)
                at_least(pe, copied, n_src * (k - 1), tick)
                for s, (src, m) in enumerate(sources):
                    ins = pe.transpose(pt[0:m, q, s * P:(s + 1) * P], fixed[:, q, s, 0:m], c.ident[:, :])
                ins.then_inc(turned, 1)

            def multiply(k, q):
                at_least(pe, copied, n_src * (k + 1), tick)
                if vector:
                    at_least(pe, vec, k - 1, tick)
                if scalar:
                    at_least(pe, sca, k - 1, tick)
                for n, (s, rhs, a, b) in enumerate(products):
                    m = rhs.shape[0]
                    lhs = c.ones[0:m, :] if s is None else xt[0:m, q, s, :]
                    ins = pe.matmul(po[:, q, a:b], lhs, rhs, start=(n == 0), stop=(n == len(products) - 1))
                ins.then_inc(multiplied, 1)

            def step(k, i, q):
                turn(k, q)
                if not isinstance(k, int) or k > 0:
                    multiply(k - 1, 1 - q)
            rounds(pe, NT, 2, step)
            multiply(NT - 1, (NT - 1) % 2)

        @block.scalar
        def _(act):
            def copy(k, q):
                at_least(act, turned, k + 1, tick)
                at_least(act, multiplied, k - 1, tick)
                for s, (src, m) in enumerate(sources):
                    act.activation(xt[0:m, q, s, :], pt[0:m, q, s * P:(s + 1) * P], ACT.Copy).then_inc(copied, 1)

            def evacuate(k, i, q):
                at_least(act, multiplied, k + 1, tick)
                if vector:
                    at_least(act, vec, k + 1, tick)
                if store:
                    at_least(act, stored[q], i * 16 * n_store, tick)
                scalar(act, k, po[:, q, :], ring[:, q, :] if store else None).then_inc(sca, 1)

            def step(k, i, q):
                copy(k, q)
                if scalar and (not isinstance(k, int) or k > 0):
                    evacuate(k - 1, i if q else i - 1, 1 - q)
            rounds(act, NT, 2, step, peeled=2)
            if scalar:
                evacuate(NT - 1, NT // 2 - 1, 1)

        if vector:
            @block.vector
            def _(dve):
                def step(k, i, q):
                    at_least(dve, multiplied, k + 1, tick)
                    vector(dve, k, po[:, q, :]).then_inc(vec, 1)
                rounds(dve, NT, 2, step)

        if store:
            @block.sync
            def _(sp):
                def step(k, i, q):
                    at_least(sp, sca, k + 1, tick)
                    for dram, a, b in store(k):
                        sp.dma_start(dram, ring[:, q, a:b]).then_inc(stored[q], 16)
                rounds(sp, NT, 2, step)
                for q in range(2):
                    sp.wait_ge(stored[q], NT // 2 * 16 * n_store)


def vector_scalar_stage(nc, c, name, steps):
    with ExitStack() as ctx:
        done = c.semaphore(name + "_done")
        block = ctx.enter_context(nc.Block())

        def run(eng, mine):
            for n, (who, step) in enumerate(steps):
                if who == mine:
                    if n:
                        eng.wait_ge(done, n)
                    step(eng).then_inc(done, 1)

        @block.vector
        def _(dve):
            run(dve, "v")

        @block.scalar
        def _(act):
            run(act, "s")


def norm_steps(c, y, squares, small, gamma=None, beta=None, residual=None, out=None):
    s, r = small[:, 0, :], small[:, 1, :]
    steps = [
        ("v", lambda e: e.tensor_reduce(s, y, AX_X, ALU.add)),
        ("v", lambda e: e.tensor_scalar(s, s, 1.0 / F, None, ALU.mult)),
        ("v", lambda e: e.tensor_tensor(y, y, wide(s, F), ALU.subtract)),
        ("s", lambda e: e.activation(squares, y, ACT.Square)),
        ("v", lambda e: e.tensor_reduce(s, squares, AX_X, ALU.add)),
        ("v", lambda e: e.tensor_scalar(s, s, 1.0 / F, LN_EPS, ALU.mult, ALU.add)),
        ("s", lambda e: e.activation(r, s, ACT.Sqrt)),
        ("v", lambda e: e.reciprocal(s, r)),
        ("v", lambda e: e.tensor_tensor(y if out is None else out, y, wide(s, F), ALU.mult)),
    ]
    if gamma is not None:
        steps += [("v", lambda e: e.tensor_tensor(y, y, over(gamma, NT), ALU.mult)),
                  ("v", lambda e: e.tensor_tensor(y, y, over(beta, NT), ALU.add))]
    if residual is not None:
        steps += [("v", lambda e: e.tensor_tensor(y, y, residual, ALU.add))]
    return steps


def split_steps(full, parts):
    return [
        ("s", lambda e: e.activation(parts[0], full, ACT.Copy)),
        ("v", lambda e: e.tensor_tensor(full, full, parts[0], ALU.subtract)),
        ("s", lambda e: e.activation(parts[1], full, ACT.Copy)),
        ("v", lambda e: e.tensor_tensor(full, full, parts[1], ALU.subtract)),
        ("s", lambda e: e.activation(parts[2], full, ACT.Copy)),
    ]


def gather_rows(pool, c, table, index, ring, index_ready, arrived, freed, tick):
    def step(k, i, r):
        at_least(pool, index_ready, k + 1, tick)
        for sem, per in freed:
            if isinstance(sem, list):
                at_least(pool, sem[r], per * i, tick)
            else:
                at_least(pool, sem, per * (k - R + 1), tick)
        for u in range(U):
            pool.indirect_dma_start(ring[:, r, u, :], None, table, bass.IndirectOffsetOnAxis(index[:, r, u:u + 1], 0))\
                .then_inc(arrived[r], 16)
    rounds(pool, BATCHES, R, step)


def take_index(act, source, index, k, i, r, arrived, index_ready, tick):
    at_least(act, arrived[r], i * 16 * U, tick)
    act.activation(index[:, r, :], source[:, bass.ds(k * U, U)], ACT.Copy).then_inc(index_ready, 1)


def is_first(k):
    return isinstance(k, int) and k == 0


def loaded_values(nc, row, k, engine, top):
    return nc.values_load_multi_w_load_instructions(
        row[:, bass.ds(k * U, U)], engines=(engine,), min_val=0, max_val=top,
        skip_runtime_bounds_check_because="the vector engine made them within these bounds")[1]


class Adds:

    def __init__(self, nc, dve, acc, buckets, psum, width, k, summed, added, tick):
        self.which = loaded_values(nc, buckets, k, DVE_ENGINE, NT - 1)
        self.dve, self.acc, self.psum, self.width, self.k, self.added, self.tick = dve, acc, psum, width, k, added, tick
        self.summed = summed

    def one(self, u):
        if u == 0:
            at_least(self.dve, self.summed, self.k + 1, self.tick)
        at_least(self.dve, self.added, self.k * U + u, self.tick)
        to = self.acc[:, bass.ds(self.which[u], 1), 0:self.width].rearrange("p one f -> p (one f)")
        self.dve.tensor_tensor(to, to, self.psum[:, u, 0:self.width], ALU.add).then_inc(self.added, 1)


def between(adds, steps):
    for n in range(max(U, len(steps))):
        if n < len(steps):
            steps[n]()
        if adds is not None and n < U:
            adds.one(n)


def load_local_rows(sp, c, rows, k, r, arrived):
    src = c.local_rows[bass.ds(k * U, U), :].rearrange("(one u) f -> one (u f)", one=1)
    sp.dma_start(rows[:, r, :], src.broadcast_to([P, U * P])).then_inc(arrived[r], 16)


def stage_attention_scores(nc, c):
    with ExitStack() as ctx:
        sem = lambda n: c.semaphore("at_" + n)
        sb = lambda n, s, d: ctx.enter_context(nc.sbuf_tensor("at_" + n, s, d))
        index, ring = sb("index", [P, R, U], I32), sb("ring", [P, R, U, 2 * F], F32)
        rows, hot_t, prod, we = sb("rows", [P, R, U * P], BF16), sb("hot_t", [P, R, U, P], BF16), sb("prod", [P, 2, U, F], F32), sb("we", [P, 2, U, H], F32)
        rank, match = sb("rank", [P, CHUNK], F32), sb("match", [P, CHUNK], F32)
        pq = ctx.enter_context(nc.psum_tensor("at_pq", [P, 2, U, 256], F32))
        index_ready, arrived, kept = sem("index"), [sem(f"arrived{r}") for r in range(R)], [sem(f"kept{r}") for r in range(R)]
        rows_in = [sem(f"rows{r}") for r in range(R)]
        hots, queried, producted, reduced, weighed, scored, ranked, tick = (
            sem(n) for n in ("hots", "queried", "producted", "reduced", "weighed", "scored", "ranked", "tick"))
        block = ctx.enter_context(nc.Block())

        @block.gpsimd
        def _(pool):
            gather_rows(pool, c, c.kv, index, ring, index_ready, arrived, [(producted, 1), (kept, 16)], tick)

        @block.sync
        def _(sp):
            def step(k, i, r):
                at_least(sp, hots, k - R + 1, tick)
                load_local_rows(sp, c, rows, k, r, rows_in)
                if not is_first(k):
                    keep(k - 1, i if r else i - 1, (r - 1) % R)

            def keep(k, i, r):
                at_least(sp, arrived[r], 16 * U * (i + 1), tick)
                sp.dma_start(c.values[bass.ds(k, 1), :, :, :].rearrange("one p u f -> p (one u) f"), ring[:, r, :, F:2 * F]).then_inc(kept[r], 16)
            rounds(sp, BATCHES, R, step)
            keep(BATCHES - 1, BATCHES // R - 1, R - 1)
            for r in range(R):
                sp.wait_ge(kept[r], 16 * BATCHES // R)

        @block.scalar
        def _(act):
            rounds(act, BATCHES, R, lambda k, i, r: take_index(act, c.gather_d, index, k, i, r, arrived, index_ready, tick))

        @block.tensor
        def _(pe):
            def step(k, i, r):
                q = r % 2
                which = loaded_values(nc, c.bucket_d, k, PE_ENGINE, NT - 1)
                at_least(pe, hots, k + 1, tick)
                at_least(pe, weighed, k - 1, tick)
                at_least(pe, producted, k - 1, tick)
                for u in range(U):
                    for n, part in enumerate(c.query_parts):
                        ins = pe.matmul(pq[:, q, u, 0:QW], hot_t[:, r, u, :],
                                        part[:, bass.ds(which[u], 1), :].rearrange("p one f -> p (one f)"),
                                        start=(n == 0), stop=(n == 2))
                ins.then_inc(queried, 1)
            rounds(pe, BATCHES, R, step)

        @block.vector
        def _(dve):
            def one_hot(k, i, r):
                at_least(dve, rows_in[r], 16 * (i + 1), tick)
                at_least(dve, queried, k - R + 1, tick)
                dve.tensor_scalar(hot_t[:, r, :, :].rearrange("p u f -> p (u f)"), rows[:, r, :], c.part[:, 0:1], None, ALU.is_equal).then_inc(hots, 1)

            def products(k, i, r):
                q = r % 2
                at_least(dve, queried, k + 1, tick)
                at_least(dve, arrived[r], 16 * U * (i + 1), tick)
                at_least(dve, reduced, k - 1, tick)
                dve.tensor_tensor(prod[:, q, :, :], pq[:, q, :, 0:F], ring[:, r, :, 0:F], ALU.mult).then_inc(producted, 1)
                at_least(dve, scored, k - 1, tick)
                dve.tensor_tensor(we[:, q, :, :], pq[:, q, :, F:QW], wide(c.weight[:, bass.ds(k * U, U)], H), ALU.mult).then_inc(weighed, 1)

            def head_sums(k, r):
                at_least(dve, producted, k + 1, tick)
                to = c.alpha[:, bass.ds(k * U, U), :].rearrange("p u h -> p (u h)")
                dve.tensor_reduce(to, prod[:, r % 2, :, :].rearrange("p u (h d) -> p (u h) d", d=D), AX_X, ALU.add).then_inc(reduced, 1)

            def finish(k, r):
                at_least(dve, reduced, k + 1, tick)
                at_least(dve, weighed, k + 1, tick)
                to = c.alpha[:, bass.ds(k * U, U), :].rearrange("p u h -> p (u h)")
                dve.tensor_tensor(to, to, we[:, r % 2, :, :].rearrange("p u h -> p (u h)"), ALU.add).then_inc(scored, 1)

            def rank_bucket(b, part):
                at_least(dve, ranked, b * 4 + part, tick)
                if part == 0:
                    ins = dve.tensor_scalar(match[:, :], c.src_bucket[:, :], c.j[:, bass.ds(b, 1)], None, ALU.is_equal)
                if part == 1:
                    ins = dve.tensor_tensor_scan(rank[:, :], c.ones[:, 0:1].broadcast_to([P, CHUNK]), match[:, :],
                                                 c.base[:, bass.ds(b, 1)], ALU.mult, ALU.add)
                if part == 2:
                    ins = dve.tensor_tensor(rank[:, :], rank[:, :], match[:, :], ALU.mult)
                if part == 3:
                    ins = dve.tensor_tensor(c.slot_of[:, :], c.slot_of[:, :], rank[:, :], ALU.add)
                ins.then_inc(ranked, 1)

            def step(k, i, r, bucket=None):
                known = k if isinstance(k, int) else R
                one_hot(k, i, r)
                if known >= 2:
                    head_sums(k - 2, (r - 2) % R)
                if known >= 1:
                    products(k - 1, i if r else i - 1, (r - 1) % R)
                if known >= 2:
                    finish(k - 2, (r - 2) % R)
                if bucket is not None:
                    rank_bucket(bucket, r)
            for r in range(R):
                step(r, 0, r, 0)
            with dve.Fori(1, NB) as i:
                for r in range(R):
                    step(i * R + r, i, r, i)
            with dve.Fori(NB, BATCHES // R) as i:
                for r in range(R):
                    step(i * R + r, i, r)
            last = BATCHES - 1
            head_sums(last - 1, R - 2)
            products(last, BATCHES // R - 1, R - 1)
            finish(last - 1, R - 2)
            head_sums(last, R - 1)
            finish(last, R - 1)
            dve.wait_ge(scored, BATCHES)


def stage_attention_max(nc, c):
    with ExitStack() as ctx:
        v, m, s = (c.semaphore("mx_" + n) for n in ("v", "m", "s"))
        sb = lambda n, shape: ctx.enter_context(nc.sbuf_tensor("mx_" + n, shape, F32))
        a = arena(c, ACC0, [H, SL])[0:SP_PARTS, :, :]
        b = arena(c, ACC0 + H * SL, [H, SL])[0:SP_PARTS, :, :]
        pen, keys = sb("pen", [P, SL + 2]), sb("keys", [P, SL])
        ends, carry = sb("ends", [P, 4, H]), sb("carry", [P, 2, H])
        row = sb("row", [H, 10, P])
        pt = ctx.enter_context(nc.psum_tensor("mx_pt", [P, 4, 512], F32))
        Q = SP_PARTS
        pieces = [(h, g) for h in range(H) for g in range(SQ // 4)]
        block = ctx.enter_context(nc.Block())
        V, M, S = {}, {}, {}
        order = [f"keys{g}" for g in range(SQ // 4)] + [f"in{h}{g}" for h, g in pieces] + ["ends", "back0", "ends1", "back1"]
        order += [f"out{n}" for n in range(2 * H)]
        for n, name in enumerate(order):
            M[name] = n + 1
        takes = ([f"keys{g}" for g in range(SQ // 4)] + [f"in{h}{g}" for h, g in pieces])
        for n, name in enumerate(takes):
            S[name] = n + 1

        @block.vector
        def _(dve):
            n = [0]

            def done(ins, name=None):
                n[0] += 1
                ins.then_inc(v, 1)
                if name:
                    V[name] = n[0]
                dve.wait_ge(v, n[0])

            dve.wait_ge(s, S[f"keys{SQ // 4 - 1}"])
            done(dve.memset(pen[:, :], 0.0))
            done(dve.tensor_tensor(pen[0:Q, 1:SL], keys[0:Q, 1:SL], keys[0:Q, 0:SL - 1], ALU.not_equal))
            done(dve.tensor_scalar(pen[0:Q, 1:SL], pen[0:Q, 1:SL], FAR, None, ALU.mult))
            done(dve.tensor_copy(ends[0:Q, 2, :], keys[0:Q, 0:1].broadcast_to([Q, H])))
            done(dve.tensor_copy(ends[0:Q, 3, :], keys[0:Q, SL - 1:SL].broadcast_to([Q, H])))
            dve.wait_ge(s, len(takes))

            def scan(to, src, initial, backward):
                for h in range(H):
                    x0 = initial if isinstance(initial, float) else initial[0:Q, h:h + 1]
                    if backward:
                        ins = dve.tensor_tensor_scan(to[:, h, ::-1], pen[0:Q, 1:SL + 1][:, ::-1], src[:, h, ::-1], x0, ALU.add, ALU.max)
                    else:
                        ins = dve.tensor_tensor_scan(to[:, h, :], pen[0:Q, 0:SL], src[:, h, :], x0, ALU.add, ALU.max)
                    n[0] += 1
                    ins.then_inc(v, 1)
                dve.wait_ge(v, n[0])

            scan(b, a, FAR, False)
            done(dve.tensor_copy(ends[0:Q, 0, :], b[:, :, SL - 1]), "ends")
            dve.wait_ge(m, M["ends"])
            for f, w in ((0, 2), (1, 3), (2, 0)):
                done(dve.tensor_copy(row[:, f, 0:Q], pt[0:H, 0, w * P:w * P + Q]), "took")
            done(dve.tensor_tensor(row[:, 3, 0:Q], row[:, 0, 0:Q], row[:, 1, 0:Q], ALU.is_equal))
            done(dve.memset(row[:, 4, :], 0.0))
            done(dve.tensor_tensor(row[:, 4, 1:Q], row[:, 0, 1:Q], row[:, 1, 0:Q - 1], ALU.is_equal))
            done(dve.tensor_tensor(row[:, 5, 0:Q], row[:, 3, 0:Q], row[:, 4, 0:Q], ALU.mult))
            done(dve.tensor_scalar(row[:, 5, 0:Q], row[:, 5, 0:Q], -FAR, FAR, ALU.mult, ALU.add))
            done(dve.tensor_tensor_scan(row[:, 6, 0:Q], row[:, 5, 0:Q], row[:, 2, 0:Q], FAR, ALU.add, ALU.max))
            done(dve.tensor_scalar(row[:, 8, 0:Q], row[:, 4, 0:Q], -FAR, FAR, ALU.mult, ALU.add))
            done(dve.memset(row[:, 7, :], FAR))
            done(dve.tensor_tensor(row[:, 7, 1:Q], row[:, 8, 1:Q], row[:, 6, 0:Q - 1], ALU.add), "carry0")
            dve.wait_ge(m, M["back0"])
            done(dve.tensor_copy(carry[0:Q, 0, :], pt[0:Q, 1, 0:H]))
            scan(b, a, carry[:, 0, :], False)
            scan(a, b, FAR, True)
            done(dve.tensor_copy(ends[0:Q, 1, :], a[:, :, 0]), "ends1")
            dve.wait_ge(m, M["ends1"])
            done(dve.tensor_copy(row[:, 2, 0:Q], pt[0:H, 0, P:P + Q]))
            done(dve.memset(row[:, 5, :], 0.0))
            done(dve.tensor_tensor(row[:, 5, 0:Q - 1], row[:, 3, 0:Q - 1], row[:, 4, 1:Q], ALU.mult))
            done(dve.tensor_scalar(row[:, 5, 0:Q], row[:, 5, 0:Q], -FAR, FAR, ALU.mult, ALU.add))
            done(dve.tensor_tensor_scan(row[:, 6, 0:Q][:, ::-1], row[:, 5, 0:Q][:, ::-1], row[:, 2, 0:Q][:, ::-1], FAR, ALU.add, ALU.max))
            done(dve.memset(row[:, 7, :], FAR))
            done(dve.tensor_tensor(row[:, 7, 0:Q - 1], row[:, 8, 1:Q], row[:, 6, 1:Q], ALU.add), "carry1")
            dve.wait_ge(m, M["back1"])
            done(dve.tensor_copy(carry[0:Q, 1, :], pt[0:Q, 1, 0:H]))
            scan(a, b, carry[:, 1, :], True)
            V["max"] = n[0]
            for h in range(H):
                for g in range(2):
                    k = 2 * h + g
                    dve.wait_ge(m, M[f"out{k}"])
                    got = pt[:, 2 + k % 2, 0:4 * Q].rearrange("p (i q) -> p q i", i=4)
                    al = c.alpha[:, :, h].rearrange("p (q i) -> p q i", i=SQ)[:, :, 4 * g:4 * g + 4]
                    done(dve.tensor_tensor(al, al, got, ALU.subtract), f"out{k}")
            done(dve.tensor_scalar(c.alpha[:, :, :], c.alpha[:, :, :], 0.0, None, ALU.min), "cut")

        @block.tensor
        def _(pe):
            def mark(ins, name):
                ins.then_inc(m, 1)

            bank = 0
            for g in range(SQ // 4):
                for i in range(4):
                    ins = pe.transpose(pt[0:Q, bank, i * P:(i + 1) * P], c.key[:, 4 * g + i::SQ], c.ident[:, :])
                mark(ins, f"keys{g}")
                bank += 1
            for h, g in pieces:
                if bank >= 4:
                    pe.wait_ge(s, bank - 3)
                for i in range(4):
                    ins = pe.transpose(pt[0:Q, bank % 4, i * P:(i + 1) * P], c.alpha[:, 4 * g + i::SQ, h], c.ident[:, :])
                mark(ins, f"in{h}{g}")
                bank += 1
            pe.wait_ge(s, len(takes))
            pe.wait_ge(v, V["ends"])
            for w in (0, 2, 3):
                ins = pe.transpose(pt[0:H, 0, w * P:w * P + Q], ends[0:Q, w, :], c.ident[0:Q, 0:Q])
            mark(ins, "ends")
            pe.wait_ge(v, V["carry0"])
            mark(pe.transpose(pt[0:Q, 1, 0:H], row[:, 7, 0:Q], c.ident[0:H, 0:H]), "back0")
            pe.wait_ge(v, V["ends1"])
            mark(pe.transpose(pt[0:H, 0, P:P + Q], ends[0:Q, 1, :], c.ident[0:Q, 0:Q]), "ends1")
            pe.wait_ge(v, V["carry1"])
            mark(pe.transpose(pt[0:Q, 1, 0:H], row[:, 7, 0:Q], c.ident[0:H, 0:H]), "back1")
            pe.wait_ge(v, V["max"])
            for h in range(H):
                for g in range(2):
                    k = 2 * h + g
                    if k >= 2:
                        pe.wait_ge(v, V[f"out{k - 2}"])
                    for i in range(4):
                        ins = pe.transpose(pt[:, 2 + k % 2, i * Q:(i + 1) * Q],
                                           a[:, h, (4 * g + i) * P:(4 * g + i + 1) * P], c.ident[0:Q, 0:Q])
                    mark(ins, f"out{k}")

        @block.scalar
        def _(act):
            for n, name in enumerate(takes):
                act.wait_ge(m, M[name])
                src = pt[0:Q, n % 4, :]
                if name.startswith("keys"):
                    g = int(name[4:])
                    to = keys[0:Q, g * 512:(g + 1) * 512]
                else:
                    h, g = int(name[2]), int(name[3])
                    to = a[:, h, g * 512:(g + 1) * 512]
                act.activation(to, src, ACT.Copy).then_inc(s, 1)
            act.wait_ge(v, V["cut"])
            act.activation(c.alpha[:, :, :], c.alpha[:, :, :], ACT.Exp).then_inc(s, 1)


def stage_attention_sums(nc, c):
    with ExitStack() as ctx:
        sem = lambda n: c.semaphore("as_" + n)
        sb = lambda n, s, d: ctx.enter_context(nc.sbuf_tensor("as_" + n, s, d))
        acc = arena(c, ACC0, [NT, C_END])
        ring = sb("ring", [P, R, U, F], F32)
        hot, msg = sb("hot", [P, 2, U, P], F32), sb("msg", [P, 2, U, C_END], F32)
        slot, rec = sb("slot", [P, R, SU], I32), sb("rec", [P, R, SU, 2], F32)
        pa = ctx.enter_context(nc.psum_tensor("as_pa", [P, 2, U, 256], F32))
        arrived, scattered = [sem(f"arrived{r}") for r in range(R)], [sem(f"scattered{r}") for r in range(R)]
        hots, made, summed, added, packed, start, tick = (sem(n) for n in ("hots", "made", "summed", "added", "packed", "start", "tick"))
        block = ctx.enter_context(nc.Block())
        S_BATCHES = CHUNK // SU

        @block.gpsimd
        def _(pool):
            def step(k, i, r):
                at_least(pool, packed, 3 * (k + 1), tick)
                for u in range(SU):
                    pool.indirect_dma_start(c.records, bass.IndirectOffsetOnAxis(slot[:, r, u:u + 1], 0), rec[:, r, u, :], None,
                                            bounds_check=SLOTS - 1, oob_is_err=False).then_inc(scattered[r], 16)
            rounds(pool, S_BATCHES, R, step)
            for r in range(R):
                pool.wait_ge(scattered[r], 16 * SU * S_BATCHES // R)

        @block.scalar
        def _(act):
            def step(k, i, r):
                at_least(act, scattered[r], 16 * SU * i, tick)
                act.activation(slot[:, r, :], c.slot_of[:, bass.ds(k * SU, SU)], ACT.Copy).then_inc(packed, 1)
                act.activation(rec[:, r, :, 0], c.dst_f[:, bass.ds(k * SU, SU)], ACT.Copy).then_inc(packed, 1)
                act.activation(rec[:, r, :, 1], c.src_f[:, bass.ds(k * SU, SU)], ACT.Copy).then_inc(packed, 1)
            rounds(act, S_BATCHES, R, step)

        @block.sync
        def _(sp):
            def step(k, i, r):
                at_least(sp, made, 4 * (k - R + 1), tick)
                sp.dma_start(ring[:, r, :, :].rearrange("p u f -> p (u f)"), c.values[bass.ds(k, 1), :, :, :].rearrange("one p u f -> p (one u f)"))\
                    .then_inc(arrived[r], 16)
            rounds(sp, BATCHES, R, step)

        @block.tensor
        def _(pe):
            def step(k, i, r):
                q = r % 2
                at_least(pe, made, 4 * (k + 1), tick)
                at_least(pe, added, U * (k - 1), tick)
                if is_first(k):
                    pe.wait_ge(start, 2)
                for u in range(U):
                    ins = pe.matmul(pa[:, q, u, 0:C_END], hot[:, q, u, :], msg[:, q, u, :], start=True, stop=True)
                ins.then_inc(summed, 1)
            rounds(pe, BATCHES, R, step)

        @block.vector
        def _(dve):
            dve.memset(acc, 0.0).then_inc(start, 1)
            dve.memset(msg[:, :, :, C_CNT:C_END], 1.0).then_inc(start, 1)
            dve.wait_ge(start, 2)

            def make(k, i, r):
                q = r % 2
                at = bass.ds(k * U, U)
                ex = c.alpha[:, at, :]

                def one_hot():
                    at_least(dve, summed, k - 1, tick)
                    dve.tensor_tensor(hot[:, q, :, :], over(c.j[:, 0:P], U), wide(c.local_d[:, at], P), ALU.is_equal).then_inc(made, 1)

                def exps():
                    dve.tensor_copy(msg[:, q, :, C_EX:C_EW], ex).then_inc(made, 1)
                    dve.tensor_tensor(msg[:, q, :, C_EW:C_CNT], ex, wide(c.weight[:, at], H), ALU.mult).then_inc(made, 1)

                def messages():
                    at_least(dve, arrived[r], 16 * (i + 1), tick)
                    dve.tensor_tensor(msg[:, q, :, 0:F].rearrange("p u (h d) -> p u h d", d=D),
                                      ex.unsqueeze(3).broadcast_to([P, U, H, D]),
                                      ring[:, r, :, :].rearrange("p u (h d) -> p u h d", d=D), ALU.mult).then_inc(made, 1)
                return [one_hot, exps, messages]

            def adds(k, r):
                return Adds(nc, dve, acc, c.bucket_d, pa[:, r % 2, :, :], C_END, k, summed, added, tick)

            def step(k, i, r):
                between(None if isinstance(k, int) and k < 2 else adds(k - 2, (r - 2) % R), make(k, i, r))
            rounds(dve, BATCHES, R, step)
            for k in (BATCHES - 2, BATCHES - 1):
                between(adds(k, k % R), [])
            dve.wait_ge(added, BATCHES * U)


def stage_edges(nc, c, name, table, acc, buckets, gather, local, layer=None):
    with ExitStack() as ctx:
        sem = lambda n: c.semaphore(name + n)
        sb = lambda n, s, d=F32: ctx.enter_context(nc.sbuf_tensor(name + n, s, d))
        pb = lambda n, s: ctx.enter_context(nc.psum_tensor(name + n, s, F32))
        index, ring = sb("index", [P, R, U], I32), sb("ring", [P, R, U, F])
        hot = sb("hot", [P, R, U, P])
        width_a = F + 1 if layer is None else F
        pa = pb("pa", [P, 2, U, 256 if layer is None else F])
        arrived, attributes = [sem(f"arrived{r}") for r in range(R)], [sem(f"attributes{r}") for r in range(R)]
        rows_in = [sem(f"rows{r}") for r in range(R)]
        index_ready, hots, summed, added, start, tick = (sem(n) for n in ("index", "hots", "summed", "added", "start", "tick"))
        hots_t, copied, first, second, third, sent, ready = (sem(n) for n in ("hots_t", "copied", "first", "second", "third", "sent", "ready"))
        if layer:
            width = A1 if layer == 1 else A2
            attr = sb("attr", [width, R, U * P])
            msg = sb("msg", [P, 2, U, P])
            tmp = sb("tmp", [P, 2, U, P])
            ph = pb("ph", [P, 2, U, F])
        if layer == 1:
            hot_t, rows = sb("hot_t", [P, R, U, P], BF16), sb("rows", [P, R, U * P], BF16)
        if layer == 2:
            pt = pb("pt", [P, 2, U, P])
            soft = sb("soft", [P, 2, U, P])
            pos = sb("pos", [P, 2, U, P])
        attr_dram = {1: c.attr1, 2: c.attr2}.get(layer)
        freed = summed if layer is None else (first if layer == 1 else sent)
        hidden_lag, message_lag, total_lag, add_lag = {None: (0, 0, 0, 1), 1: (1, 2, 3, 4), 2: (2, 3, 3, 4)}[layer]
        peeled = 2 if layer else 1
        block = ctx.enter_context(nc.Block())

        def behind(k, i, r, n):
            if isinstance(k, int) and k < n:
                return None
            return k - n, i if r >= n else i - 1, (r - n) % R

        def in_steps(eng, parts):
            def step(k, i, r):
                for lag, part in parts:
                    at = behind(k, i, r, lag)
                    if at is not None:
                        part(*at)
            rounds(eng, BATCHES, R, step, peeled)
            for k in range(BATCHES, BATCHES + max(lag for lag, part in parts)):
                for lag, part in parts:
                    if k - lag < BATCHES:
                        part(k - lag, (k - lag) // R, (k - lag) % R)

        @block.gpsimd
        def _(pool):
            gather_rows(pool, c, table, index, ring, index_ready, arrived, [(freed, 1)], tick)

        if layer:
            @block.sync
            def _(sp):
                def step(k, i, r):
                    e0 = loaded_values(nc, c.edge0, k, SP_ENGINE, E - 1)
                    at_least(sp, ready, k - R + 1, tick)
                    if layer == 1:
                        at_least(sp, hots_t, k - R + 1, tick)
                        load_local_rows(sp, c, rows, k, r, rows_in)
                    for u in range(U):
                        sp.dma_start(attr[:, r, u * P:(u + 1) * P], attr_dram[:, bass.ds(e0[u], P)]).then_inc(attributes[r], 16)
                rounds(sp, BATCHES, R, step)

        @block.scalar
        def _(act):
            def next_index(k, i, r):
                take_index(act, gather, index, k, i, r, arrived, index_ready, tick)

            def softplus(k, i, r):
                q = r % 2
                x = pt[:, q, :, :]
                at_least(act, ready, k + 1, tick)
                at_least(act, second, k - 1, tick)
                act.activation(tmp[:, q, :, :], x, ACT.Abs, bias=c.w["mlp_b0"][:, 0:1]).then_inc(copied, 1)
                act.activation(pos[:, q, :, :], x, ACT.Relu, bias=c.w["mlp_b0"][:, 0:1]).then_inc(copied, 1)
                at_least(act, copied, 4 * k + 1, tick)
                act.activation(tmp[:, q, :, :], tmp[:, q, :, :], ACT.Exp, scale=-1.0).then_inc(copied, 1)
                at_least(act, copied, 4 * k + 3, tick)
                act.activation(tmp[:, q, :, :], tmp[:, q, :, :], ACT.Ln, bias=c.ones[:, 0:1]).then_inc(copied, 1)

            def relu(k, i, r):
                q = r % 2
                at_least(act, first, k + 1, tick)
                at_least(act, summed, k - 1, tick)
                act.activation(msg[:, q, :, :], tmp[:, q, :, :], ACT.Relu).then_inc(sent, 1)

            if layer == 2:
                act.preload_act_table_set("natural_log_exp_and_others")
            in_steps(act, [(0, next_index)] + {None: [], 1: [(2, relu)], 2: [(1, softplus)]}[layer])

        @block.tensor
        def _(pe):
            def turn(k, i, r):
                at_least(pe, attributes[r], 16 * U * (i + 1), tick)
                at_least(pe, copied, 4 * (k - 1), tick)
                pe.matmul(pt[:, r % 2, :, :].rearrange("p u f -> p (u f)"), c.w["mlp_w0"][:, :], attr[:, r, :], start=True, stop=True).then_inc(ready, 1)

            def hidden(k, i, r):
                q = r % 2
                if layer == 1:
                    which = loaded_values(nc, buckets, k, PE_ENGINE, NT - 1)
                    at_least(pe, hots_t, k + 1, tick)
                    at_least(pe, attributes[r], 16 * U * (i + 1), tick)
                    at_least(pe, first, k - 1, tick)
                    for u in range(U):
                        for n, part in enumerate(c.dst_parts):
                            pe.matmul(ph[:, q, u, :], hot_t[:, r, u, :], part[:, bass.ds(which[u], 1), :].rearrange("p one f -> p (one f)"),
                                      start=(n == 0), stop=False)
                        ins = pe.matmul(ph[:, q, u, :], attr[:, r, u * P:(u + 1) * P], c.w["w1e"][:, :], start=False, stop=True)
                    ins.then_inc(ready, 1)
                if layer == 2:
                    at_least(pe, second, k + 1, tick)
                    at_least(pe, sent, k - 1, tick)
                    for u in range(U):
                        pe.matmul(ph[:, q, u, :], c.ones_bf[:, :], c.b2_rows[:, :], start=True, stop=False)
                        ins = pe.matmul(ph[:, q, u, :], soft[:, q, u, :], c.w["mlp_w2"][:, :], start=False, stop=True)
                    ins.then_inc(third, 1)

            def total(k, i, r):
                q = r % 2
                if layer is None:
                    at_least(pe, arrived[r], 16 * U * (i + 1), tick)
                else:
                    at_least(pe, sent, k + 1, tick)
                at_least(pe, hots, (U if layer == 2 else 1) * (k + 1), tick)
                at_least(pe, added, U * (k - 1), tick)
                for u in range(U):
                    rhs = ring[:, r, u, :] if layer is None else msg[:, q, u, :]
                    ins = pe.matmul(pa[:, q, u, 0:F], hot[:, r, u, :], rhs, start=True, stop=True)
                    if layer is None:
                        ins = pe.matmul(pa[:, q, u, F:F + 1], hot[:, r, u, :], c.ones[:, 0:1], start=True, stop=True)
                ins.then_inc(summed, 1)

            in_steps(pe, ([(0, turn)] if layer == 2 else []) + ([(hidden_lag, hidden)] if layer else []) + [(total_lag, total)])

        @block.vector
        def _(dve):
            dve.memset(acc, 0.0).then_inc(start, 1)
            dve.wait_ge(start, 1)

            def one_hot(k, i, r):
                if layer == 2:
                    def tile_hot(u):
                        if u == 0:
                            at_least(dve, summed, k - R + 1, tick)
                        dve.tensor_scalar(hot[:, r, u, :], c.j[:, 0:P], local[:, bass.ds(k * U + u, 1)], c.cutoff[:, bass.ds(k * U + u, 1)],
                                          ALU.is_equal, ALU.mult).then_inc(hots, 1)
                    return [lambda u=u: tile_hot(u) for u in range(U)]

                def edges_hot():
                    at_least(dve, summed, k - R + 1, tick)
                    dve.tensor_tensor(hot[:, r, :, :], over(c.j[:, 0:P], U), wide(local[:, bass.ds(k * U, U)], P), ALU.is_equal).then_inc(hots, 1)
                return [edges_hot]

            def one_hot_turned(k, i, r):
                at_least(dve, rows_in[r], 16 * (i + 1), tick)
                at_least(dve, ready, k - R + 1, tick)
                dve.tensor_scalar(hot_t[:, r, :, :].rearrange("p u f -> p (u f)"), rows[:, r, :], c.part[:, 0:1], None, ALU.is_equal).then_inc(hots_t, 1)

            def message(k, i, r):
                q = r % 2
                if layer == 1:
                    at_least(dve, ready, k + 1, tick)
                    at_least(dve, arrived[r], 16 * U * (i + 1), tick)
                    at_least(dve, sent, k - 1, tick)
                    dve.tensor_tensor(tmp[:, q, :, :], ph[:, q, :, :], ring[:, r, :, :], ALU.add).then_inc(first, 1)
                if layer == 2:
                    at_least(dve, third, k + 1, tick)
                    at_least(dve, arrived[r], 16 * U * (i + 1), tick)
                    at_least(dve, summed, k - 1, tick)
                    dve.tensor_tensor(msg[:, q, :, :], ph[:, q, :, :], ring[:, r, :, :], ALU.mult).then_inc(sent, 1)

            def soften(k, i, r):
                q = r % 2
                at_least(dve, copied, 4 * (k + 1), tick)
                at_least(dve, third, k - 1, tick)
                dve.scalar_tensor_tensor(out=soft[:, q, :, :].rearrange("p u f -> p (u f)"), in0=pos[:, q, :, :].rearrange("p u f -> p (u f)"),
                                         scalar=-LOG2, in1=tmp[:, q, :, :].rearrange("p u f -> p (u f)"), op0=ALU.add, op1=ALU.add).then_inc(second, 1)

            def step(k, i, r):
                new = not (isinstance(k, int) and k >= BATCHES)
                there = lambda n: (not isinstance(k, int) or n <= k < BATCHES + n)
                steps = []
                if layer == 1 and new:
                    steps.append(lambda: one_hot_turned(k, i, r))
                if layer == 2 and there(2):
                    steps.append(lambda: soften(*behind(k, i, r, 2)))
                if layer and there(message_lag):
                    steps.append(lambda: message(*behind(k, i, r, message_lag)))
                if new:
                    steps += one_hot(k, i, r)
                adds = None
                if there(add_lag):
                    ka, ia, ra = behind(k, i, r, add_lag)
                    adds = Adds(nc, dve, acc, buckets, pa[:, ra % 2, :, :], width_a, ka, summed, added, tick)
                between(adds, steps)
            rounds(dve, BATCHES, R, step, peeled)
            for k in range(BATCHES, BATCHES + add_lag):
                step(k, k // R, k % R)
            dve.wait_ge(added, BATCHES * U)


def load_weights(nc, c, ctx, t, name, natural=(), rows=(), wide_rows=()):
    loaded = c.semaphore(name + "_weights")
    loads = []
    for group, how in ((natural, 0), (rows, 0), (wide_rows, 1)):
        for attr, src in group:
            src = t[src] if isinstance(src, str) else src
            tile = ctx.enter_context(nc.sbuf_tensor(name + "_" + attr, [P, src.shape[1]] if how else list(src.shape), F32))
            c.w[attr] = tile
            loads.append((tile[:, :], src.broadcast_to([P, src.shape[1]]) if how else src))
    with ExitStack() as inner:
        block = inner.enter_context(nc.Block())

        @block.sync
        def _(sp):
            for to, src in loads:
                sp.dma_start(to, src).then_inc(loaded, 16)
            sp.wait_ge(loaded, 16 * len(loads))


def tile_rows(table, k, a=0, b=None):
    return table[bass.ds(k, 1), :, a:b if b else table.shape[2]].rearrange("one p f -> p (one f)")


def at_tile(whole, k, a=0, b=None):
    return whole[:, bass.ds(k, 1), a:b if b else whole.shape[2]].rearrange("p one f -> p (one f)")


def attention_layer(nc, c, t, small):
    with ExitStack() as ctx:
        load_weights(nc, c, ctx, t, "l0", natural=[(n, "L0_" + n) for n in ("wq", "wk", "wv", "wskip", "wo")],
                     rows=[("bias4", "L0_bias4"), ("bo", "L0_bo")],
                     wide_rows=[(n, "L0_" + n) for n in ("we", "gamma", "beta")])
        q_full = arena(c, 3 * NT * QW // 2, [NT, QW])
        by_we = arena(c, 3 * NT * QW // 2 + NT * QW, [NT, F])
        c.alpha = arena(c, B2_0, [TILES, H])
        c.query_parts = [arena(c, n * NT * QW // 2, [NT, QW], BF16) for n in range(3)]

        def keep(k):
            return [(tile_rows(c.kv3, k), 0, 2 * F), (tile_rows(c.skip, k), 2 * F, 3 * F)]

        sweep(nc, c, "qkv", [(lambda k: at_tile(c.x, k), P)],
              [(None, c.w["bias4"][:, :], 0, 4 * F)] + [(0, w[:, :], n * F, (n + 1) * F) for n, w in enumerate((c.w["wq"], c.w["wk"], c.w["wv"], c.w["wskip"]))],
              vector=lambda e, k, po: e.tensor_scalar(at_tile(q_full, k, 0, F), po[:, 0:F], 1.0 / D ** 0.5, None, ALU.mult),
              scalar=lambda e, k, po, ring: e.activation(ring[:, :], po[:, F:4 * F], ACT.Copy), store=keep)
        vector_scalar_stage(nc, c, "query", [
            ("v", lambda e: e.tensor_tensor(by_we, q_full[:, :, 0:F], over(c.w["we"][:, :], NT), ALU.mult)),
            ("v", lambda e: e.tensor_reduce(q_full[:, :, F:QW], by_we.rearrange("p t (h d) -> p t h d", d=D), AX_X, ALU.add)),
        ] + split_steps(q_full, c.query_parts))
        stage_attention_scores(nc, c)
        stage_attention_max(nc, c)
        stage_attention_sums(nc, c)
        load_whole(nc, c, arena(c, B2_0, [NT, F]), c.skip, "skip")

        acc, heads, y = arena(c, ACC0, [NT, C_END]), arena(c, B1_0, [NT, F]), arena(c, B2_0, [NT, F])
        by_head = heads.rearrange("p t (h d) -> p t h d", d=D)
        den = acc[:, :, C_EX:C_EW]
        spread = lambda a: a.unsqueeze(3).broadcast_to([P, NT, H, D])
        vector_scalar_stage(nc, c, "heads", [
            ("v", lambda e: e.tensor_copy(c.count[:, :], acc[:, :, C_CNT])),
            ("v", lambda e: e.tensor_scalar(den, den, 1e-16, None, ALU.max)),
            ("v", lambda e: e.reciprocal(den, den)),
            ("v", lambda e: e.tensor_copy(by_head, spread(acc[:, :, C_EW:C_CNT]))),
            ("v", lambda e: e.tensor_tensor(heads, heads, over(c.w["we"][:, :], NT), ALU.mult)),
            ("v", lambda e: e.tensor_tensor(heads, heads, acc[:, :, 0:F], ALU.add)),
            ("v", lambda e: e.tensor_tensor(by_head, by_head, spread(den), ALU.mult)),
            ("v", lambda e: e.tensor_tensor(heads, heads, y, ALU.add)),
        ])
        sweep(nc, c, "wo", [(lambda k: at_tile(heads, k), P)], [(None, c.w["bo"][:, :], 0, F), (0, c.w["wo"][:, :], 0, F)],
              vector=lambda e, k, po: e.tensor_tensor(at_tile(y, k), po[:, 0:F], at_tile(c.x, k), ALU.add))
        vector_scalar_stage(nc, c, "norm0", norm_steps(c, y, heads, small, c.w["gamma"][:, :], c.w["beta"][:, :], c.x[:, :, :])
                            + norm_steps(c, y, heads, small, out=c.x[:, :, :]))


def load_whole(nc, c, to, table, name):
    with ExitStack() as ctx:
        loaded = c.semaphore(name + "_loaded")
        block = ctx.enter_context(nc.Block())

        @block.sync
        def _(sp):
            sp.dma_start(to, table.rearrange("t p f -> p t f")).then_inc(loaded, 16)
            sp.wait_ge(loaded, 16)


def edge_mlp_layer(nc, c, t, small):
    with ExitStack() as ctx:
        load_weights(nc, c, ctx, t, "l1", natural=[(n, "L1_" + n) for n in ("w1s", "w1d", "w1e", "w2", "b2_col", "wu")],
                     rows=[("b1", "L1_b1"), ("bu", "L1_bu")], wide_rows=[("gamma", "L1_gamma"), ("beta", "L1_beta")])
        acc, full, mid, y = arena(c, ACC0, [NT, F]), arena(c, ACC0, [NT, F]), arena(c, B1_0, [NT, F]), arena(c, B2_0, [NT, F])
        c.dst_parts = [arena(c, B1_0 + n * NT * F // 2, [NT, F], BF16) for n in range(3)]
        w_both = ctx.enter_context(nc.sbuf_tensor("l1_both", [P, F], F32))
        b_both = ctx.enter_context(nc.sbuf_tensor("l1_b_both", [P, F], F32))
        b_row = ctx.enter_context(nc.sbuf_tensor("l1_b_row", [1, F], F32))
        sweep(nc, c, "l1in", [(lambda k: at_tile(c.x, k), P)],
              [(0, c.w["w1s"][:, :], 0, F), (0, c.w["w1d"][:, :], F, 2 * F), (None, c.w["b1"][:, :], F, 2 * F)],
              vector=lambda e, k, po: e.tensor_copy(at_tile(full, k), po[:, F:2 * F]),
              scalar=lambda e, k, po, ring: e.activation(ring[:, 0:F], po[:, 0:F], ACT.Copy),
              store=lambda k: [(tile_rows(c.table3, k), 0, F)])
        vector_scalar_stage(nc, c, "split1", split_steps(full, c.dst_parts))
        with ExitStack() as inner:
            made = c.semaphore("l1_made")
            took = c.semaphore("l1_took")
            pw = inner.enter_context(nc.psum_tensor("l1_pw", [P, 512], F32))
            block = inner.enter_context(nc.Block())

            @block.tensor
            def _(pe):
                pe.matmul(pw[:, 0:F], c.w["w2"][:, :], c.w["wu"][:, :], start=True, stop=True).then_inc(made, 1)
                pe.matmul(pw[:, F:2 * F], c.w["b2_col"][:, 0:1].broadcast_to([P, P]), c.w["wu"][:, :], start=True, stop=True).then_inc(made, 1)

            @block.vector
            def _(dve):
                dve.wait_ge(made, 2)
                dve.tensor_copy(w_both[:, :], pw[:, 0:F]).then_inc(took, 1)
                dve.tensor_copy(b_both[:, :], pw[:, F:2 * F]).then_inc(took, 1)
        stage_edges(nc, c, "e1_", c.table, acc, c.bucket_d, c.gather_d, c.local_d, layer=1)
        sweep(nc, c, "l1out", [(lambda k: at_tile(acc, k), P)], [(None, c.w["bu"][:, :], 0, F), (0, w_both[:, :], 0, F)],
              vector=lambda e, k, po: e.scalar_tensor_tensor(out=at_tile(mid, k), in0=b_both[:, :], scalar=c.count[:, bass.ds(k, 1)],
                                                             in1=po[:, 0:F], op0=ALU.mult, op1=ALU.add))
        vector_scalar_stage(nc, c, "norm1", [
            ("s", lambda e: e.activation(y, mid, ACT.Relu)),
            ("v", lambda e: e.tensor_tensor(y, y, c.x[:, :, :], ALU.add)),
        ] + norm_steps(c, y, mid, small, c.w["gamma"][:, :], c.w["beta"][:, :], c.x[:, :, :]) + norm_steps(c, y, mid, small, out=c.x[:, :, :]))


def bias_parts(nc, c, ctx):
    rest = ctx.enter_context(nc.sbuf_tensor("l2_rest", [P, F], F32))
    parts = ctx.enter_context(nc.sbuf_tensor("l2_b2_parts", [P, 3, F], BF16))
    c.b2_rows = ctx.enter_context(nc.sbuf_tensor("l2_b2_rows", [65, F], BF16))
    c.ones_bf = ctx.enter_context(nc.sbuf_tensor("l2_ones", [65, P], BF16))
    vector_scalar_stage(nc, c, "bias2", [
        ("v", lambda e: e.memset(c.ones_bf[:, :], 1.0)),
        ("v", lambda e: e.memset(c.b2_rows[:, :], 0.0)),
        ("v", lambda e: e.tensor_copy(rest[:, :], c.w["mlp_b2"][:, :])),
    ] + split_steps(rest[:, :], [parts[:, n, :] for n in range(3)])
      + [("v", lambda e, n=n: e.tensor_copy(c.b2_rows[32 * n:32 * n + 1, :], parts[32 * n:32 * n + 1, n, :])) for n in range(3)])


def filter_layer(nc, c, t, small):
    with ExitStack() as ctx:
        load_weights(nc, c, ctx, t, "l2", natural=[(n, "L2_" + n) for n in ("mlp_w0", "mlp_b0", "mlp_w2", "lin1", "lin2", "lin")],
                     wide_rows=[("mlp_b2", "L2_mlp_b2")], rows=[("lin2_b", "L2_lin2_b"), ("lin_b", "L2_lin_b")])
        acc, h1, z = arena(c, ACC0, [NT, F]), arena(c, B1_0, [NT, F]), arena(c, B2_0, [NT, F])
        sweep(nc, c, "l2in", [(lambda k: at_tile(c.x, k), P)], [(0, c.w["lin1"][:, :], 0, F)],
              vector=lambda e, k, po: e.tensor_copy(at_tile(h1, k), po[:, 0:F]),
              scalar=lambda e, k, po, ring: e.activation(ring[:, 0:F], po[:, 0:F], ACT.Copy),
              store=lambda k: [(tile_rows(c.table3, k), 0, F)])
        bias_parts(nc, c, ctx)
        stage_edges(nc, c, "e2_", c.table, acc, c.bucket_d, c.gather_d, c.local_d, layer=2)
        vector_scalar_stage(nc, c, "l2sum", [("v", lambda e: e.tensor_tensor(h1, h1, acc, ALU.add))])
        sweep(nc, c, "l2mid", [(lambda k: at_tile(h1, k), P)], [(None, c.w["lin2_b"][:, :], 0, F), (0, c.w["lin2"][:, :], 0, F)],
              vector=lambda e, k, po: e.tensor_copy(at_tile(z, k), po[:, 0:F]))
        vector_scalar_stage(nc, c, "l2soft", [
            ("s", lambda e: e.activation(h1, z, ACT.Abs)),
            ("s", lambda e: e.activation(h1, h1, ACT.Exp, scale=-1.0)),
            ("s", lambda e: e.activation(h1, h1, ACT.Ln, bias=c.ones[:, 0:1])),
            ("s", lambda e: e.activation(z, z, ACT.Relu)),
            ("v", lambda e: e.scalar_tensor_tensor(out=h1, in0=z, scalar=-LOG2, in1=h1, op0=ALU.add, op1=ALU.add)),
        ])
        sweep(nc, c, "l2out", [(lambda k: at_tile(h1, k), P)], [(None, c.w["lin_b"][:, :], 0, F), (0, c.w["lin"][:, :], 0, F)],
              vector=lambda e, k, po: e.tensor_tensor(at_tile(z, k), po[:, 0:F], at_tile(c.x, k), ALU.add))
        vector_scalar_stage(nc, c, "norm2", norm_steps(c, z, h1, small, out=c.x[:, :, :]))


def stage_records(nc, c, gather_s, local_s):
    with ExitStack() as ctx:
        sem = lambda n: c.semaphore("re_" + n)
        loaded, stored, turned, took = sem("loaded"), sem("stored"), sem("turned"), sem("took")
        rec = arena(c, ACC0, [JC, 2 * P])
        ps = ctx.enter_context(nc.psum_tensor("re_ps", [P, 2, 2, 512], F32))
        full = TILES // P
        rest = TILES - full * P
        slots = c.records.rearrange("(j p) two -> j (p two)", p=P)
        block = ctx.enter_context(nc.Block())

        @block.sync
        def _(sp):
            sp.dma_start(c.table3.rearrange("t p f -> p t f"), c.x[:, :, :]).then_inc(stored, 16)
            sp.dma_start(rec[:, 0:full, :], slots[0:full * P, :].rearrange("(k j) f -> j k f", j=P)).then_inc(loaded, 16)
            sp.dma_start(rec[0:rest, full, :], slots[full * P:TILES, :]).then_inc(loaded, 16)
            sp.wait_ge(stored, 16)

        @block.tensor
        def _(pe):
            pe.wait_ge(loaded, 32)
            for f in range(2):
                for k in range(JC):
                    q = min(P, TILES - k * P)
                    ins = pe.transpose(ps[:, f, k // 4, k % 4 * P:k % 4 * P + q], rec[0:q, k, f::2], c.ident[0:q, 0:q])
            ins.then_inc(turned, 1)

        @block.vector
        def _(dve):
            dve.wait_ge(turned, 1)
            for h, (a, b) in enumerate(((0, 512), (512, TILES))):
                dve.tensor_scalar(gather_s[:, a:b], ps[:, 0, h, 0:b - a], float(N - 1), None, ALU.min).then_inc(took, 1)
                dve.tensor_tensor(local_s[:, a:b], ps[:, 1, h, 0:b - a], c.window_s[:, a:b], ALU.subtract).then_inc(took, 1)


def gated_layer(nc, c, t, small, out):
    with ExitStack() as ctx:
        load_weights(nc, c, ctx, t, "l3", natural=[(n, "L3_" + n) for n in ("w_in", "w_out", "wih1", "wih2", "whh", "b_in_col", "b_out_col")],
                     rows=[("b_ih", "L3_b_ih"), ("b_hh", "L3_b_hh")])
        with ExitStack() as edges:
            gather_s = edges.enter_context(nc.sbuf_tensor("gather_s", [P, TILES], F32))
            local_s = edges.enter_context(nc.sbuf_tensor("local_s", [P, TILES], F32))
            fwd, rev = arena(c, ACC0, [NT, F + 1]), arena(c, B1_0, [NT, F + 1])
            stage_records(nc, c, gather_s, local_s)
            stage_edges(nc, c, "e3_", c.table, fwd, c.bucket_d, c.gather_d, c.local_d)
            stage_edges(nc, c, "e4_", c.table, rev, c.bucket_s, gather_s, local_s)
        p_in = ctx.enter_context(nc.sbuf_tensor("l3_p_in", [P, 3 * F], F32))
        p_out = ctx.enter_context(nc.sbuf_tensor("l3_p_out", [P, 3 * F], F32))
        bias = [ctx.enter_context(nc.sbuf_tensor(f"l3_bias{n}", [1, 4 * F], F32)) for n in range(3)]
        seen = ctx.enter_context(nc.sbuf_tensor("l3_seen", [P, NT, 2], F32))
        with ExitStack() as inner:
            made = c.semaphore("l3_made")
            took = c.semaphore("l3_took")
            pw = inner.enter_context(nc.psum_tensor("l3_pw", [P, 4, 512], F32))
            block = inner.enter_context(nc.Block())

            @block.tensor
            def _(pe):
                pe.matmul(pw[:, 0, 0:3 * F], c.w["w_in"][:, :], c.w["wih1"][:, :], start=True, stop=True).then_inc(made, 1)
                pe.matmul(pw[:, 1, 0:3 * F], c.w["w_out"][:, :], c.w["wih2"][:, :], start=True, stop=True).then_inc(made, 1)
                pe.matmul(pw[0:1, 2, 0:3 * F], c.w["b_in_col"][:, :], c.w["wih1"][:, :], start=True, stop=True).then_inc(made, 1)
                pe.matmul(pw[0:1, 3, 0:3 * F], c.w["b_out_col"][:, :], c.w["wih2"][:, :], start=True, stop=True).then_inc(made, 1)

            @block.vector
            def _(dve):
                n = [0]

                def done(ins):
                    n[0] += 1
                    ins.then_inc(took, 1)
                    dve.wait_ge(took, n[0])
                dve.wait_ge(made, 4)
                done(dve.tensor_copy(p_in[:, :], pw[:, 0, 0:3 * F]))
                done(dve.tensor_copy(p_out[:, :], pw[:, 1, 0:3 * F]))
                for b, bank in ((0, 2), (1, 3)):
                    done(dve.memset(bias[b][:, :], 0.0))
                    done(dve.tensor_copy(bias[b][:, 0:3 * F], pw[0:1, bank, 0:3 * F]))
                done(dve.tensor_tensor(bias[2][:, 0:2 * F], c.w["b_ih"][:, 0:2 * F], c.w["b_hh"][:, 0:2 * F], ALU.add))
                done(dve.tensor_copy(bias[2][:, 2 * F:3 * F], c.w["b_ih"][:, 2 * F:3 * F]))
                done(dve.tensor_copy(bias[2][:, 3 * F:4 * F], c.w["b_hh"][:, 2 * F:3 * F]))
                for n_, acc in enumerate((fwd, rev)):
                    count = acc[:, :, F]
                    done(dve.tensor_scalar(seen[:, :, n_], count, 1.0, None, ALU.min))
                    done(dve.tensor_scalar(count, count, 1.0, None, ALU.max))
                    done(dve.reciprocal(count, count))
                    done(dve.tensor_tensor(acc[:, :, 0:F], acc[:, :, 0:F], wide(count, F), ALU.mult))
        y = arena(c, B2_0, [NT, F])
        stage_gates(nc, c, fwd, rev, seen, p_in, p_out, bias, y)
        squares = arena(c, B1_0, [NT, F])
        vector_scalar_stage(nc, c, "norm3", norm_steps(c, y, squares, small))
        with ExitStack() as last:
            stored = c.semaphore("stored")
            block = last.enter_context(nc.Block())
            whole = N // P * P

            @block.sync
            def _(sp):
                sp.dma_start(out[0:whole, :].rearrange("(t p) f -> p t f", p=P), y[:, 0:N // P, :]).then_inc(stored, 16)
                sp.dma_start(out[whole:N, :], y[0:N - whole, N // P, :]).then_inc(stored, 16)
                sp.wait_ge(stored, 32)


def stage_gates(nc, c, fwd, rev, seen, p_in, p_out, bias, y):
    with ExitStack() as ctx:
        sem = lambda n: c.semaphore("ga_" + n)
        turned, copied, multiplied, squashed, vec, tick = (sem(n) for n in ("turned", "copied", "multiplied", "squashed", "vec", "tick"))
        xt = ctx.enter_context(nc.sbuf_tensor("ga_xt", [P, 2, 3, P], F32))
        st = ctx.enter_context(nc.sbuf_tensor("ga_st", [1, 2, 2, P], F32))
        gates = ctx.enter_context(nc.sbuf_tensor("ga_gates", [P, 2, 2 * F], F32))
        new = ctx.enter_context(nc.sbuf_tensor("ga_new", [P, 2, F], F32))
        pt = ctx.enter_context(nc.psum_tensor("ga_pt", [P, 2, 512], F32))
        ps = ctx.enter_context(nc.psum_tensor("ga_ps", [P, 2, 512], F32))
        po = ctx.enter_context(nc.psum_tensor("ga_po", [P, 2, 512], F32))
        VEC = 5
        staged = sem("staged")
        fixed = ctx.enter_context(nc.sbuf_tensor("ga_fixed", [P, 2, 3, P], F32))
        flags = ctx.enter_context(nc.sbuf_tensor("ga_flags", [P, 2, 2], F32))
        block = ctx.enter_context(nc.Block())

        @block.gpsimd
        def _(pool):
            def step(k, i, q):
                at_least(pool, turned, k - 1, tick)
                for n, src in enumerate((at_tile(fwd, k, 0, F), at_tile(rev, k, 0, F), at_tile(c.x, k))):
                    pool.tensor_copy(fixed[:, q, n, :], src).then_inc(staged, 1)
                pool.tensor_copy(flags[:, q, :], at_tile(seen, k)).then_inc(staged, 1)
            rounds(pool, NT, 2, step)

        @block.tensor
        def _(pe):
            def turn(k, q):
                at_least(pe, staged, 4 * (k + 1), tick)
                at_least(pe, copied, 3 * (k - 1), tick)
                for n in range(3):
                    pe.transpose(pt[:, q, n * P:(n + 1) * P], fixed[:, q, n, :], c.ident[:, :])
                for n in range(2):
                    ins = pe.transpose(ps[0:1, q, n * P:(n + 1) * P], flags[:, q, n:n + 1], c.ident[:, :])
                ins.then_inc(turned, 1)

            def multiply(k, q):
                at_least(pe, copied, 3 * (k + 1), tick)
                at_least(pe, vec, VEC * (k - 1), tick)
                b = po[:, q, :]
                pe.matmul(b, c.ones[0:1, :], bias[2][:, :], start=True, stop=False)
                pe.matmul(b, st[:, q, 0, :], bias[0][:, :], start=False, stop=False)
                pe.matmul(b, st[:, q, 1, :], bias[1][:, :], start=False, stop=False)
                pe.matmul(b[:, 0:3 * F], xt[:, q, 0, :], p_in[:, :], start=False, stop=False)
                pe.matmul(b[:, 0:3 * F], xt[:, q, 1, :], p_out[:, :], start=False, stop=False)
                pe.matmul(b[:, 0:2 * F], xt[:, q, 2, :], c.w["whh"][:, 0:2 * F], start=False, stop=False)
                pe.matmul(b[:, 3 * F:4 * F], xt[:, q, 2, :], c.w["whh"][:, 2 * F:3 * F], start=False, stop=True).then_inc(multiplied, 1)

            def step(k, i, q):
                turn(k, q)
                if not is_first(k):
                    multiply(k - 1, 1 - q)
            rounds(pe, NT, 2, step)
            multiply(NT - 1, 1)

        @block.scalar
        def _(act):
            def copy(k, q):
                at_least(act, turned, k + 1, tick)
                at_least(act, multiplied, k - 1, tick)
                act.activation(xt[:, q, :, :], pt[:, q, 0:3 * P].rearrange("p (n m) -> p n m", m=P), ACT.Copy).then_inc(copied, 1)
                for n in range(2):
                    act.activation(st[:, q, n, :], ps[0:1, q, n * P:(n + 1) * P], ACT.Copy).then_inc(copied, 1)

            def squash(k, q):
                at_least(act, multiplied, k + 1, tick)
                at_least(act, vec, VEC * (k - 1), tick)
                act.activation(gates[:, q, :], po[:, q, 0:2 * F], ACT.Sigmoid).then_inc(squashed, 1)
                at_least(act, vec, VEC * k + 2, tick)
                act.activation(new[:, q, :], new[:, q, :], ACT.Tanh).then_inc(squashed, 1)

            def step(k, i, q):
                copy(k, q)
                if not is_first(k):
                    squash(k - 1, 1 - q)
            rounds(act, NT, 2, step)
            squash(NT - 1, 1)

        @block.vector
        def _(dve):
            def step(k, i, q):
                n, x, to = new[:, q, :], at_tile(c.x, k), at_tile(y, k)
                r, z = gates[:, q, 0:F], gates[:, q, F:2 * F]
                at_least(dve, squashed, 2 * k + 1, tick)
                dve.tensor_tensor(n, r, po[:, q, 3 * F:4 * F], ALU.mult).then_inc(vec, 1)
                at_least(dve, vec, VEC * k + 1, tick)
                dve.tensor_tensor(n, n, po[:, q, 2 * F:3 * F], ALU.add).then_inc(vec, 1)
                at_least(dve, squashed, 2 * k + 2, tick)
                dve.tensor_tensor(to, x, n, ALU.subtract).then_inc(vec, 1)
                at_least(dve, vec, VEC * k + 3, tick)
                dve.tensor_tensor(to, to, z, ALU.mult).then_inc(vec, 1)
                at_least(dve, vec, VEC * k + 4, tick)
                dve.tensor_tensor(to, to, n, ALU.add).then_inc(vec, 1)
            rounds(dve, NT, 2, step)
            dve.wait_ge(vec, VEC * NT)
            dve.tensor_tensor(y, y, c.x[:, :, :], ALU.add).then_inc(vec, 1)


def gnn_kernel(nc, t, out):
    c = Core(nc)
    scratch = lambda name, shape: nc.dram_tensor(name, shape, F32, kind="Internal").ap()
    c.records = scratch("records", (SLOTS, 2))
    c.kv3 = scratch("keys_values", (NT, P, 2 * F))
    c.kv = c.kv3.rearrange("t p f -> (t p) f")
    c.local_rows = nc.dram_tensor("local_rows", (TILES, P), BF16, kind="Internal").ap()
    c.skip = scratch("skip", (NT, P, F))
    c.values = scratch("edge_values", (BATCHES, P, U, F))
    c.table3 = scratch("table", (NT, P, F))
    c.table = c.table3.rearrange("t p f -> (t p) f")
    c.attr1, c.attr2 = t["edge_attr_32"], t["edge_attr_50"]
    with ExitStack() as ctx:
        sb = lambda ctx, name, shape, dt=F32: ctx.enter_context(nc.sbuf_tensor(name, shape, dt))
        c.arena = sb(ctx, "arena", [P, ARENA])
        c.x = sb(ctx, "nodes", [P, NT, F])
        c.ident, c.ones = sb(ctx, "ident", [P, P]), sb(ctx, "ones", [P, P])
        c.j, c.part, c.bounds = sb(ctx, "j", [P, TILES]), sb(ctx, "part", [P, 1]), sb(ctx, "bounds", [P, NB])
        c.gather_d, c.local_d, c.weight, c.cutoff = (sb(ctx, n, [P, TILES]) for n in ("gather_d", "local_d", "weight", "cutoff"))
        c.window_s = sb(ctx, "window_s", [P, TILES], BF16)
        c.count = sb(ctx, "count", [P, NT])
        small = sb(ctx, "small", [P, 2, NT])
        ints = sb(ctx, "ints", [P, TILES], I32)
        c.bucket_d, c.edge0, c.bucket_s = ints[0:1, :], ints[32:33, :], ints[64:65, :]
        with ExitStack() as early:
            c.key = sb(early, "key", [P, TILES])
            c.src_f, c.dst_f, c.src_bucket, c.slot_of = (sb(early, n, [P, CHUNK]) for n in ("src_f", "dst_f", "src_bucket", "slot_of"))
            c.base = sb(early, "base", [P, NB])
            with ExitStack() as first:
                c.before, c.previous = sb(first, "before", [P, P]), sb(first, "previous", [P, P])
                c.src_i, c.dst_i = arena(c, ACC0 + 2048, [CHUNK], I32), arena(c, ACC0 + 2048 + CHUNK, [CHUNK], I32)
                stage_setup(nc, c, t)
                stage_lists(nc, c, t)
            attention_layer(nc, c, t, small)
        c.clear_semaphores()
        edge_mlp_layer(nc, c, t, small)
        c.clear_semaphores()
        filter_layer(nc, c, t, small)
        c.clear_semaphores()
        gated_layer(nc, c, t, small, out)


def kernel(**inputs):
    import numpy as np
    import concourse.bacc as bacc
    from concourse.bass_utils import run_bass_kernel_spmd as run

    g = {name: np.asarray(a) for name, a in inputs.items()}
    row = lambda name: g[name].reshape(1, -1)
    heads = lambda name: g[name].transpose(1, 0, 2).reshape(F, H * D)
    pad = EP - E
    at = {
        "x": g["x"],
        "src": np.concatenate([g["src"], np.full(pad, NOWHERE, g["src"].dtype)]),
        "dst": np.concatenate([g["dst"], np.full(pad, NOWHERE, g["dst"].dtype)]),
        "edge_weight": np.concatenate([g["edge_weight"], np.zeros(pad, np.float32)]),
        "edge_attr_32": np.pad(g["edge_attr_32"].T, ((0, 0), (0, pad))),
        "edge_attr_50": np.pad(g["edge_attr_50"].T, ((0, 0), (0, pad))),
        "L0_wq": heads("L0_gnn_Wq"), "L0_wk": heads("L0_gnn_Wk"), "L0_wv": heads("L0_gnn_Wv"), "L0_wskip": heads("L0_gnn_Wskip"),
        "L0_bias4": np.concatenate([row("L0_gnn_bq"), row("L0_gnn_bk"), row("L0_gnn_bv"), row("L0_gnn_bskip")], axis=1),
        "L0_we": row("L0_gnn_We"), "L0_wo": g["L0_gnn_Wo"], "L0_bo": row("L0_gnn_bo"),
        "L0_gamma": row("L0_gnn_gamma"), "L0_beta": row("L0_gnn_beta"),
        "L1_w1s": g["L1_gnn_W1"][:, 0:F].T, "L1_w1d": g["L1_gnn_W1"][:, F:2 * F].T, "L1_w1e": g["L1_gnn_W1"][:, 2 * F:].T,
        "L1_w2": g["L1_gnn_W2"], "L1_b2_col": g["L1_gnn_b2"].reshape(F, 1), "L1_wu": g["L1_gnn_Wu"].T,
        "L1_b1": row("L1_gnn_b1"), "L1_bu": row("L1_gnn_bu"), "L1_gamma": row("L1_gnn_gamma"), "L1_beta": row("L1_gnn_beta"),
        "L2_mlp_w0": g["L2_gnn_mlp_w0"].T, "L2_mlp_b0": g["L2_gnn_mlp_b0"].reshape(F, 1), "L2_mlp_w2": g["L2_gnn_mlp_w2"].T,
        "L2_mlp_b2": row("L2_gnn_mlp_b2"), "L2_lin1": g["L2_gnn_lin1_w"].T, "L2_lin2": g["L2_gnn_lin2_w"].T,
        "L2_lin2_b": row("L2_gnn_lin2_b"), "L2_lin": g["L2_gnn_lin_w"].T, "L2_lin_b": row("L2_gnn_lin_b"),
        "L3_w_in": g["L3_gnn_W_in"], "L3_w_out": g["L3_gnn_W_out"], "L3_b_in_col": g["L3_gnn_b_in"].reshape(F, 1),
        "L3_b_out_col": g["L3_gnn_b_out"].reshape(F, 1), "L3_wih1": g["L3_gnn_w_ih"][:, 0:F].T, "L3_wih2": g["L3_gnn_w_ih"][:, F:2 * F].T,
        "L3_whh": g["L3_gnn_w_hh"].T, "L3_b_ih": row("L3_gnn_b_ih"), "L3_b_hh": row("L3_gnn_b_hh"),
    }
    nc = bacc.Bacc("TRN2", target_bir_lowering=False, num_devices=1)
    arrays, t = {}, {}
    for name, a in at.items():
        a = np.ascontiguousarray(a)
        arrays[name] = a
        t[name] = nc.dram_tensor(name, a.shape, mybir.dt.from_np(a.dtype), kind="ExternalInput").ap()
    out = nc.dram_tensor("out", (N, F), F32, kind="ExternalOutput").ap()
    gnn_kernel(nc, t, out)
    return run(nc, [arrays], core_ids=[0]).results[0]["out"]
```

```python
from contextlib import ExitStack

import concourse.bass as bass
from concourse import mybir

F32 = mybir.dt.float32
I32 = mybir.dt.int32
BF16 = mybir.dt.bfloat16
ALU = mybir.AluOpType
ACT = mybir.ActivationFunctionType
AX_X = mybir.AxisListType.X
PE_ENGINE = mybir.EngineType.PE
DVE_ENGINE = mybir.EngineType.DVE
SP_ENGINE = mybir.EngineType.SP

P = 128
N = 6250
E = 106250
F = 128
H = 8
D = F // H
A1, A2 = 32, 50
NB = -(-N // P)
NT = NB + 1
U = 4
R = 4
TILES = -(-(E // P + NB) // (U * R)) * U * R
BATCHES = TILES // U
SLOTS = TILES * P
CHUNK = -(-(E + P) // P)
EP = CHUNK * P
NOWHERE = 1 << 20
REV = F + 2
PIECE = 10
G = 4
JC = -(-TILES // P)
SQ = 8
SP_PARTS = TILES // SQ
SL = SQ * P
FAR = -1.0e30
LN_EPS = 1e-5
LOG2 = 0.6931471805599453
assert R == 4 and U == 4 and TILES % SQ == 0 and NB <= BATCHES // R - 1

C_EX, C_EW, C_CNT, C_END = F, F + H, F + 2 * H, F + 2 * H + 1
QW = F + H

BIASES, BIAS_N = {}, 0
for _name, _width in (("L0_bias4", 4 * F), ("L0_bo", F), ("L1_b1", F), ("L1_bu", F), ("L2_mlp_b2", F), ("L2_lin2_b", F), ("L2_lin_b", F)):
    BIASES[_name] = (BIAS_N, BIAS_N + _width)
    BIAS_N += _width

ACC0, ACC_N = 0, NT * C_END + 6
B1_0 = ACC_N
B1_N = 2 * H * SL - ACC_N
B2_0 = B1_0 + B1_N
B2_N = TILES * H
ARENA = B2_0 + B2_N


def at_least(eng, sem, value, tick):
    if isinstance(value, int):
        if value > 0:
            eng.wait_ge(sem, value)
        return
    eng.wait_ge(sem, value)
    eng.sem_inc(tick, 1)


def rounds(eng, count, ring, step, peeled=1):
    for k in range(peeled * ring):
        step(k, k // ring, k % ring)
    with eng.Fori(peeled, count // ring) as i:
        for r in range(ring):
            step(i * ring + r, i, r)
    for k in range(count // ring * ring, count):
        step(k, k // ring, k % ring)


def staggered(eng, count, ring, parts, peeled=2):
    def step(k, i, r):
        for lag, part in parts:
            if isinstance(k, int) and not lag <= k < count + lag:
                continue
            at = k - lag
            part(at, at // ring if isinstance(k, int) else (i if r >= lag else i - 1), (r - lag) % ring)
    rounds(eng, count, ring, step, peeled)
    for k in range(count, count + max(lag for lag, part in parts)):
        step(k, k // ring, k % ring)


def bias(c, name):
    a, b = BIASES[name]
    return c.bias_rows[:, a:b]


class Core:

    def __init__(self, nc):
        self.nc, self.used, self.w = nc, [], {}

    def semaphore(self, name):
        self.used.append(self.nc.alloc_semaphore(name=name))
        return self.used[-1]

    def clear_semaphores(self):
        self.nc.clear_and_free_semaphores(self.used)
        self.nc.all_engine_barrier()
        self.used = []


def arena(c, start, shape, dtype=F32):
    n = 1
    for s in shape:
        n *= s
    words = n if dtype != BF16 else n // 2
    ap = c.arena[:, start:start + words]
    if dtype != F32:
        ap = ap.bitcast(dtype)
    if len(shape) == 2:
        return ap.rearrange("p (a b) -> p a b", b=shape[1])
    if len(shape) == 3:
        return ap.rearrange("p (a b c) -> p a b c", b=shape[1], c=shape[2])
    return ap


def wide(ap, n):
    return ap.unsqueeze(2).broadcast_to([ap.shape[0], ap.shape[1], n])


def over(ap, n):
    return ap.unsqueeze(1).broadcast_to([ap.shape[0], n, ap.shape[1]])


def stage_setup(nc, c, t):
    with ExitStack() as ctx:
        sem = lambda n: c.semaphore(n)
        loaded, base, ready, cleared = sem("su_loaded"), sem("su_base"), sem("su_ready"), sem("su_cleared")
        ints, copied = sem("su_ints"), sem("su_copied")
        jint = ctx.enter_context(nc.sbuf_tensor("jint", [P, TILES], I32))
        pint = ctx.enter_context(nc.sbuf_tensor("pint", [P, 8], I32))
        loads = [(c.src_i, t["src"].rearrange("(p n) -> p n", p=P)),
                 (c.dst_i, t["dst"].rearrange("(p n) -> p n", p=P))]
        whole = N // P * P
        biases, split = sem("su_biases"), sem("su_split")
        rest = arena(c, B1_0, [BIAS_N])[0:65, :]
        parts = [arena(c, B1_0 + BIAS_N + n * BIAS_N // 2, [BIAS_N], BF16)[0:65, :] for n in range(3)]
        steps = [("v", lambda e: e.memset(c.ones_bf[:, :], 1.0)), ("v", lambda e: e.memset(c.bias_rows[:, :], 0.0))]
        steps += split_steps(rest, parts)
        steps += [("v", lambda e, n=n: e.tensor_copy(c.bias_rows[32 * n:32 * n + 1, :], parts[n][32 * n:32 * n + 1, :])) for n in range(3)]

        def bias_steps(eng, mine):
            eng.wait_ge(biases, 16 * len(BIASES))
            for n, (who, step) in enumerate(steps):
                if who == mine:
                    if n:
                        eng.wait_ge(split, n)
                    step(eng).then_inc(split, 1)
        block = ctx.enter_context(nc.Block())

        @block.sync
        def _(sp):
            for name, (a, b) in BIASES.items():
                sp.dma_start(rest[:, a:b], t[name].broadcast_to([65, b - a])).then_inc(biases, 16)
            for dst, src in loads:
                sp.dma_start(dst, src).then_inc(loaded, 16)
            sp.dma_start(c.x[:, 0:N // P, :], t["x"][0:whole, :].rearrange("(t p) f -> p t f", p=P)).then_inc(loaded, 16)
            sp.wait_ge(cleared, 1)
            sp.dma_start(c.x[0:N - whole, N // P, :], t["x"][whole:N, :]).then_inc(loaded, 16)
            sp.wait_ge(loaded, 16 * (len(loads) + 2))

        @block.gpsimd
        def _(pool):
            pool.iota(jint[:, :], [[1, TILES]], base=0, channel_multiplier=0).then_inc(ints, 1)
            pool.iota(pint[:, :], [[0, 8]], base=0, channel_multiplier=1).then_inc(ints, 1)
            pool.memset(c.ones[:, :], 1.0).then_inc(base, 1)
            pool.memset(c.ident[:, :], 0.0).then_inc(base, 1)
            pool.wait_ge(base, 2)
            pool.affine_select(out=c.ident[:, :], in_=c.ident[:, :], compare_op=ALU.not_equal, fill=1.0,
                               base=0, pattern=[[-1, P]], channel_multiplier=1).then_inc(base, 1)
            pool.affine_select(out=c.before[:, :], in_=c.ones[:, :], compare_op=ALU.is_gt, fill=0.0,
                               base=0, pattern=[[1, P]], channel_multiplier=-1).then_inc(base, 1)
            pool.affine_select(out=c.previous[:, :], in_=c.ones[:, :], compare_op=ALU.is_equal, fill=0.0,
                               base=1, pattern=[[-1, P]], channel_multiplier=1).then_inc(base, 1)

        @block.scalar
        def _(act):
            bias_steps(act, "s")
            act.wait_ge(loaded, 16 * (len(loads) + 2))
            act.activation(c.src_f[:, :], c.src_i, ACT.Copy).then_inc(copied, 1)
            act.activation(c.dst_f[:, :], c.dst_i, ACT.Copy).then_inc(copied, 1)

        @block.vector
        def _(dve):
            dve.memset(c.x[:, N // P:NT, :], 0.0).then_inc(cleared, 1)
            dve.wait_ge(ints, 2)
            dve.tensor_copy(c.j[:, :], jint[:, :]).then_inc(ready, 1)
            dve.tensor_copy(c.part[:, :], pint[:, 0:1]).then_inc(ready, 1)
            dve.wait_ge(ready, 2)
            dve.tensor_scalar(c.bounds[:, :], c.j[:, 0:NB], float(P), float(P), ALU.mult, ALU.add).then_inc(ready, 1)
            bias_steps(dve, "v")


def stage_lists(nc, c, t):
    with ExitStack() as ctx:
        sem = lambda n: c.semaphore(n)
        sb = lambda n, s, d: ctx.enter_context(nc.sbuf_tensor(n, s, d))
        pb = lambda n, s, d: ctx.enter_context(nc.psum_tensor(n, s, d))
        v, m = sem("li_v"), sem("li_m")
        gathered, floats, turned = [sem(f"li_gathered{i}") for i in range(3)], sem("li_floats"), sem("li_turned")
        sined, stored = sem("li_sined"), sem("li_stored")
        count = c.counts
        small = {s: sb(f"li_small_{s}", [P, 8], F32) for s in "ds"}
        whole = {s: sb(f"li_whole_{s}", [P, 1], I32) for s in "ds"}
        inside, past, wider = arena(c, B1_0, [TILES]), arena(c, B1_0 + TILES, [TILES]), sb("li_wider", [P, P], F32)
        slot0 = sb("li_slot0", [NB, NB], F32)
        own = sb("li_own", [P, NB], F32)
        cols_f, cols_i = sb("li_cols_f", [P, 8], F32), c.cols_i
        bucket_c = sb("li_bucket_c", [P, 8], F32)
        rows_bf = arena(c, ACC0 + 4 * 1024, [JC, P], BF16)
        fields_i = arena(c, ACC0, [2, JC, P], I32)
        fields = arena(c, B1_0 + 2 * TILES, [3, JC, P])
        bucket_f, mask, mask2 = (arena(c, B1_0 + 2 * TILES + 3 * JC * P + n * TILES, [TILES]) for n in range(3))
        half = TILES // 2
        ps = pb("li_ps", [P, 512], F32)
        psw = pb("li_psw", [P, 2, 512], F32)
        psb = pb("li_psb", [P, 2, 512], F32)
        psf = pb("li_psf", [P, 2, 512], F32)
        psc = pb("li_psc", [P, 512], F32)
        flat = {"src": t["src"], "dst": t["dst"], "w": t["edge_weight"]}
        block = ctx.enter_context(nc.Block())
        V = {}
        M = {name: n + 1 for n, name in enumerate([
            "dends", "dstarts", "dfirst", "cols", "dbucket", "sends", "sstarts", "sfirst", "sbucket", "base",
            "turnedsrc", "turneddst", "turnedw"])}

        @block.vector
        def _(dve):
            n = [0]

            def done(ins, name=None):
                n[0] += 1
                ins.then_inc(v, 1)
                if name:
                    V[name] = n[0]
                dve.wait_ge(v, n[0])

            def tiles_of(side):
                s = small[side][0:NB, :]
                dve.wait_ge(m, M[side + "ends"])
                done(dve.tensor_copy(s[:, 0:1], ps[0:NB, 0:1]), side + "ends")
                dve.wait_ge(m, M[side + "starts"])
                done(dve.tensor_copy(s[:, 1:2], ps[0:NB, 1:2]))
                done(dve.tensor_tensor(s[:, 2:3], s[:, 0:1], s[:, 1:2], ALU.subtract))
                done(dve.tensor_scalar(whole[side][0:NB, :], s[:, 2:3], float(P - 1), None, ALU.add))
                done(dve.tensor_scalar(whole[side][0:NB, :], whole[side][0:NB, :], 7, None, ALU.arith_shift_right))
                done(dve.tensor_copy(s[:, 3:4], whole[side][0:NB, :]))
                done(dve.tensor_scalar(s[:, 3:4], s[:, 3:4], 1.0, None, ALU.max), side + "tiles")
                dve.wait_ge(m, M[side + "first"])
                done(dve.tensor_copy(s[:, 4:5], ps[0:NB, 2:3]))
                done(dve.tensor_tensor(s[:, 5:6], s[:, 4:5], s[:, 3:4], ALU.add))
                done(dve.scalar_tensor_tensor(out=s[:, 6:7], in0=s[:, 4:5], scalar=-float(P), in1=s[:, 1:2],
                                              op0=ALU.mult, op1=ALU.add))
                done(dve.tensor_scalar(past[0:NB, :], c.j[0:NB, :], s[:, 5:6], None, ALU.is_ge), side + "past")

            tiles_of("d")
            s = small["d"][0:NB, :]
            done(dve.tensor_scalar(inside[0:NB, :], c.j[0:NB, :], s[:, 4:5], None, ALU.is_ge))
            done(dve.tensor_tensor(inside[0:NB, :], inside[0:NB, :], past[0:NB, :], ALU.subtract))
            done(dve.tensor_scalar(wider[0:NB, :], c.ones[0:NB, :], s[:, 6:7], None, ALU.mult), "wider")
            done(dve.memset(cols_f[:, :], 0.0))
            done(dve.memset(bucket_c[:, :], 0.0))
            dve.wait_ge(m, M["cols"])
            for k in range(JC):
                q = min(P, TILES - k * P)
                done(dve.tensor_scalar(cols_f[0:q, k:k + 1], c.part[0:q, :], float(P), float(k * P * P), ALU.mult, ALU.add))
                done(dve.tensor_tensor(cols_f[0:q, k:k + 1], cols_f[0:q, k:k + 1], ps[0:q, 8 + k:9 + k], ALU.add))
            done(dve.tensor_scalar(cols_i[:, :], cols_f[:, :], float(E - 1), None, ALU.min), "columns")
            dve.wait_ge(m, M["dbucket"])
            for k in range(JC):
                q = min(P, TILES - k * P)
                done(dve.tensor_scalar(bucket_c[0:q, k:k + 1], psc[0:q, k:k + 1], -float(P), None, ALU.mult))
            for h in range(2):
                at = slice(h * half, (h + 1) * half)
                done(dve.scalar_tensor_tensor(out=mask[32:33, at], in0=c.j[32:33, at], scalar=float(P), in1=psw[32:33, h, 0:half],
                                              op0=ALU.mult, op1=ALU.add))
                done(dve.tensor_copy(bucket_f[:, at], psb[:, h, 0:half]))
            done(dve.tensor_scalar(c.edge0, mask[32:33, :], float(E - 1), None, ALU.min))
            done(dve.tensor_copy(c.bucket_d, bucket_f[0:1, :]), "dused")

            tiles_of("s")
            dve.wait_ge(m, M["sbucket"])
            for h in range(2):
                at = slice(h * half, (h + 1) * half)
                done(dve.tensor_copy(c.bucket_s[:, at], psb[64:65, h, 0:half]))
            done(dve.tensor_scalar(slot0[:, :], c.ident[0:NB, 0:NB], small["s"][0:NB, 4:5], float(P), ALU.mult, ALU.mult))
            done(dve.tensor_copy(own[:, :], count["s"][:, :]))
            done(dve.tensor_tensor(own[:, 1:NB], count["s"][:, 1:NB], count["s"][:, 0:NB - 1], ALU.subtract), "own")
            dve.wait_ge(m, M["base"])
            done(dve.tensor_scalar(c.base[:, :], ps[:, 64:64 + NB], -1.0, None, ALU.add))
            done(dve.tensor_scalar(c.src_i, c.src_i, 7, None, ALU.arith_shift_right))
            done(dve.tensor_copy(c.src_bucket[:, :], c.src_i))
            done(dve.tensor_scalar(c.slot_of[:, :], c.src_bucket[:, :], float(NB), float(4 * SLOTS), ALU.is_ge, ALU.mult))

            dve.wait_ge(floats, 2)
            for k in range(JC):
                q = min(P, TILES - k * P)
                done(dve.tensor_scalar(rows_bf[0:q, k, :], fields[0:q, 1, k, :], bucket_c[0:q, k:k + 1], None, ALU.add), "rows")
            for f, name in enumerate(["src", "dst", "w"]):
                dve.wait_ge(m, M["turned" + name])
                for h, (a, b) in enumerate(((0, 512), (512, TILES))):
                    got = psf[:, h, 0:b - a]
                    if name == "src":
                        ins = dve.tensor_scalar(c.gather_d[:, a:b], got, float(N - 1), None, ALU.min)
                    elif name == "dst":
                        ins = dve.scalar_tensor_tensor(out=c.local_d[:, a:b], in0=bucket_f[:, a:b], scalar=-float(P), in1=got,
                                                       op0=ALU.mult, op1=ALU.add)
                    else:
                        ins = dve.tensor_copy(c.weight[:, a:b], got)
                    done(ins, f"took{name}{h}")
            done(dve.tensor_scalar(mask, c.local_d[:, :], 0.0, None, ALU.is_ge))
            done(dve.tensor_scalar(mask2, c.local_d[:, :], float(P), None, ALU.is_lt))
            done(dve.tensor_tensor(mask, mask, mask2, ALU.mult))
            done(dve.scalar_tensor_tensor(out=mask2, in0=bucket_f, scalar=float(P), in1=c.local_d[:, :], op0=ALU.mult, op1=ALU.add))
            done(dve.scalar_tensor_tensor(out=mask, in0=mask2, scalar=1.0, in1=mask, op0=ALU.add, op1=ALU.mult))
            done(dve.tensor_scalar(c.key[:, :], mask, -1.0, None, ALU.add))
            big = 1.5 * 2.0 ** 23
            done(dve.tensor_scalar(mask, c.weight[:, :], 1.0 / 20.0, None, ALU.mult))
            done(dve.tensor_scalar(mask2, mask, big, None, ALU.add))
            done(dve.tensor_scalar(mask2, mask2, -big, None, ALU.add))
            done(dve.tensor_tensor(mask, mask, mask2, ALU.subtract), "sine_arg")
            dve.wait_ge(sined, 1)
            done(dve.tensor_tensor(mask, mask2, mask2, ALU.mult))
            done(dve.tensor_scalar(c.cutoff[:, :], mask, -1.0, 1.0, ALU.mult, ALU.add))

        @block.gpsimd
        def _(pool):
            pool.wait_ge(v, V["columns"])
            for f, name in enumerate(["src", "dst", "w"]):
                table = flat[name].rearrange("(e one) -> e one", one=1)
                for k in range(JC):
                    to = fields[:, 2, k, :] if name == "w" else fields_i[:, f, k, :]
                    pool.indirect_dma_start(to, None, table, bass.IndirectOffsetOnAxis(cols_i[:, k:k + 1], 0))\
                        .then_inc(gathered[f], 16)

        @block.sync
        def _(sp):
            sp.wait_ge(v, V["rows"])
            full, rest = TILES // P, TILES % P
            sp.dma_start(c.local_rows[0:full * P, :].rearrange("(k j) f -> j k f", j=P), rows_bf[:, 0:full, :]).then_inc(stored, 16)
            sp.dma_start(c.local_rows[full * P:TILES, :], rows_bf[0:rest, full, :]).then_inc(stored, 16)
            sp.wait_ge(stored, 32)

        @block.scalar
        def _(act):
            for f in range(2):
                act.wait_ge(gathered[f], 16 * JC)
                act.activation(fields[:, f, :, :], fields_i[:, f, :, :], ACT.Copy).then_inc(floats, 1)
            act.wait_ge(v, V["sine_arg"])
            act.activation(mask2, mask, ACT.Sin, scale=3.141592653589793).then_inc(sined, 1)

        @block.tensor
        def _(pe):
            n = [0]

            def mark(ins, name):
                n[0] += 1
                ins.then_inc(m, 1)
                assert M[name] == n[0]

            for side in "ds":
                s = small[side]
                if side == "s":
                    pe.wait_ge(v, V["dused"])
                mark(pe.matmul(ps[0:NB, 0:1], count[side][:, :], c.ones[:, 0:1], start=True, stop=True), side + "ends")
                pe.wait_ge(v, V[side + "ends"])
                mark(pe.matmul(ps[0:NB, 1:2], c.previous[0:NB, 0:NB], s[0:NB, 0:1], start=True, stop=True), side + "starts")
                pe.wait_ge(v, V[side + "tiles"])
                mark(pe.matmul(ps[0:NB, 2:3], c.before[0:NB, 0:NB], s[0:NB, 3:4], start=True, stop=True), side + "first")
                if side == "d":
                    pe.wait_ge(v, V["wider"])
                    for k in range(JC):
                        q = min(P, TILES - k * P)
                        ins = pe.matmul(ps[0:q, 8 + k:9 + k], inside[0:NB, k * P:k * P + q], s[0:NB, 6:7], start=True, stop=True)
                    mark(ins, "cols")
                    for h in range(2):
                        pe.matmul(psw[:, h, 0:half], wider[0:NB, :], inside[0:NB, h * half:(h + 1) * half], start=True, stop=True)
                pe.wait_ge(v, V[side + "past"])
                for h in range(2):
                    ins = pe.matmul(psb[:, h, 0:half], c.ones[0:NB, :], past[0:NB, h * half:(h + 1) * half], start=True, stop=True)
                if side == "d":
                    for k in range(JC):
                        q = min(P, TILES - k * P)
                        ins = pe.matmul(psc[0:q, k:k + 1], past[0:NB, k * P:k * P + q], c.ones[0:NB, 0:1], start=True, stop=True)
                mark(ins, side + "bucket")
            pe.wait_ge(v, V["own"])
            pe.matmul(ps[:, 64:64 + NB], c.before[:, :], own[:, :], start=True, stop=False)
            mark(pe.matmul(ps[:, 64:64 + NB], c.ones[0:NB, :], slot0[:, :], start=False, stop=True), "base")
            for f, name in enumerate(["src", "dst", "w"]):
                if f < 2:
                    pe.wait_ge(floats, f + 1)
                else:
                    pe.wait_ge(gathered[2], 16 * JC)
                if f:
                    pe.wait_ge(v, V[f"took{['src', 'dst', 'w'][f - 1]}1"])
                for k in range(JC):
                    q = min(P, TILES - k * P)
                    ins = pe.transpose(psf[:, k // 4, k % 4 * P:k % 4 * P + q], fields[0:q, f, k, :], c.ident[0:q, 0:q])
                mark(ins, "turned" + name)


def count_edges(c, dve, junk, counted, tick):
    for n, (side, key) in enumerate((("d", c.dst_f), ("s", c.src_f))):
        def one(b):
            return dve.tensor_scalar(junk[:, :], key[:, :], c.bounds[:, bass.ds(b, 1)], 0.0, ALU.is_lt,
                                     ALU.add, accum_out=c.counts[side][:, bass.ds(b, 1)])
        if n:
            dve.wait_ge(counted, NB)
        one(0).then_inc(counted, 1)
        with dve.Fori(1, NB) as b:
            at_least(dve, counted, b + n * NB, tick)
            one(b).then_inc(counted, 1)
    dve.wait_ge(counted, 2 * NB)


def sweep(nc, c, name, sources, products, vector=None, scalar=None, store=None, beside=None):
    with ExitStack() as ctx:
        sem = lambda n: c.semaphore(name + n)
        turned, copied, multiplied, tick = sem("_turned"), sem("_copied"), sem("_multiplied"), sem("_tick")
        staged, vec, sca = sem("_staged"), sem("_vector"), sem("_scalar")
        n_src = len(sources)
        n_store = len(store(0)) if store else 0
        n_sca = len(scalar) if scalar else 0
        stored = [sem(f"_stored{q}") for q in range(G)]
        fixed = ctx.enter_context(nc.sbuf_tensor(name + "_fixed", [P, G, n_src, P], F32))
        xt = ctx.enter_context(nc.sbuf_tensor(name + "_xt", [P, G, n_src, P], F32))
        ring = ctx.enter_context(nc.sbuf_tensor(name + "_ring", [P, G, 384], F32)) if store else None
        pt = ctx.enter_context(nc.psum_tensor(name + "_pt", [P, G, 512], F32))
        po = ctx.enter_context(nc.psum_tensor(name + "_po", [P, G, 512], F32))
        block = ctx.enter_context(nc.Block())

        @block.gpsimd
        def _(pool):
            def stage(k, i, q):
                at_least(pool, turned, k - G + 1, tick)
                for s, (src, m) in enumerate(sources):
                    pool.tensor_copy(fixed[:, q, s, 0:m], src(k)).then_inc(staged, 1)
            staggered(pool, NT, G, [(0, stage)])

        @block.tensor
        def _(pe):
            def turn(k, i, q):
                at_least(pe, staged, n_src * (k + 1), tick)
                at_least(pe, copied, n_src * (k - G + 1), tick)
                for s, (src, m) in enumerate(sources):
                    ins = pe.transpose(pt[0:m, q, s * P:(s + 1) * P], fixed[:, q, s, 0:m], c.ident[:, :])
                ins.then_inc(turned, 1)

            def multiply(k, i, q):
                at_least(pe, copied, n_src * (k + 1), tick)
                if vector:
                    at_least(pe, vec, k - G + 1, tick)
                if scalar:
                    at_least(pe, sca, n_sca * (k - G + 1), tick)
                for n, (s, rhs, a, b) in enumerate(products):
                    m = rhs.shape[0]
                    lhs = c.ones_bf[0:m, :] if s is None else xt[0:m, q, s, :]
                    ins = pe.matmul(po[:, q, a:b], lhs, rhs, start=(n == 0), stop=(n == len(products) - 1))
                ins.then_inc(multiplied, 1)
            staggered(pe, NT, G, [(0, turn), (2, multiply)])

        @block.scalar
        def _(act):
            def copy(k, i, q):
                at_least(act, turned, k + 1, tick)
                at_least(act, multiplied, k - G + 1, tick)
                for s, (src, m) in enumerate(sources):
                    act.activation(xt[0:m, q, s, :], pt[0:m, q, s * P:(s + 1) * P], ACT.Copy).then_inc(copied, 1)

            def evacuate(k, i, q):
                at_least(act, multiplied, k + 1, tick)
                if vector:
                    at_least(act, vec, k + 1, tick)
                if store:
                    at_least(act, stored[q], i * 16 * n_store, tick)
                for take in scalar:
                    take(act, k, po[:, q, :], ring[:, q, :]).then_inc(sca, 1)
            staggered(act, NT, G, [(0, copy)] + ([(3, evacuate)] if scalar else []))

        if vector:
            @block.vector
            def _(dve):
                def take(k, i, q):
                    at_least(dve, multiplied, k + 1, tick)
                    vector(dve, k, po[:, q, :]).then_inc(vec, 1)
                staggered(dve, NT, G, [(0, take)])

        if beside:
            @block.vector
            def _(dve):
                beside(dve)

        if store:
            @block.sync
            def _(sp):
                def send(k, i, q):
                    at_least(sp, sca, n_sca * (k + 1), tick)
                    for dram, a, b in store(k):
                        sp.dma_start(dram, ring[:, q, a:b]).then_inc(stored[q], 16)
                staggered(sp, NT, G, [(0, send)])
                for q in range(G):
                    sp.wait_ge(stored[q], -(-(NT - q) // G) * 16 * n_store)


def vector_scalar_stage(nc, c, name, steps):
    with ExitStack() as ctx:
        done = c.semaphore(name + "_done")
        block = ctx.enter_context(nc.Block())

        def run(eng, mine):
            for n, (who, step) in enumerate(steps):
                if who == mine:
                    if n:
                        eng.wait_ge(done, n)
                    step(eng).then_inc(done, 1)

        @block.vector
        def _(dve):
            run(dve, "v")

        @block.scalar
        def _(act):
            run(act, "s")


def piece_stage(nc, c, name, steps, beside=None):
    with ExitStack() as ctx:
        pieces = [slice(a, a + PIECE) for a in range(0, NT, PIECE)]
        done = [c.semaphore(f"{name}_done{j}") for j in range(len(pieces))]
        made = c.semaphore(name + "_made")
        block = ctx.enter_context(nc.Block())

        def run(eng, mine):
            for n, (who, step) in enumerate(steps):
                if who == mine:
                    for j, at in enumerate(pieces):
                        if n:
                            eng.wait_ge(done[j], n)
                        if who == "p":
                            eng.wait_ge(made, j + 1)
                        step(eng, at).then_inc(done[j], 1)

        @block.vector
        def _(dve):
            run(dve, "v")

        @block.scalar
        def _(act):
            run(act, "s")

        if beside:
            @block.gpsimd
            def _(pool):
                for at in pieces:
                    beside(pool, at).then_inc(made, 1)
                run(pool, "p")


def norm_steps(c, y, squares, small, to):
    s, r = small[:, 0, :], small[:, 1, :]
    return [
        ("v", lambda e, at: e.tensor_reduce(s[:, at], y[:, at, :], AX_X, ALU.add)),
        ("v", lambda e, at: e.tensor_scalar(s[:, at], s[:, at], 1.0 / F, None, ALU.mult)),
        ("v", lambda e, at: e.tensor_tensor(y[:, at, :], y[:, at, :], wide(s[:, at], F), ALU.subtract)),
        ("s", lambda e, at: e.activation(squares[:, at, :], y[:, at, :], ACT.Square)),
        ("v", lambda e, at: e.tensor_reduce(s[:, at], squares[:, at, :], AX_X, ALU.add)),
        ("v", lambda e, at: e.tensor_scalar(s[:, at], s[:, at], 1.0 / F, LN_EPS, ALU.mult, ALU.add)),
        ("s", lambda e, at: e.activation(r[:, at], s[:, at], ACT.Sqrt)),
        ("v", lambda e, at: e.reciprocal(s[:, at], r[:, at])),
        ("v", lambda e, at: e.tensor_tensor(to[:, at, :], y[:, at, :], wide(s[:, at], F), ALU.mult)),
    ]


def norm_stage(nc, c, name, y, squares, small, first=(), affine=None, plus=None):
    if affine is None:
        piece_stage(nc, c, name, list(first) + norm_steps(c, y, squares, small, c.x))
        return
    gamma, beta = affine
    piece_stage(nc, c, name, list(first) + norm_steps(c, y, squares, small, y) + [
        ("v", lambda e, at: e.tensor_tensor(y[:, at, :], y[:, at, :], over(gamma, PIECE), ALU.mult)),
        ("p", lambda e, at: e.tensor_tensor(y[:, at, :], y[:, at, :], plus[:, at, :], ALU.add)),
    ] + norm_steps(c, y, squares, small, c.x),
                beside=lambda pool, at: pool.tensor_tensor(plus[:, at, :], c.x[:, at, :], over(beta, PIECE), ALU.add))


def split_steps(full, parts):
    return [
        ("s", lambda e: e.activation(parts[0], full, ACT.Copy)),
        ("v", lambda e: e.tensor_tensor(full, full, parts[0], ALU.subtract)),
        ("s", lambda e: e.activation(parts[1], full, ACT.Copy)),
        ("v", lambda e: e.tensor_tensor(full, full, parts[1], ALU.subtract)),
        ("s", lambda e: e.activation(parts[2], full, ACT.Copy)),
    ]


def split_pieces(full, parts, rest=None):
    rest = full if rest is None else rest
    return [
        ("s", lambda e, at: e.activation(parts[0][:, at, :], full[:, at, :], ACT.Copy)),
        ("v", lambda e, at: e.tensor_tensor(rest[:, at, :], full[:, at, :], parts[0][:, at, :], ALU.subtract)),
        ("s", lambda e, at: e.activation(parts[1][:, at, :], rest[:, at, :], ACT.Copy)),
        ("v", lambda e, at: e.tensor_tensor(rest[:, at, :], rest[:, at, :], parts[1][:, at, :], ALU.subtract)),
        ("s", lambda e, at: e.activation(parts[2][:, at, :], rest[:, at, :], ACT.Copy)),
    ]


def gather_rows(pool, c, table, index, ring, index_ready, arrived, freed, tick):
    def step(k, i, r):
        at_least(pool, index_ready, k + 1, tick)
        for sem, per in freed:
            if isinstance(sem, list):
                at_least(pool, sem[r], per * i, tick)
            else:
                at_least(pool, sem, per * (k - R + 1), tick)
        for u in range(U):
            pool.indirect_dma_start(ring[:, r, u, :], None, table, bass.IndirectOffsetOnAxis(index[:, r, u:u + 1], 0))\
                .then_inc(arrived[r], 16)
    rounds(pool, BATCHES, R, step)


def take_index(act, source, index, k, i, r, arrived, index_ready, tick):
    at_least(act, arrived[r], i * 16 * U, tick)
    act.activation(index[:, r, :], source[:, bass.ds(k * U, U)], ACT.Copy).then_inc(index_ready, 1)


def is_first(k):
    return isinstance(k, int) and k == 0


def loaded_values(nc, row, k, engine, top):
    return nc.values_load_multi_w_load_instructions(
        row[:, bass.ds(k * U, U)], engines=(engine,), min_val=0, max_val=top,
        skip_runtime_bounds_check_because="the vector engine made them within these bounds")[1]


class Adds:

    def __init__(self, nc, dve, acc, buckets, psum, width, k, summed, added, tick):
        self.which = loaded_values(nc, buckets, k, DVE_ENGINE, NT - 1)
        self.dve, self.acc, self.psum, self.width, self.k, self.added, self.tick = dve, acc, psum, width, k, added, tick
        self.summed = summed

    def one(self, u):
        if u == 0:
            at_least(self.dve, self.summed, self.k + 1, self.tick)
        before = self.k * U + u
        if not isinstance(before, int) or before > 0:
            self.dve.wait_ge(self.added, before)
        to = self.acc[:, bass.ds(self.which[u], 1), 0:self.width].rearrange("p one f -> p (one f)")
        self.dve.tensor_tensor(to, to, self.psum[:, u, 0:self.width], ALU.add).then_inc(self.added, 1)


def between(make_adds, steps):
    adds = None
    for n in range(max(U, len(steps))):
        if n < len(steps):
            steps[n]()
        if n == 0 and make_adds:
            adds = make_adds()
        if adds and n < U:
            adds.one(n)


def load_local_rows(sp, c, rows, k, r, arrived):
    src = c.local_rows[bass.ds(k * U, U), :].rearrange("(one u) f -> one (u f)", one=1)
    sp.dma_start(rows[:, r, :], src.broadcast_to([P, U * P])).then_inc(arrived[r], 16)


def stage_attention_scores(nc, c):
    with ExitStack() as ctx:
        sem = lambda n: c.semaphore("at_" + n)
        sb = lambda n, s, d: ctx.enter_context(nc.sbuf_tensor("at_" + n, s, d))
        index, ring = sb("index", [P, R, U], I32), sb("ring", [P, R, U, 2 * F], F32)
        rows, hot_t, prod, we = sb("rows", [P, R, U * P], BF16), sb("hot_t", [P, R, U, P], BF16), sb("prod", [P, 2, U, F], F32), sb("we", [P, 2, U, H], F32)
        rank, match = sb("rank", [P, CHUNK], F32), sb("match", [P, CHUNK], F32)
        pq = ctx.enter_context(nc.psum_tensor("at_pq", [P, 2, U, 256], F32))
        index_ready, arrived, kept = sem("index"), [sem(f"arrived{r}") for r in range(R)], [sem(f"kept{r}") for r in range(R)]
        rows_in = [sem(f"rows{r}") for r in range(R)]
        hots, queried, producted, reduced, weighed, scored, ranked, tick = (
            sem(n) for n in ("hots", "queried", "producted", "reduced", "weighed", "scored", "ranked", "tick"))
        block = ctx.enter_context(nc.Block())

        @block.gpsimd
        def _(pool):
            gather_rows(pool, c, c.kv, index, ring, index_ready, arrived, [(producted, 1), (kept, 16)], tick)

        @block.sync
        def _(sp):
            def step(k, i, r):
                at_least(sp, hots, k - R + 1, tick)
                load_local_rows(sp, c, rows, k, r, rows_in)
                if not is_first(k):
                    keep(k - 1, i if r else i - 1, (r - 1) % R)

            def keep(k, i, r):
                at_least(sp, arrived[r], 16 * U * (i + 1), tick)
                sp.dma_start(c.values[bass.ds(k, 1), :, :, :].rearrange("one p u f -> p (one u) f"), ring[:, r, :, F:2 * F]).then_inc(kept[r], 16)
            rounds(sp, BATCHES, R, step)
            keep(BATCHES - 1, BATCHES // R - 1, R - 1)
            for r in range(R):
                sp.wait_ge(kept[r], 16 * BATCHES // R)

        @block.scalar
        def _(act):
            rounds(act, BATCHES, R, lambda k, i, r: take_index(act, c.gather_d, index, k, i, r, arrived, index_ready, tick))

        @block.tensor
        def _(pe):
            def step(k, i, r):
                q = r % 2
                which = loaded_values(nc, c.bucket_d, k, PE_ENGINE, NT - 1)
                at_least(pe, hots, k + 1, tick)
                at_least(pe, weighed, k - 1, tick)
                at_least(pe, producted, k - 1, tick)
                for u in range(U):
                    for n, part in enumerate(c.query_parts):
                        ins = pe.matmul(pq[:, q, u, 0:QW], hot_t[:, r, u, :],
                                        part[:, bass.ds(which[u], 1), :].rearrange("p one f -> p (one f)"),
                                        start=(n == 0), stop=(n == 2))
                ins.then_inc(queried, 1)
            rounds(pe, BATCHES, R, step)

        @block.vector
        def _(dve):
            def one_hot(k, i, r):
                at_least(dve, rows_in[r], 16 * (i + 1), tick)
                at_least(dve, queried, k - R + 1, tick)
                dve.tensor_scalar(hot_t[:, r, :, :].rearrange("p u f -> p (u f)"), rows[:, r, :], c.part[:, 0:1], None, ALU.is_equal).then_inc(hots, 1)

            def products(k, i, r):
                q = r % 2
                at_least(dve, queried, k + 1, tick)
                at_least(dve, arrived[r], 16 * U * (i + 1), tick)
                at_least(dve, reduced, k - 1, tick)
                dve.tensor_tensor(prod[:, q, :, :], pq[:, q, :, 0:F], ring[:, r, :, 0:F], ALU.mult).then_inc(producted, 1)
                at_least(dve, scored, k - 1, tick)
                dve.tensor_tensor(we[:, q, :, :], pq[:, q, :, F:QW], wide(c.weight[:, bass.ds(k * U, U)], H), ALU.mult).then_inc(weighed, 1)

            def head_sums(k, r):
                at_least(dve, producted, k + 1, tick)
                to = c.alpha[:, bass.ds(k * U, U), :].rearrange("p u h -> p (u h)")
                dve.tensor_reduce(to, prod[:, r % 2, :, :].rearrange("p u (h d) -> p (u h) d", d=D), AX_X, ALU.add).then_inc(reduced, 1)

            def finish(k, r):
                at_least(dve, reduced, k + 1, tick)
                at_least(dve, weighed, k + 1, tick)
                to = c.alpha[:, bass.ds(k * U, U), :].rearrange("p u h -> p (u h)")
                dve.tensor_tensor(to, to, we[:, r % 2, :, :].rearrange("p u h -> p (u h)"), ALU.add).then_inc(scored, 1)

            def rank_bucket(b, part):
                at_least(dve, ranked, b * 4 + part, tick)
                if part == 0:
                    ins = dve.tensor_scalar(match[:, :], c.src_bucket[:, :], c.j[:, bass.ds(b, 1)], None, ALU.is_equal)
                if part == 1:
                    ins = dve.tensor_tensor_scan(rank[:, :], c.ones[:, 0:1].broadcast_to([P, CHUNK]), match[:, :],
                                                 c.base[:, bass.ds(b, 1)], ALU.mult, ALU.add)
                if part == 2:
                    ins = dve.tensor_tensor(rank[:, :], rank[:, :], match[:, :], ALU.mult)
                if part == 3:
                    ins = dve.tensor_tensor(c.slot_of[:, :], c.slot_of[:, :], rank[:, :], ALU.add)
                ins.then_inc(ranked, 1)

            def step(k, i, r, bucket=None):
                known = k if isinstance(k, int) else R
                one_hot(k, i, r)
                if known >= 2:
                    head_sums(k - 2, (r - 2) % R)
                if known >= 1:
                    products(k - 1, i if r else i - 1, (r - 1) % R)
                if known >= 2:
                    finish(k - 2, (r - 2) % R)
                if bucket is not None:
                    rank_bucket(bucket, r)
            for r in range(R):
                step(r, 0, r, 0)
            with dve.Fori(1, NB) as i:
                for r in range(R):
                    step(i * R + r, i, r, i)
            with dve.Fori(NB, BATCHES // R) as i:
                for r in range(R):
                    step(i * R + r, i, r)
            last = BATCHES - 1
            head_sums(last - 1, R - 2)
            products(last, BATCHES // R - 1, R - 1)
            finish(last - 1, R - 2)
            head_sums(last, R - 1)
            finish(last, R - 1)
            dve.wait_ge(scored, BATCHES)


def stage_attention_max(nc, c):
    with ExitStack() as ctx:
        v, m, s = (c.semaphore("mx_" + n) for n in ("v", "m", "s"))
        sb = lambda n, shape: ctx.enter_context(nc.sbuf_tensor("mx_" + n, shape, F32))
        a = arena(c, ACC0, [H, SL])[0:SP_PARTS, :, :]
        b = arena(c, ACC0 + H * SL, [H, SL])[0:SP_PARTS, :, :]
        pen, keys = sb("pen", [P, SL + 2]), sb("keys", [P, SL])
        ends, carry = sb("ends", [P, 4, H]), sb("carry", [P, 2, H])
        row = sb("row", [H, 10, P])
        pt = ctx.enter_context(nc.psum_tensor("mx_pt", [P, 4, 512], F32))
        Q = SP_PARTS
        pieces = [(h, g) for h in range(H) for g in range(SQ // 4)]
        block = ctx.enter_context(nc.Block())
        V, M, S = {}, {}, {}
        order = [f"keys{g}" for g in range(SQ // 4)] + [f"in{h}{g}" for h, g in pieces] + ["ends", "back0", "ends1", "back1"]
        order += [f"out{n}" for n in range(2 * H)]
        for n, name in enumerate(order):
            M[name] = n + 1
        takes = ([f"keys{g}" for g in range(SQ // 4)] + [f"in{h}{g}" for h, g in pieces])
        for n, name in enumerate(takes):
            S[name] = n + 1

        @block.vector
        def _(dve):
            n = [0]

            def done(ins, name=None):
                n[0] += 1
                ins.then_inc(v, 1)
                if name:
                    V[name] = n[0]
                dve.wait_ge(v, n[0])

            dve.wait_ge(s, S[f"keys{SQ // 4 - 1}"])
            done(dve.memset(pen[:, :], 0.0))
            done(dve.tensor_tensor(pen[0:Q, 1:SL], keys[0:Q, 1:SL], keys[0:Q, 0:SL - 1], ALU.not_equal))
            done(dve.tensor_scalar(pen[0:Q, 1:SL], pen[0:Q, 1:SL], FAR, None, ALU.mult))
            done(dve.tensor_copy(ends[0:Q, 2, :], keys[0:Q, 0:1].broadcast_to([Q, H])))
            done(dve.tensor_copy(ends[0:Q, 3, :], keys[0:Q, SL - 1:SL].broadcast_to([Q, H])))
            dve.wait_ge(s, len(takes))

            def scan(to, src, initial, backward):
                for h in range(H):
                    x0 = initial if isinstance(initial, float) else initial[0:Q, h:h + 1]
                    if backward:
                        ins = dve.tensor_tensor_scan(to[:, h, ::-1], pen[0:Q, 1:SL + 1][:, ::-1], src[:, h, ::-1], x0, ALU.add, ALU.max)
                    else:
                        ins = dve.tensor_tensor_scan(to[:, h, :], pen[0:Q, 0:SL], src[:, h, :], x0, ALU.add, ALU.max)
                    n[0] += 1
                    ins.then_inc(v, 1)
                dve.wait_ge(v, n[0])

            scan(b, a, FAR, False)
            done(dve.tensor_copy(ends[0:Q, 0, :], b[:, :, SL - 1]), "ends")
            dve.wait_ge(m, M["ends"])
            for f, w in ((0, 2), (1, 3), (2, 0)):
                done(dve.tensor_copy(row[:, f, 0:Q], pt[0:H, 0, w * P:w * P + Q]), "took")
            done(dve.tensor_tensor(row[:, 3, 0:Q], row[:, 0, 0:Q], row[:, 1, 0:Q], ALU.is_equal))
            done(dve.memset(row[:, 4, :], 0.0))
            done(dve.tensor_tensor(row[:, 4, 1:Q], row[:, 0, 1:Q], row[:, 1, 0:Q - 1], ALU.is_equal))
            done(dve.tensor_tensor(row[:, 5, 0:Q], row[:, 3, 0:Q], row[:, 4, 0:Q], ALU.mult))
            done(dve.tensor_scalar(row[:, 5, 0:Q], row[:, 5, 0:Q], -FAR, FAR, ALU.mult, ALU.add))
            done(dve.tensor_tensor_scan(row[:, 6, 0:Q], row[:, 5, 0:Q], row[:, 2, 0:Q], FAR, ALU.add, ALU.max))
            done(dve.tensor_scalar(row[:, 8, 0:Q], row[:, 4, 0:Q], -FAR, FAR, ALU.mult, ALU.add))
            done(dve.memset(row[:, 7, :], FAR))
            done(dve.tensor_tensor(row[:, 7, 1:Q], row[:, 8, 1:Q], row[:, 6, 0:Q - 1], ALU.add), "carry0")
            dve.wait_ge(m, M["back0"])
            done(dve.tensor_copy(carry[0:Q, 0, :], pt[0:Q, 1, 0:H]))
            scan(b, a, carry[:, 0, :], False)
            scan(a, b, FAR, True)
            done(dve.tensor_copy(ends[0:Q, 1, :], a[:, :, 0]), "ends1")
            dve.wait_ge(m, M["ends1"])
            done(dve.tensor_copy(row[:, 2, 0:Q], pt[0:H, 0, P:P + Q]))
            done(dve.memset(row[:, 5, :], 0.0))
            done(dve.tensor_tensor(row[:, 5, 0:Q - 1], row[:, 3, 0:Q - 1], row[:, 4, 1:Q], ALU.mult))
            done(dve.tensor_scalar(row[:, 5, 0:Q], row[:, 5, 0:Q], -FAR, FAR, ALU.mult, ALU.add))
            done(dve.tensor_tensor_scan(row[:, 6, 0:Q][:, ::-1], row[:, 5, 0:Q][:, ::-1], row[:, 2, 0:Q][:, ::-1], FAR, ALU.add, ALU.max))
            done(dve.memset(row[:, 7, :], FAR))
            done(dve.tensor_tensor(row[:, 7, 0:Q - 1], row[:, 8, 1:Q], row[:, 6, 1:Q], ALU.add), "carry1")
            dve.wait_ge(m, M["back1"])
            done(dve.tensor_copy(carry[0:Q, 1, :], pt[0:Q, 1, 0:H]))
            scan(a, b, carry[:, 1, :], True)
            V["max"] = n[0]
            for h in range(H):
                for g in range(2):
                    k = 2 * h + g
                    dve.wait_ge(m, M[f"out{k}"])
                    got = pt[:, 2 + k % 2, 0:4 * Q].rearrange("p (i q) -> p q i", i=4)
                    al = c.alpha[:, :, h].rearrange("p (q i) -> p q i", i=SQ)[:, :, 4 * g:4 * g + 4]
                    done(dve.tensor_tensor(al, al, got, ALU.subtract), f"out{k}")
            done(dve.tensor_scalar(c.alpha[:, :, :], c.alpha[:, :, :], 0.0, None, ALU.min), "cut")

        @block.tensor
        def _(pe):
            def mark(ins, name):
                ins.then_inc(m, 1)

            bank = 0
            for g in range(SQ // 4):
                for i in range(4):
                    ins = pe.transpose(pt[0:Q, bank, i * P:(i + 1) * P], c.key[:, 4 * g + i::SQ], c.ident[:, :])
                mark(ins, f"keys{g}")
                bank += 1
            for h, g in pieces:
                if bank >= 4:
                    pe.wait_ge(s, bank - 3)
                for i in range(4):
                    ins = pe.transpose(pt[0:Q, bank % 4, i * P:(i + 1) * P], c.alpha[:, 4 * g + i::SQ, h], c.ident[:, :])
                mark(ins, f"in{h}{g}")
                bank += 1
            pe.wait_ge(s, len(takes))
            pe.wait_ge(v, V["ends"])
            for w in (0, 2, 3):
                ins = pe.transpose(pt[0:H, 0, w * P:w * P + Q], ends[0:Q, w, :], c.ident[0:Q, 0:Q])
            mark(ins, "ends")
            pe.wait_ge(v, V["carry0"])
            mark(pe.transpose(pt[0:Q, 1, 0:H], row[:, 7, 0:Q], c.ident[0:H, 0:H]), "back0")
            pe.wait_ge(v, V["ends1"])
            mark(pe.transpose(pt[0:H, 0, P:P + Q], ends[0:Q, 1, :], c.ident[0:Q, 0:Q]), "ends1")
            pe.wait_ge(v, V["carry1"])
            mark(pe.transpose(pt[0:Q, 1, 0:H], row[:, 7, 0:Q], c.ident[0:H, 0:H]), "back1")
            pe.wait_ge(v, V["max"])
            for h in range(H):
                for g in range(2):
                    k = 2 * h + g
                    if k >= 2:
                        pe.wait_ge(v, V[f"out{k - 2}"])
                    for i in range(4):
                        ins = pe.transpose(pt[:, 2 + k % 2, i * Q:(i + 1) * Q],
                                           a[:, h, (4 * g + i) * P:(4 * g + i + 1) * P], c.ident[0:Q, 0:Q])
                    mark(ins, f"out{k}")

        @block.scalar
        def _(act):
            for n, name in enumerate(takes):
                act.wait_ge(m, M[name])
                src = pt[0:Q, n % 4, :]
                if name.startswith("keys"):
                    g = int(name[4:])
                    to = keys[0:Q, g * 512:(g + 1) * 512]
                else:
                    h, g = int(name[2]), int(name[3])
                    to = a[:, h, g * 512:(g + 1) * 512]
                act.activation(to, src, ACT.Copy).then_inc(s, 1)
            act.wait_ge(v, V["cut"])
            act.activation(c.alpha[:, :, :], c.alpha[:, :, :], ACT.Exp).then_inc(s, 1)


def stage_attention_sums(nc, c):
    with ExitStack() as ctx:
        sem = lambda n: c.semaphore("as_" + n)
        sb = lambda n, s, d: ctx.enter_context(nc.sbuf_tensor("as_" + n, s, d))
        acc = arena(c, ACC0, [NT, C_END])
        ring = sb("ring", [P, R, U, F], F32)
        hot, msg = sb("hot", [P, R, U, P], F32), sb("msg", [P, R, U, C_END], F32)
        by_tile = arena(c, B1_0, [JC, P])
        slot, high7, high9, wrong, row = (arena(c, B1_0 + JC * P + n * TILES, [TILES]) for n in range(5))
        whole = arena(c, B1_0 + JC * P + 5 * TILES, [TILES], I32)
        shifted = arena(c, B1_0 + JC * P + 6 * TILES, [TILES], I32)
        pt = ctx.enter_context(nc.psum_tensor("as_pt", [P, 2, 512], F32))
        kept, gathered, turned, numbered = sem("kept"), sem("gathered"), sem("turned"), sem("numbered")
        pa = ctx.enter_context(nc.psum_tensor("as_pa", [P, 2, U, 256], F32))
        arrived = [sem(f"arrived{r}") for r in range(R)]
        messages, made, summed, added, start, tick = (sem(n) for n in ("messages", "made", "summed", "added", "start", "tick"))
        block = ctx.enter_context(nc.Block())

        @block.gpsimd
        def _(pool):
            pool.wait_ge(kept, 16)
            table = c.slots.rearrange("(e one) -> e one", one=1)
            for k in range(JC):
                pool.indirect_dma_start(by_tile[:, k, :], None, table, bass.IndirectOffsetOnAxis(c.cols_i[:, k:k + 1], 0)).then_inc(gathered, 16)

            def step(k, i, r):
                at_least(pool, arrived[r], 16 * (i + 1), tick)
                at_least(pool, summed, k - R + 1, tick)
                pool.tensor_tensor(msg[:, r, :, 0:F].rearrange("p u (h d) -> p u h d", d=D),
                                   c.alpha[:, bass.ds(k * U, U), :].unsqueeze(3).broadcast_to([P, U, H, D]),
                                   ring[:, r, :, :].rearrange("p u (h d) -> p u h d", d=D), ALU.mult).then_inc(messages, 1)
            rounds(pool, BATCHES, R, step)

        @block.sync
        def _(sp):
            sp.dma_start(c.slots.rearrange("(p n) -> p n", p=P), c.slot_of[:, :]).then_inc(kept, 16)

            def step(k, i, r):
                at_least(sp, messages, k - R + 1, tick)
                sp.dma_start(ring[:, r, :, :].rearrange("p u f -> p (u f)"), c.values[bass.ds(k, 1), :, :, :].rearrange("one p u f -> p (one u f)"))\
                    .then_inc(arrived[r], 16)
            rounds(sp, BATCHES, R, step)

        @block.tensor
        def _(pe):
            def step(k, i, r):
                q = r % 2
                at_least(pe, messages, k + 1, tick)
                at_least(pe, made, 3 * (k + 1), tick)
                at_least(pe, added, U * (k - 1), tick)
                if is_first(k):
                    pe.wait_ge(start, 2)
                for u in range(U):
                    ins = pe.matmul(pa[:, q, u, 0:C_END], hot[:, r, u, :], msg[:, r, u, :], start=True, stop=True)
                ins.then_inc(summed, 1)
            rounds(pe, BATCHES, R, step)
            pe.wait_ge(gathered, 16 * JC)
            for k in range(JC):
                q = min(P, TILES - k * P)
                ins = pe.transpose(pt[:, k // 4, k % 4 * P:k % 4 * P + q], by_tile[0:q, k, :], c.ident[0:q, 0:q])
            ins.then_inc(turned, 1)

        @block.vector
        def _(dve):
            dve.memset(acc, 0.0).then_inc(start, 1)
            dve.memset(msg[:, :, :, C_CNT:C_END], 1.0).then_inc(start, 1)
            dve.wait_ge(start, 2)

            def make(k, i, r):
                at = bass.ds(k * U, U)
                ex = c.alpha[:, at, :]

                def one_hot():
                    at_least(dve, summed, k - R + 1, tick)
                    dve.tensor_tensor(hot[:, r, :, :], over(c.j[:, 0:P], U), wide(c.local_d[:, at], P), ALU.is_equal).then_inc(made, 1)

                def exps():
                    dve.tensor_copy(msg[:, r, :, C_EX:C_EW], ex).then_inc(made, 1)

                def weighted():
                    dve.tensor_tensor(msg[:, r, :, C_EW:C_CNT], ex, wide(c.weight[:, at], H), ALU.mult).then_inc(made, 1)
                return [one_hot, exps, weighted]

            def adds(k, r):
                return Adds(nc, dve, acc, c.bucket_d, pa[:, r % 2, :, :], C_END, k, summed, added, tick)

            def step(k, i, r):
                between(None if isinstance(k, int) and k < 2 else lambda: adds(k - 2, (r - 2) % R), make(k, i, r))
            rounds(dve, BATCHES, R, step)
            for k in (BATCHES - 2, BATCHES - 1):
                between(lambda: adds(k, k % R), [])

            n = [0]

            def done(ins):
                n[0] += 1
                ins.then_inc(numbered, 1)
                dve.wait_ge(numbered, n[0])
            dve.wait_ge(turned, 1)
            for h, (a, b) in enumerate(((0, 512), (512, TILES))):
                done(dve.tensor_copy(slot[:, a:b], pt[:, h, 0:b - a]))
            done(dve.tensor_copy(whole, slot))
            for shift, to in ((7, high7), (9, high9)):
                done(dve.tensor_scalar(shifted, whole, shift, None, ALU.arith_shift_right))
                done(dve.tensor_copy(to, shifted))
            done(dve.tensor_scalar(wrong, c.key[:, :], 0.0, float(4 * SLOTS), ALU.is_lt, ALU.mult))
            done(dve.scalar_tensor_tensor(out=row, in0=slot, scalar=4.0, in1=wrong, op0=ALU.mult, op1=ALU.add))
            done(dve.scalar_tensor_tensor(out=row, in0=high7, scalar=-511.0, in1=row, op0=ALU.mult, op1=ALU.add))
            done(dve.scalar_tensor_tensor(out=c.key[:, :], in0=high9, scalar=508.0, in1=row, op0=ALU.mult, op1=ALU.add))
            done(dve.tensor_copy(whole, c.gather_d[:, :]))
            done(dve.tensor_scalar(shifted, whole, 7, None, ALU.arith_shift_right))
            done(dve.tensor_copy(high7, shifted))
            done(dve.scalar_tensor_tensor(out=c.src_local[:, :], in0=high7, scalar=-float(P), in1=c.gather_d[:, :], op0=ALU.mult, op1=ALU.add))
            dve.wait_ge(added, BATCHES * U)


def stage_edges(nc, c, name, table, acc, buckets, gather, local, layer):
    with ExitStack() as ctx:
        sem = lambda n: c.semaphore(name + n)
        sb = lambda n, s, d=F32: ctx.enter_context(nc.sbuf_tensor(name + n, s, d))
        pb = lambda n, s: ctx.enter_context(nc.psum_tensor(name + n, s, F32))
        index, ring = sb("index", [P, R, U], I32), sb("ring", [P, R, U, F])
        hot = sb("hot", [P, R, U, P])
        pa = pb("pa", [P, 2, U, F])
        arrived, attributes = [sem(f"arrived{r}") for r in range(R)], [sem(f"attributes{r}") for r in range(R)]
        rows_in = [sem(f"rows{r}") for r in range(R)]
        index_ready, hots, summed, added, start, tick = (sem(n) for n in ("index", "hots", "summed", "added", "start", "tick"))
        hots_t, copied, first, second, third, sent, ready = (sem(n) for n in ("hots_t", "copied", "first", "second", "third", "sent", "ready"))
        width = A1 if layer == 1 else A2
        attr = sb("attr", [width, R, U * P])
        msg = sb("msg", [P, 2, U, P])
        tmp = sb("tmp", [P, 2, U, P])
        ph = pb("ph", [P, 2, U, F])
        if layer == 1:
            hot_t, rows = sb("hot_t", [P, R, U, P], BF16), sb("rows", [P, R, U * P], BF16)
            filler, filled = sb("filler", [P, U, REV]), sem("filled")
        if layer == 2:
            pt = pb("pt", [P, 2, U, P])
            soft = sb("soft", [P, 2, U, P])
            pos = sb("pos", [P, 2, U, P])
        attr_dram = {1: c.attr1, 2: c.attr2}[layer]
        freed = first if layer == 1 else sent
        hidden_lag, message_lag, total_lag, add_lag = {1: (1, 2, 3, 4), 2: (2, 3, 3, 4)}[layer]
        block = ctx.enter_context(nc.Block())

        def behind(k, i, r, n):
            return k - n, i if r >= n else i - 1, (r - n) % R

        @block.gpsimd
        def _(pool):
            gather_rows(pool, c, table, index, ring, index_ready, arrived, [(freed, 1)], tick)

        @block.sync
        def _(sp):
            def step(k, i, r):
                e0 = loaded_values(nc, c.edge0, k, SP_ENGINE, E - 1)
                at_least(sp, ready, k - R + 1, tick)
                if layer == 1:
                    at_least(sp, hots_t, k - R + 1, tick)
                    load_local_rows(sp, c, rows, k, r, rows_in)
                for u in range(U):
                    sp.dma_start(attr[:, r, u * P:(u + 1) * P], attr_dram[:, bass.ds(e0[u], P)]).then_inc(attributes[r], 16)
                if layer == 1:
                    if is_first(k):
                        sp.wait_ge(start, 3)
                    sp.dma_start(c.by_src[bass.ds(k, 1), :, :, :].rearrange("one p u f -> p (one u) f"), filler[:, :, :]).then_inc(filled, 16)
            rounds(sp, BATCHES, R, step)
            if layer == 1:
                sp.wait_ge(filled, 16 * BATCHES)

        @block.scalar
        def _(act):
            def next_index(k, i, r):
                take_index(act, gather, index, k, i, r, arrived, index_ready, tick)

            def softplus(k, i, r):
                q = r % 2
                x = pt[:, q, :, :]
                at_least(act, ready, k + 1, tick)
                at_least(act, second, k - 1, tick)
                act.activation(tmp[:, q, :, :], x, ACT.Abs, bias=c.w["mlp_b0"][:, 0:1]).then_inc(copied, 1)
                act.activation(pos[:, q, :, :], x, ACT.Relu, bias=c.w["mlp_b0"][:, 0:1]).then_inc(copied, 1)
                at_least(act, copied, 4 * k + 1, tick)
                act.activation(tmp[:, q, :, :], tmp[:, q, :, :], ACT.Exp, scale=-1.0).then_inc(copied, 1)
                at_least(act, copied, 4 * k + 3, tick)
                act.activation(tmp[:, q, :, :], tmp[:, q, :, :], ACT.Ln, bias=c.ones[:, 0:1]).then_inc(copied, 1)

            def relu(k, i, r):
                q = r % 2
                at_least(act, first, k + 1, tick)
                at_least(act, summed, k - 1, tick)
                act.activation(msg[:, q, :, :], tmp[:, q, :, :], ACT.Relu).then_inc(sent, 1)

            if layer == 2:
                act.preload_act_table_set("natural_log_exp_and_others")
            staggered(act, BATCHES, R, [(0, next_index)] + {1: [(2, relu)], 2: [(1, softplus)]}[layer])

        @block.tensor
        def _(pe):
            def turn(k, i, r):
                at_least(pe, attributes[r], 16 * U * (i + 1), tick)
                at_least(pe, copied, 4 * (k - 1), tick)
                pe.matmul(pt[:, r % 2, :, :].rearrange("p u f -> p (u f)"), c.w["mlp_w0"][:, :], attr[:, r, :], start=True, stop=True).then_inc(ready, 1)

            def hidden(k, i, r):
                q = r % 2
                if layer == 1:
                    which = loaded_values(nc, buckets, k, PE_ENGINE, NT - 1)
                    at_least(pe, hots_t, k + 1, tick)
                    at_least(pe, attributes[r], 16 * U * (i + 1), tick)
                    at_least(pe, first, k - 1, tick)
                    for u in range(U):
                        for n, part in enumerate(c.dst_parts):
                            pe.matmul(ph[:, q, u, :], hot_t[:, r, u, :], part[:, bass.ds(which[u], 1), :].rearrange("p one f -> p (one f)"),
                                      start=(n == 0), stop=False)
                        ins = pe.matmul(ph[:, q, u, :], attr[:, r, u * P:(u + 1) * P], c.w["w1e"][:, :], start=False, stop=True)
                    ins.then_inc(ready, 1)
                if layer == 2:
                    at_least(pe, second, k + 1, tick)
                    at_least(pe, sent, k - 1, tick)
                    for u in range(U):
                        pe.matmul(ph[:, q, u, :], c.ones_bf[:, :], bias(c, "L2_mlp_b2"), start=True, stop=False)
                        ins = pe.matmul(ph[:, q, u, :], soft[:, q, u, :], c.w["mlp_w2"][:, :], start=False, stop=True)
                    ins.then_inc(third, 1)

            def total(k, i, r):
                q = r % 2
                at_least(pe, sent, k + 1, tick)
                at_least(pe, hots, (U if layer == 2 else 1) * (k + 1), tick)
                at_least(pe, added, U * (k - 1), tick)
                for u in range(U):
                    ins = pe.matmul(pa[:, q, u, :], hot[:, r, u, :], msg[:, q, u, :], start=True, stop=True)
                ins.then_inc(summed, 1)

            staggered(pe, BATCHES, R, ([(0, turn)] if layer == 2 else []) + [(hidden_lag, hidden), (total_lag, total)])

        @block.vector
        def _(dve):
            dve.memset(acc, 0.0).then_inc(start, 1)
            dve.wait_ge(start, 1)
            if layer == 1:
                dve.memset(filler[:, :, :], 0.0).then_inc(start, 1)
                dve.wait_ge(start, 2)
                dve.memset(filler[:, :, F + 1:REV], float(NOWHERE)).then_inc(start, 1)

            def one_hot(k, i, r):
                if layer == 2:
                    def tile_hot(u):
                        if u == 0:
                            at_least(dve, summed, k - R + 1, tick)
                        dve.tensor_scalar(hot[:, r, u, :], c.j[:, 0:P], local[:, bass.ds(k * U + u, 1)], c.cutoff[:, bass.ds(k * U + u, 1)],
                                          ALU.is_equal, ALU.mult).then_inc(hots, 1)
                    return [lambda u=u: tile_hot(u) for u in range(U)]

                def edges_hot():
                    at_least(dve, summed, k - R + 1, tick)
                    dve.tensor_tensor(hot[:, r, :, :], over(c.j[:, 0:P], U), wide(local[:, bass.ds(k * U, U)], P), ALU.is_equal).then_inc(hots, 1)
                return [edges_hot]

            def one_hot_turned(k, i, r):
                at_least(dve, rows_in[r], 16 * (i + 1), tick)
                at_least(dve, ready, k - R + 1, tick)
                dve.tensor_scalar(hot_t[:, r, :, :].rearrange("p u f -> p (u f)"), rows[:, r, :], c.part[:, 0:1], None, ALU.is_equal).then_inc(hots_t, 1)

            def message(k, i, r):
                q = r % 2
                if layer == 1:
                    at_least(dve, ready, k + 1, tick)
                    at_least(dve, arrived[r], 16 * U * (i + 1), tick)
                    at_least(dve, sent, k - 1, tick)
                    dve.tensor_tensor(tmp[:, q, :, :], ph[:, q, :, :], ring[:, r, :, :], ALU.add).then_inc(first, 1)
                if layer == 2:
                    at_least(dve, third, k + 1, tick)
                    at_least(dve, arrived[r], 16 * U * (i + 1), tick)
                    at_least(dve, summed, k - 1, tick)
                    dve.tensor_tensor(msg[:, q, :, :], ph[:, q, :, :], ring[:, r, :, :], ALU.mult).then_inc(sent, 1)

            def soften(k, i, r):
                q = r % 2
                at_least(dve, copied, 4 * (k + 1), tick)
                at_least(dve, third, k - 1, tick)
                dve.scalar_tensor_tensor(out=soft[:, q, :, :].rearrange("p u f -> p (u f)"), in0=pos[:, q, :, :].rearrange("p u f -> p (u f)"),
                                         scalar=-LOG2, in1=tmp[:, q, :, :].rearrange("p u f -> p (u f)"), op0=ALU.add, op1=ALU.add).then_inc(second, 1)

            def step(k, i, r):
                new = not (isinstance(k, int) and k >= BATCHES)
                there = lambda n: (not isinstance(k, int) or n <= k < BATCHES + n)
                steps = []
                if layer == 1 and new:
                    steps.append(lambda: one_hot_turned(k, i, r))
                if layer == 2 and there(2):
                    steps.append(lambda: soften(*behind(k, i, r, 2)))
                if there(message_lag):
                    steps.append(lambda: message(*behind(k, i, r, message_lag)))
                if new:
                    steps += one_hot(k, i, r)
                def adds():
                    ka, ia, ra = behind(k, i, r, add_lag)
                    return Adds(nc, dve, acc, buckets, pa[:, ra % 2, :, :], F, ka, summed, added, tick)
                between(adds if there(add_lag) else None, steps)
            rounds(dve, BATCHES, R, step, peeled=2)
            for k in range(BATCHES, BATCHES + add_lag):
                step(k, k // R, k % R)
            dve.wait_ge(added, BATCHES * U)


def load_weights(nc, c, ctx, t, name, natural=(), rows=(), wide_rows=()):
    loaded = c.semaphore(name + "_weights")
    loads = []
    for group, how in ((natural, 0), (rows, 0), (wide_rows, 1)):
        for attr, src in group:
            src = t[src] if isinstance(src, str) else src
            tile = ctx.enter_context(nc.sbuf_tensor(name + "_" + attr, [P, src.shape[1]] if how else list(src.shape), F32))
            c.w[attr] = tile
            loads.append((tile[:, :], src.broadcast_to([P, src.shape[1]]) if how else src))
    with ExitStack() as inner:
        block = inner.enter_context(nc.Block())

        @block.sync
        def _(sp):
            for to, src in loads:
                sp.dma_start(to, src).then_inc(loaded, 16)
            sp.wait_ge(loaded, 16 * len(loads))


def tile_rows(table, k, a=0, b=None):
    return table[bass.ds(k, 1), :, a:b if b else table.shape[2]].rearrange("one p f -> p (one f)")


def at_tile(whole, k, a=0, b=None):
    return whole[:, bass.ds(k, 1), a:b if b else whole.shape[2]].rearrange("p one f -> p (one f)")


def attention_layer(nc, c, t, small):
    with ExitStack() as ctx:
        load_weights(nc, c, ctx, t, "l0", natural=[(n, "L0_" + n) for n in ("wq", "wk", "wv", "wskip", "wo")],
                     wide_rows=[(n, "L0_" + n) for n in ("we", "gamma", "beta")])
        by_we = arena(c, 3 * NT * QW // 2, [NT, F])
        q_full = arena(c, 3 * NT * QW // 2 + NT * F, [NT, QW])
        c.alpha = arena(c, B2_0, [TILES, H])
        c.query_parts = [arena(c, n * NT * QW // 2, [NT, QW], BF16) for n in range(3)]

        junk = arena(c, ACC0 + 4096, [CHUNK])
        counted, tick = c.semaphore("counted"), c.semaphore("counted_tick")

        def keep(k):
            return [(tile_rows(c.kv3, k), 0, 2 * F), (tile_rows(c.skip, k), 2 * F, 3 * F)]

        sweep(nc, c, "qkv", [(lambda k: at_tile(c.x, k), P)],
              [(None, bias(c, "L0_bias4"), 0, 4 * F)] + [(0, w[:, :], n * F, (n + 1) * F) for n, w in enumerate((c.w["wq"], c.w["wk"], c.w["wv"], c.w["wskip"]))],
              scalar=[lambda e, k, po, ring: e.activation(ring[:, :], po[:, F:4 * F], ACT.Copy),
                      lambda e, k, po, ring: e.activation(at_tile(q_full, k, 0, F), po[:, 0:F], ACT.Copy, scale=1.0 / D ** 0.5)],
              store=keep, beside=lambda dve: count_edges(c, dve, junk, counted, tick))
        stage_lists(nc, c, t)
        piece_stage(nc, c, "query", [
            ("v", lambda e, at: e.tensor_tensor(by_we[:, at, :], q_full[:, at, 0:F], over(c.w["we"][:, :], PIECE), ALU.mult)),
            ("v", lambda e, at: e.tensor_reduce(q_full[:, at, F:QW], by_we[:, at, :].rearrange("p t (h d) -> p t h d", d=D), AX_X, ALU.add)),
        ] + split_pieces(q_full, c.query_parts))
        stage_attention_scores(nc, c)
        stage_attention_max(nc, c)
        stage_attention_sums(nc, c)
        load_whole(nc, c, arena(c, B2_0, [NT, F]), c.skip, "skip")

        acc, heads, y = arena(c, ACC0, [NT, C_END]), arena(c, B1_0, [NT, F]), arena(c, B2_0, [NT, F])
        by_head = heads.rearrange("p t (h d) -> p t h d", d=D)
        den = acc[:, :, C_EX:C_EW]
        spread = lambda a: a.unsqueeze(3).broadcast_to([P, NT, H, D])
        vector_scalar_stage(nc, c, "heads", [
            ("v", lambda e: e.tensor_copy(c.count[:, :], acc[:, :, C_CNT])),
            ("v", lambda e: e.tensor_scalar(den, den, 1e-16, None, ALU.max)),
            ("v", lambda e: e.reciprocal(den, den)),
            ("v", lambda e: e.tensor_copy(by_head, spread(acc[:, :, C_EW:C_CNT]))),
            ("v", lambda e: e.tensor_tensor(heads, heads, over(c.w["we"][:, :], NT), ALU.mult)),
            ("v", lambda e: e.tensor_tensor(heads, heads, acc[:, :, 0:F], ALU.add)),
            ("v", lambda e: e.tensor_tensor(by_head, by_head, spread(den), ALU.mult)),
            ("v", lambda e: e.tensor_tensor(heads, heads, y, ALU.add)),
        ])
        sweep(nc, c, "wo", [(lambda k: at_tile(heads, k), P)], [(None, bias(c, "L0_bo"), 0, F), (0, c.w["wo"][:, :], 0, F)],
              vector=lambda e, k, po: e.tensor_tensor(at_tile(y, k), po[:, 0:F], at_tile(c.x, k), ALU.add))
        norm_stage(nc, c, "norm0", y, heads, small, affine=(c.w["gamma"][:, :], c.w["beta"][:, :]), plus=arena(c, ACC0, [NT, F]))


def load_whole(nc, c, to, table, name):
    with ExitStack() as ctx:
        loaded = c.semaphore(name + "_loaded")
        block = ctx.enter_context(nc.Block())

        @block.sync
        def _(sp):
            sp.dma_start(to, table.rearrange("t p f -> p t f")).then_inc(loaded, 16)
            sp.wait_ge(loaded, 16)


def edge_mlp_layer(nc, c, t, small):
    with ExitStack() as ctx:
        load_weights(nc, c, ctx, t, "l1", natural=[(n, "L1_" + n) for n in ("w1s", "w1d", "w1e", "w2", "b2_col", "wu")],
                     wide_rows=[("gamma", "L1_gamma"), ("beta", "L1_beta")])
        acc, full, mid, y = arena(c, ACC0, [NT, F]), arena(c, ACC0, [NT, F]), arena(c, B1_0, [NT, F]), arena(c, B2_0, [NT, F])
        c.dst_parts = [arena(c, B1_0 + n * NT * F // 2, [NT, F], BF16) for n in range(3)]
        w_both = ctx.enter_context(nc.sbuf_tensor("l1_both", [P, F], F32))
        b_both = ctx.enter_context(nc.sbuf_tensor("l1_b_both", [P, F], F32))
        sweep(nc, c, "l1in", [(lambda k: at_tile(c.x, k), P)],
              [(0, c.w["w1s"][:, :], 0, F), (0, c.w["w1d"][:, :], F, 2 * F), (None, bias(c, "L1_b1"), F, 2 * F)],
              vector=lambda e, k, po: e.tensor_copy(at_tile(full, k), po[:, F:2 * F]),
              scalar=[lambda e, k, po, ring: e.activation(ring[:, 0:F], po[:, 0:F], ACT.Copy)],
              store=lambda k: [(tile_rows(c.table3, k), 0, F)])
        piece_stage(nc, c, "split1", split_pieces(full, c.dst_parts))
        with ExitStack() as inner:
            made = c.semaphore("l1_made")
            took = c.semaphore("l1_took")
            pw = inner.enter_context(nc.psum_tensor("l1_pw", [P, 512], F32))
            block = inner.enter_context(nc.Block())

            @block.tensor
            def _(pe):
                pe.matmul(pw[:, 0:F], c.w["w2"][:, :], c.w["wu"][:, :], start=True, stop=True).then_inc(made, 1)
                pe.matmul(pw[:, F:2 * F], c.w["b2_col"][:, 0:1].broadcast_to([P, P]), c.w["wu"][:, :], start=True, stop=True).then_inc(made, 1)

            @block.vector
            def _(dve):
                dve.wait_ge(made, 2)
                dve.tensor_copy(w_both[:, :], pw[:, 0:F]).then_inc(took, 1)
                dve.tensor_copy(b_both[:, :], pw[:, F:2 * F]).then_inc(took, 1)
        stage_edges(nc, c, "e1_", c.table, acc, c.bucket_d, c.gather_d, c.local_d, layer=1)
        sweep(nc, c, "l1out", [(lambda k: at_tile(acc, k), P)], [(None, bias(c, "L1_bu"), 0, F), (0, w_both[:, :], 0, F)],
              vector=lambda e, k, po: e.scalar_tensor_tensor(out=at_tile(mid, k), in0=b_both[:, :], scalar=c.count[:, bass.ds(k, 1)],
                                                             in1=po[:, 0:F], op0=ALU.mult, op1=ALU.add))
        norm_stage(nc, c, "norm1", y, mid, small,
                   first=[("v", lambda e, at: e.scalar_tensor_tensor(out=y[:, at, :], in0=mid[:, at, :], scalar=0.0, in1=c.x[:, at, :], op0=ALU.max, op1=ALU.add))],
                   affine=(c.w["gamma"][:, :], c.w["beta"][:, :]), plus=arena(c, ACC0, [NT, F]))


def filter_layer(nc, c, t, small):
    with ExitStack() as ctx:
        load_weights(nc, c, ctx, t, "l2", natural=[(n, "L2_" + n) for n in ("mlp_w0", "mlp_b0", "mlp_w2", "lin1", "lin2", "lin")])
        acc, h1, z = arena(c, ACC0, [NT, F]), arena(c, B1_0, [NT, F]), arena(c, B2_0, [NT, F])
        sweep(nc, c, "l2in", [(lambda k: at_tile(c.x, k), P)], [(0, c.w["lin1"][:, :], 0, F)],
              vector=lambda e, k, po: e.tensor_copy(at_tile(h1, k), po[:, 0:F]),
              scalar=[lambda e, k, po, ring: e.activation(ring[:, 0:F], po[:, 0:F], ACT.Copy)],
              store=lambda k: [(tile_rows(c.table3, k), 0, F)])
        stage_edges(nc, c, "e2_", c.table, acc, c.bucket_d, c.gather_d, c.local_d, layer=2)
        vector_scalar_stage(nc, c, "l2sum", [("v", lambda e: e.tensor_tensor(h1, h1, acc, ALU.add))])
        sweep(nc, c, "l2mid", [(lambda k: at_tile(h1, k), P)], [(None, bias(c, "L2_lin2_b"), 0, F), (0, c.w["lin2"][:, :], 0, F)],
              vector=lambda e, k, po: e.tensor_copy(at_tile(z, k), po[:, 0:F]))
        piece_stage(nc, c, "l2soft", [
            ("v", lambda e, at: e.tensor_scalar(h1[:, at, :], z[:, at, :], 0.0, None, ALU.max)),
            ("s", lambda e, at: e.activation(z[:, at, :], z[:, at, :], ACT.Abs)),
            ("s", lambda e, at: e.activation(z[:, at, :], z[:, at, :], ACT.Exp, scale=-1.0)),
            ("s", lambda e, at: e.activation(z[:, at, :], z[:, at, :], ACT.Ln, bias=c.ones[:, 0:1])),
            ("v", lambda e, at: e.scalar_tensor_tensor(out=h1[:, at, :], in0=h1[:, at, :], scalar=-LOG2, in1=z[:, at, :], op0=ALU.add, op1=ALU.add)),
        ])
        sweep(nc, c, "l2out", [(lambda k: at_tile(h1, k), P)], [(None, bias(c, "L2_lin_b"), 0, F), (0, c.w["lin"][:, :], 0, F)],
              vector=lambda e, k, po: e.tensor_tensor(at_tile(z, k), po[:, 0:F], at_tile(c.x, k), ALU.add))
        norm_stage(nc, c, "norm2", z, h1, small)


def stage_rows_by_src(nc, c):
    with ExitStack() as ctx:
        sem = lambda n: c.semaphore("rs_" + n)
        sb = lambda n, s, d=F32: ctx.enter_context(nc.sbuf_tensor("rs_" + n, s, d))
        place, out = sb("place", [P, R, U], I32), sb("out", [P, R, U, REV])
        rows, hot_t = sb("rows", [P, R, U * P], BF16), sb("hot_t", [P, R, U, P], BF16)
        ph = ctx.enter_context(nc.psum_tensor("rs_ph", [P, 2, U, F], F32))
        rows_in, scattered = [sem(f"rows{r}") for r in range(R)], [sem(f"scattered{r}") for r in range(R)]
        start, hots_t, ready, packed, tick = (sem(n) for n in ("start", "hots_t", "ready", "packed", "tick"))
        PACKS = 3
        block = ctx.enter_context(nc.Block())

        @block.sync
        def _(sp):
            def step(k, i, r):
                at_least(sp, hots_t, k - R + 1, tick)
                load_local_rows(sp, c, rows, k, r, rows_in)
            rounds(sp, BATCHES, R, step)

        @block.vector
        def _(dve):
            dve.memset(out[:, :, :, F:F + 1], 1.0).then_inc(start, 1)

            def step(k, i, r):
                at_least(dve, rows_in[r], 16 * (i + 1), tick)
                at_least(dve, ready, k - R + 1, tick)
                dve.tensor_scalar(hot_t[:, r, :, :].rearrange("p u f -> p (u f)"), rows[:, r, :], c.part[:, 0:1], None, ALU.is_equal).then_inc(hots_t, 1)
            rounds(dve, BATCHES, R, step)

        @block.tensor
        def _(pe):
            def step(k, i, r):
                q = r % 2
                which = loaded_values(nc, c.bucket_d, k, PE_ENGINE, NT - 1)
                at_least(pe, hots_t, k + 1, tick)
                at_least(pe, packed, PACKS * (k - 1), tick)
                for u in range(U):
                    for n, part in enumerate(c.dst_parts):
                        ins = pe.matmul(ph[:, q, u, :], hot_t[:, r, u, :], part[:, bass.ds(which[u], 1), :].rearrange("p one f -> p (one f)"),
                                        start=(n == 0), stop=(n == 2))
                ins.then_inc(ready, 1)
            rounds(pe, BATCHES, R, step)

        @block.scalar
        def _(act):
            def step(k, i, r):
                at = bass.ds(k * U, U)
                at_least(act, scattered[r], 16 * U * i, tick)
                act.activation(place[:, r, :], c.key[:, at], ACT.Copy).then_inc(packed, 1)
                act.activation(out[:, r, :, F + 1], c.src_local[:, at], ACT.Copy).then_inc(packed, 1)
                at_least(act, ready, k + 1, tick)
                act.activation(out[:, r, :, 0:F], ph[:, r % 2, :, :], ACT.Copy).then_inc(packed, 1)
            act.wait_ge(start, 1)
            rounds(act, BATCHES, R, step)

        @block.gpsimd
        def _(pool):
            table = c.by_src.rearrange("b p u f -> (b p u) f")

            def step(k, i, r):
                at_least(pool, packed, PACKS * (k + 1), tick)
                for u in range(U):
                    pool.indirect_dma_start(table, bass.IndirectOffsetOnAxis(place[:, r, u:u + 1], 0), out[:, r, u, :], None,
                                            bounds_check=SLOTS - 1, oob_is_err=False).then_inc(scattered[r], 16)
            rounds(pool, BATCHES, R, step)
            for r in range(R):
                pool.wait_ge(scattered[r], 16 * U * BATCHES // R)


def stage_both_ways(nc, c, fwd, rev):
    with ExitStack() as ctx:
        sem = lambda n: c.semaphore("bw_" + n)
        sb = lambda n, s, d=F32: ctx.enter_context(nc.sbuf_tensor("bw_" + n, s, d))
        index = sb("index", [P, R, U], I32)
        ring, hot = [sb("ring_f", [P, R, U, F]), sb("ring_r", [P, R, U, REV])], [sb("hot_f", [P, R, U, P]), sb("hot_r", [P, R, U, P])]
        pa = [ctx.enter_context(nc.psum_tensor("bw_pa" + n, [P, 2, U, 256], F32)) for n in "fr"]
        index_ready, start, tick = sem("index"), sem("start"), sem("tick")
        arrived = [[sem(f"arrived_{n}{r}") for r in range(R)] for n in "fr"]
        hots, summed, added = ([sem(f"{what}_{n}") for n in "fr"] for what in ("hots", "summed", "added"))
        accs, buckets = (fwd, rev), (c.bucket_d, c.bucket_s)
        block = ctx.enter_context(nc.Block())

        @block.gpsimd
        def _(pool):
            gather_rows(pool, c, c.table, index, ring[0], index_ready, arrived[0], [(summed[0], 1)], tick)

        @block.sync
        def _(sp):
            def step(k, i, r):
                at_least(sp, summed[1], k - R + 1, tick)
                sp.dma_start(ring[1][:, r, :, :].rearrange("p u f -> p (u f)"), c.by_src[bass.ds(k, 1), :, :, :].rearrange("one p u f -> p (one u f)"))\
                    .then_inc(arrived[1][r], 16)
            rounds(sp, BATCHES, R, step)

        @block.scalar
        def _(act):
            rounds(act, BATCHES, R, lambda k, i, r: take_index(act, c.gather_d, index, k, i, r, arrived[0], index_ready, tick))

        @block.tensor
        def _(pe):
            def step(k, i, r):
                for way in (1, 0):
                    at_least(pe, hots[way], k + 1, tick)
                    if way == 0:
                        at_least(pe, arrived[0][r], 16 * U * (i + 1), tick)
                    at_least(pe, added[way], U * (k - 1), tick)
                    for u in range(U):
                        to, lhs = pa[way][:, r % 2, u, :], hot[way][:, r, u, :]
                        if way:
                            ins = pe.matmul(to[:, 0:F + 1], lhs, ring[1][:, r, u, 0:F + 1], start=True, stop=True)
                        else:
                            pe.matmul(to[:, 0:F], lhs, ring[0][:, r, u, :], start=True, stop=True)
                            ins = pe.matmul(to[:, F:F + 1], lhs, c.ones[:, 0:1], start=True, stop=True)
                    ins.then_inc(summed[way], 1)
            rounds(pe, BATCHES, R, step)

        @block.vector
        def _(dve):
            dve.memset(fwd, 0.0).then_inc(start, 1)
            dve.memset(rev, 0.0).then_inc(start, 1)
            dve.wait_ge(start, 2)

            def step(k, i, r):
                def one_hot(way):
                    at_least(dve, summed[way], k - R + 1, tick)
                    if way:
                        at_least(dve, arrived[1][r], 16 * (i + 1), tick)
                    inside = ring[1][:, r, :, F + 1] if way else c.local_d[:, bass.ds(k * U, U)]
                    dve.tensor_tensor(hot[way][:, r, :, :], over(c.j[:, 0:P], U), wide(inside, P), ALU.is_equal).then_inc(hots[way], 1)
                known = k if isinstance(k, int) else R
                if known < BATCHES:
                    one_hot(1)
                    one_hot(0)
                if known >= 2:
                    pair = [Adds(nc, dve, accs[way], buckets[way], pa[way][:, r % 2, :, :], F + 1, k - 2, summed[way], added[way], tick)
                            for way in range(2)]
                    for u in range(U):
                        pair[1].one(u)
                        pair[0].one(u)
            rounds(dve, BATCHES, R, step)
            for k in (BATCHES, BATCHES + 1):
                step(k, k // R, k % R)
            for way in range(2):
                dve.wait_ge(added[way], BATCHES * U)


def gated_layer(nc, c, t, small, out):
    with ExitStack() as ctx:
        load_weights(nc, c, ctx, t, "l3", natural=[(n, "L3_" + n) for n in ("w_in", "w_out", "wih1", "wih2", "whh", "b_in_col", "b_out_col")],
                     rows=[("b_ih", "L3_b_ih"), ("b_hh", "L3_b_hh")])
        fwd, rev = arena(c, ACC0, [NT, F + 1]), arena(c, B1_0, [NT, F + 1])
        parts0 = ARENA - 3 * NT * F // 2
        rest = arena(c, ACC0, [NT, F])
        c.dst_parts = [arena(c, parts0 + n * NT * F // 2, [NT, F], BF16) for n in range(3)]
        with ExitStack() as inner:
            stored = c.semaphore("l3_table")
            block = inner.enter_context(nc.Block())

            @block.sync
            def _(sp):
                sp.dma_start(c.table3.rearrange("t p f -> p t f"), c.x[:, :, :]).then_inc(stored, 16)
                sp.wait_ge(stored, 16)
        piece_stage(nc, c, "split3", split_pieces(c.x, c.dst_parts, rest))
        stage_rows_by_src(nc, c)
        stage_both_ways(nc, c, fwd, rev)
        p_in = ctx.enter_context(nc.sbuf_tensor("l3_p_in", [P, 3 * F], F32))
        p_out = ctx.enter_context(nc.sbuf_tensor("l3_p_out", [P, 3 * F], F32))
        gate_rows = ctx.enter_context(nc.sbuf_tensor("l3_gate_rows", [9, 4 * F], BF16))
        seen = ctx.enter_context(nc.sbuf_tensor("l3_seen", [P, NT, 9], F32))
        with ExitStack() as inner:
            made = c.semaphore("l3_made")
            took, kept = c.semaphore("l3_took"), c.semaphore("l3_kept")
            biases = inner.enter_context(nc.sbuf_tensor("l3_biases", [1, 3, 4 * F], F32))
            parts = inner.enter_context(nc.sbuf_tensor("l3_parts", [1, 3, 3, 4 * F], BF16))
            PARTS_READY = 13
            pw = inner.enter_context(nc.psum_tensor("l3_pw", [P, 4, 512], F32))
            block = inner.enter_context(nc.Block())

            @block.tensor
            def _(pe):
                pe.matmul(pw[:, 0, 0:3 * F], c.w["w_in"][:, :], c.w["wih1"][:, :], start=True, stop=True).then_inc(made, 1)
                pe.matmul(pw[:, 1, 0:3 * F], c.w["w_out"][:, :], c.w["wih2"][:, :], start=True, stop=True).then_inc(made, 1)
                pe.matmul(pw[0:1, 2, 0:3 * F], c.w["b_in_col"][:, :], c.w["wih1"][:, :], start=True, stop=True).then_inc(made, 1)
                pe.matmul(pw[0:1, 3, 0:3 * F], c.w["b_out_col"][:, :], c.w["wih2"][:, :], start=True, stop=True).then_inc(made, 1)

            @block.vector
            def _(dve):
                n = [0]

                def done(ins):
                    n[0] += 1
                    ins.then_inc(took, 1)
                    dve.wait_ge(took, n[0])
                dve.wait_ge(made, 4)
                done(dve.tensor_copy(p_in[:, :], pw[:, 0, 0:3 * F]))
                done(dve.tensor_copy(p_out[:, :], pw[:, 1, 0:3 * F]))
                done(dve.memset(biases[:, 0:2, :], 0.0))
                for b, bank in ((0, 2), (1, 3)):
                    done(dve.tensor_copy(biases[:, b, 0:3 * F], pw[0:1, bank, 0:3 * F]))
                done(dve.tensor_tensor(biases[:, 2, 0:2 * F], c.w["b_ih"][:, 0:2 * F], c.w["b_hh"][:, 0:2 * F], ALU.add))
                done(dve.tensor_copy(biases[:, 2, 2 * F:3 * F], c.w["b_ih"][:, 2 * F:3 * F]))
                done(dve.tensor_copy(biases[:, 2, 3 * F:4 * F], c.w["b_hh"][:, 2 * F:3 * F]))
                done(dve.tensor_copy(parts[:, 0, :, :], biases[:, :, :]))
                for p in range(2):
                    done(dve.tensor_tensor(biases[:, :, :], biases[:, :, :], parts[:, p, :, :], ALU.subtract))
                    done(dve.tensor_copy(parts[:, p + 1, :, :], biases[:, :, :]))
                parts_ready = n[0]
                assert parts_ready == PARTS_READY
                done(dve.memset(seen[:, :, :], 1.0))
                for n_, acc in enumerate((fwd, rev)):
                    count = acc[:, :, F]
                    done(dve.tensor_scalar(seen[:, :, n_::3], wide(count, 3), 1.0, None, ALU.min))
                    done(dve.tensor_scalar(count, count, 1.0, None, ALU.max))
                    done(dve.reciprocal(count, count))
                    done(dve.tensor_tensor(acc[:, :, 0:F], acc[:, :, 0:F], wide(count, F), ALU.mult))

            @block.sync
            def _(sp):
                sp.wait_ge(took, PARTS_READY)
                sp.dma_start(c.gate_rows, parts[:, :, :, :].rearrange("one p b n -> one (p b n)")).then_inc(kept, 16)
                sp.wait_ge(kept, 16)
                sp.dma_start(gate_rows[:, :], c.gate_rows.rearrange("one (m n) -> (one m) n", m=9)).then_inc(kept, 16)
                sp.wait_ge(kept, 32)
        y = arena(c, B2_0, [NT, F])
        stage_gates(nc, c, fwd, rev, seen, p_in, p_out, gate_rows, y)
        squares = arena(c, B1_0, [NT, F])
        norm_stage(nc, c, "norm3", y, squares, small,
                   first=[("v", lambda e, at: e.tensor_tensor(y[:, at, :], y[:, at, :], c.x[:, at, :], ALU.add))])
        with ExitStack() as last:
            stored = c.semaphore("stored")
            block = last.enter_context(nc.Block())
            whole = N // P * P

            @block.sync
            def _(sp):
                sp.dma_start(out[0:whole, :].rearrange("(t p) f -> p t f", p=P), c.x[:, 0:N // P, :]).then_inc(stored, 16)
                sp.dma_start(out[whole:N, :], c.x[0:N - whole, N // P, :]).then_inc(stored, 16)
                sp.wait_ge(stored, 32)


def stage_gates(nc, c, fwd, rev, seen, p_in, p_out, gate_rows, y):
    with ExitStack() as ctx:
        sem = lambda n: c.semaphore("ga_" + n)
        turned, copied, multiplied, gated, inner, tanhed, ended, staged, tick = (
            sem(n) for n in ("turned", "copied", "multiplied", "gated", "inner", "tanhed", "ended", "staged", "tick"))
        sb = lambda n, shape, d=F32: ctx.enter_context(nc.sbuf_tensor("ga_" + n, shape, d))
        xt, st = sb("xt", [P, G, 3, P]), sb("st", [9, G, P], BF16)
        gates, new = sb("gates", [P, G, 2 * F]), sb("new", [P, G, F])
        fixed, flags = sb("fixed", [P, G, 3, P]), sb("flags", [P, G, 9])
        pt = ctx.enter_context(nc.psum_tensor("ga_pt", [P, G, 4, P], F32))
        po = ctx.enter_context(nc.psum_tensor("ga_po", [P, G, 512], F32))
        block = ctx.enter_context(nc.Block())

        @block.gpsimd
        def _(pool):
            def stage(k, i, q):
                at_least(pool, turned, k - G + 1, tick)
                for n, src in enumerate((at_tile(fwd, k, 0, F), at_tile(rev, k, 0, F), at_tile(c.x, k))):
                    pool.tensor_copy(fixed[:, q, n, :], src).then_inc(staged, 1)
                pool.tensor_copy(flags[:, q, :], at_tile(seen, k)).then_inc(staged, 1)
            staggered(pool, NT, G, [(0, stage)])

        @block.tensor
        def _(pe):
            def turn(k, i, q):
                at_least(pe, staged, 4 * (k + 1), tick)
                at_least(pe, copied, 2 * (k - G + 1), tick)
                for n in range(3):
                    pe.transpose(pt[:, q, n, :], fixed[:, q, n, :], c.ident[:, :])
                pe.transpose(pt[0:9, q, 3, :], flags[:, q, :], c.ident[:, :]).then_inc(turned, 1)

            def multiply(k, i, q):
                at_least(pe, copied, 2 * (k + 1), tick)
                at_least(pe, inner, 2 * (k - G + 1), tick)
                b = po[:, q, :]
                pe.matmul(b, st[:, q, :], gate_rows[:, :], start=True, stop=False)
                pe.matmul(b[:, 0:3 * F], xt[:, q, 0, :], p_in[:, :], start=False, stop=False)
                pe.matmul(b[:, 0:3 * F], xt[:, q, 1, :], p_out[:, :], start=False, stop=False)
                pe.matmul(b[:, 0:2 * F], xt[:, q, 2, :], c.w["whh"][:, 0:2 * F], start=False, stop=False)
                pe.matmul(b[:, 3 * F:4 * F], xt[:, q, 2, :], c.w["whh"][:, 2 * F:3 * F], start=False, stop=True).then_inc(multiplied, 1)
            staggered(pe, NT, G, [(0, turn), (2, multiply)])

        @block.scalar
        def _(act):
            def copy(k, i, q):
                at_least(act, turned, k + 1, tick)
                at_least(act, multiplied, k - G + 1, tick)
                act.activation(xt[:, q, :, :], pt[:, q, 0:3, :], ACT.Copy).then_inc(copied, 1)
                act.activation(st[:, q, :], pt[0:9, q, 3, :], ACT.Copy).then_inc(copied, 1)

            def squash(k, i, q):
                at_least(act, multiplied, k + 1, tick)
                at_least(act, ended, 3 * (k - G + 1), tick)
                act.activation(gates[:, q, :], po[:, q, 0:2 * F], ACT.Sigmoid).then_inc(gated, 1)

            def tanh(k, i, q):
                at_least(act, inner, 2 * (k + 1), tick)
                act.activation(new[:, q, :], new[:, q, :], ACT.Tanh).then_inc(tanhed, 1)
            staggered(act, NT, G, [(0, copy), (3, squash), (4, tanh)])

        @block.vector
        def _(dve):
            def candidate(k, i, q):
                at_least(dve, gated, k + 1, tick)
                at_least(dve, ended, 3 * (k - G + 1), tick)
                dve.tensor_tensor(new[:, q, :], gates[:, q, 0:F], po[:, q, 3 * F:4 * F], ALU.mult).then_inc(inner, 1)
                at_least(dve, inner, 2 * k + 1, tick)
                dve.tensor_tensor(new[:, q, :], new[:, q, :], po[:, q, 2 * F:3 * F], ALU.add).then_inc(inner, 1)

            def blend(k, i, q):
                to = at_tile(y, k)
                at_least(dve, tanhed, k + 1, tick)
                dve.tensor_tensor(to, at_tile(c.x, k), new[:, q, :], ALU.subtract).then_inc(ended, 1)
                at_least(dve, ended, 3 * k + 1, tick)
                dve.tensor_tensor(to, to, gates[:, q, F:2 * F], ALU.mult).then_inc(ended, 1)
                at_least(dve, ended, 3 * k + 2, tick)
                dve.tensor_tensor(to, to, new[:, q, :], ALU.add).then_inc(ended, 1)
            staggered(dve, NT, G, [(0, candidate), (1, blend)])


def gnn_kernel(nc, t, out):
    c = Core(nc)
    scratch = lambda name, shape: nc.dram_tensor(name, shape, F32, kind="Internal").ap()
    c.by_src = scratch("rows_by_src", (BATCHES, P, U, REV))
    c.slots = scratch("slots", (EP,))
    c.kv3 = scratch("keys_values", (NT, P, 2 * F))
    c.kv = c.kv3.rearrange("t p f -> (t p) f")
    c.local_rows = nc.dram_tensor("local_rows", (TILES, P), BF16, kind="Internal").ap()
    c.gate_rows = nc.dram_tensor("gate_rows", (1, 9 * 4 * F), BF16, kind="Internal").ap()
    c.skip = scratch("skip", (NT, P, F))
    c.values = scratch("edge_values", (BATCHES, P, U, F))
    c.table3 = scratch("table", (NT, P, F))
    c.table = c.table3.rearrange("t p f -> (t p) f")
    c.attr1, c.attr2 = t["edge_attr_32"], t["edge_attr_50"]
    with ExitStack() as ctx:
        sb = lambda ctx, name, shape, dt=F32: ctx.enter_context(nc.sbuf_tensor(name, shape, dt))
        c.arena = sb(ctx, "arena", [P, ARENA])
        c.x = sb(ctx, "nodes", [P, NT, F])
        c.ident, c.ones = sb(ctx, "ident", [P, P]), sb(ctx, "ones", [P, P])
        c.bias_rows, c.ones_bf = sb(ctx, "bias_rows", [65, BIAS_N], BF16), sb(ctx, "ones_bf", [65, P], BF16)
        c.j, c.part, c.bounds = sb(ctx, "j", [P, TILES]), sb(ctx, "part", [P, 1]), sb(ctx, "bounds", [P, NB])
        c.gather_d, c.local_d, c.weight, c.cutoff = (sb(ctx, n, [P, TILES]) for n in ("gather_d", "local_d", "weight", "cutoff"))
        c.src_local, c.cols_i = sb(ctx, "src_local", [P, TILES], BF16), sb(ctx, "cols_i", [P, 8], I32)
        c.key = sb(ctx, "key", [P, TILES])
        c.count = sb(ctx, "count", [P, NT])
        small = sb(ctx, "small", [P, 2, NT])
        ints = sb(ctx, "ints", [P, TILES], I32)
        c.bucket_d, c.edge0, c.bucket_s = ints[0:1, :], ints[32:33, :], ints[64:65, :]
        with ExitStack() as early:
            c.src_f, c.dst_f, c.src_bucket, c.slot_of = (sb(early, n, [P, CHUNK]) for n in ("src_f", "dst_f", "src_bucket", "slot_of"))
            c.base = sb(early, "base", [P, NB])
            c.before, c.previous = sb(early, "before", [P, P]), sb(early, "previous", [P, P])
            c.counts = {s: sb(early, f"counts_{s}", [P, NB]) for s in "ds"}
            c.src_i, c.dst_i = arena(c, ACC0 + 2048, [CHUNK], I32), arena(c, ACC0 + 2048 + CHUNK, [CHUNK], I32)
            stage_setup(nc, c, t)
            attention_layer(nc, c, t, small)
        c.clear_semaphores()
        edge_mlp_layer(nc, c, t, small)
        c.clear_semaphores()
        filter_layer(nc, c, t, small)
        c.clear_semaphores()
        gated_layer(nc, c, t, small, out)


def kernel(**inputs):
    import numpy as np
    import concourse.bacc as bacc
    from concourse.bass_utils import run_bass_kernel_spmd as run

    g = {name: np.asarray(a) for name, a in inputs.items()}
    row = lambda name: g[name].reshape(1, -1)
    heads = lambda name: g[name].transpose(1, 0, 2).reshape(F, H * D)
    pad = EP - E
    at = {
        "x": g["x"],
        "src": np.concatenate([g["src"], np.full(pad, NOWHERE, g["src"].dtype)]),
        "dst": np.concatenate([g["dst"], np.full(pad, NOWHERE, g["dst"].dtype)]),
        "edge_weight": np.concatenate([g["edge_weight"], np.zeros(pad, np.float32)]),
        "edge_attr_32": np.pad(g["edge_attr_32"].T, ((0, 0), (0, pad))),
        "edge_attr_50": np.pad(g["edge_attr_50"].T, ((0, 0), (0, pad))),
        "L0_wq": heads("L0_gnn_Wq"), "L0_wk": heads("L0_gnn_Wk"), "L0_wv": heads("L0_gnn_Wv"), "L0_wskip": heads("L0_gnn_Wskip"),
        "L0_bias4": np.concatenate([row("L0_gnn_bq"), row("L0_gnn_bk"), row("L0_gnn_bv"), row("L0_gnn_bskip")], axis=1),
        "L0_we": row("L0_gnn_We"), "L0_wo": g["L0_gnn_Wo"], "L0_bo": row("L0_gnn_bo"),
        "L0_gamma": row("L0_gnn_gamma"), "L0_beta": row("L0_gnn_beta"),
        "L1_w1s": g["L1_gnn_W1"][:, 0:F].T, "L1_w1d": g["L1_gnn_W1"][:, F:2 * F].T, "L1_w1e": g["L1_gnn_W1"][:, 2 * F:].T,
        "L1_w2": g["L1_gnn_W2"], "L1_b2_col": g["L1_gnn_b2"].reshape(F, 1), "L1_wu": g["L1_gnn_Wu"].T,
        "L1_b1": row("L1_gnn_b1"), "L1_bu": row("L1_gnn_bu"), "L1_gamma": row("L1_gnn_gamma"), "L1_beta": row("L1_gnn_beta"),
        "L2_mlp_w0": g["L2_gnn_mlp_w0"].T, "L2_mlp_b0": g["L2_gnn_mlp_b0"].reshape(F, 1), "L2_mlp_w2": g["L2_gnn_mlp_w2"].T,
        "L2_mlp_b2": row("L2_gnn_mlp_b2"), "L2_lin1": g["L2_gnn_lin1_w"].T, "L2_lin2": g["L2_gnn_lin2_w"].T,
        "L2_lin2_b": row("L2_gnn_lin2_b"), "L2_lin": g["L2_gnn_lin_w"].T, "L2_lin_b": row("L2_gnn_lin_b"),
        "L3_w_in": g["L3_gnn_W_in"], "L3_w_out": g["L3_gnn_W_out"], "L3_b_in_col": g["L3_gnn_b_in"].reshape(F, 1),
        "L3_b_out_col": g["L3_gnn_b_out"].reshape(F, 1), "L3_wih1": g["L3_gnn_w_ih"][:, 0:F].T, "L3_wih2": g["L3_gnn_w_ih"][:, F:2 * F].T,
        "L3_whh": g["L3_gnn_w_hh"].T, "L3_b_ih": row("L3_gnn_b_ih"), "L3_b_hh": row("L3_gnn_b_hh"),
    }
    nc = bacc.Bacc("TRN2", target_bir_lowering=False, num_devices=1)
    arrays, t = {}, {}
    for name, a in at.items():
        a = np.ascontiguousarray(a)
        arrays[name] = a
        t[name] = nc.dram_tensor(name, a.shape, mybir.dt.from_np(a.dtype), kind="ExternalInput").ap()
    out = nc.dram_tensor("out", (N, F), F32, kind="ExternalOutput").ap()
    gnn_kernel(nc, t, out)
    return run(nc, [arrays], core_ids=[0]).results[0]["out"]
```
